# Optimizing a Trainium2 kernel written in Bass

```python
import numpy as np
import jax
import jax.numpy as jnp

def _softmax(x, axis=-1):
    return jax.nn.softmax(x, axis=axis)

def _gelu(x):
    return jax.nn.gelu(x, approximate=True)

def _silu(x):
    return jax.nn.silu(x)

def _sigmoid(x):
    return jax.nn.sigmoid(x)

def _layernorm(x, axis=-1, eps=1e-05):
    m = jnp.mean(x, axis=axis, keepdims=True)
    v = jnp.var(x, axis=axis, keepdims=True)
    return (x - m) / jnp.sqrt(v + eps)

def _scatter_add(tgt, idx, src, axis=0):
    return tgt.at[idx].add(src)

def _segment_sum(src, seg, n):
    return jax.ops.segment_sum(src, seg, n)
kernel_name = 'mk_decoder_postln_d2_seqx_r8_508bc6'

def setup_inputs(seed: int=0):
    np.random.seed(seed)
    _w = jnp.asarray

    def _rec_inputs():
        import jax
        import jax.numpy as jnp
        _rk = jax.random.key(seed)
        x = -0.0003929 + 0.9999 * jax.random.normal(jax.random.fold_in(_rk, 1), (8, 128, 256), jnp.float32)
        _lenS = 128 - jax.random.randint(jax.random.fold_in(_rk, 7), (8,), 0, max(1, 128 // 4) + 1, jnp.int32)
        _lenS2 = 128 - jax.random.randint(jax.random.fold_in(_rk, 8), (8,), 0, max(1, 128 // 4) + 1, jnp.int32)
        _ctx_2048P = jax.random.normal(jax.random.fold_in(_rk, 11), (8, 16, 256), jnp.float32)
        _ctx_2048c = jax.random.dirichlet(jax.random.fold_in(_rk, 511), 0.3 * jnp.ones((16,), jnp.float32), (8, 128))
        _ctx_2048t = jnp.einsum('bsk,bkd->bsd', _ctx_2048c, _ctx_2048P)
        _ctx_2048t = _ctx_2048t * jax.lax.rsqrt(jnp.mean(jnp.square(_ctx_2048t)) + 1e-12) * 0.953939
        ctx_2048 = -1.39393e-06 + 0.999914 * (_ctx_2048t + 0.3 * jax.random.normal(jax.random.fold_in(_rk, 611), (8, 128, 256), jnp.float32))
        itok_BxS_0_1023 = jax.random.randint(jax.random.fold_in(_rk, 12), (8, 128), 0, 128, jnp.int32)
        _validS = jnp.arange(128)[None, :] < _lenS[:, None]
        _validS2 = jnp.arange(128)[None, :] < _lenS2[:, None]
        _causal = jnp.tril(jnp.ones((128, 128), dtype=bool))
        mask_BxSxS2_ff0 = jnp.where(jnp.ones((8, 128, 128), dtype=bool), 0.0, -1000000000.0).astype(jnp.float32)
        return (x, ctx_2048, itok_BxS_0_1023, mask_BxSxS2_ff0)
    x, ctx_2048, itok_BxS_0_1023, mask_BxSxS2_ff0 = _rec_inputs()

    def _L0_attn_setup():
        import jax, jax.numpy as jnp
        import numpy as np
        D_MODEL = 256
        NUM_HEADS = 16
        KV_HEADS = 4
        HEAD_DIM = D_MODEL // NUM_HEADS
        SEQ = 512
        BATCH = 1
        ROPE_THETA = 10000.0

        def _rope_cache(T, dim, base, dtype):
            inv_freq = 1.0 / base ** (jnp.arange(0, dim, 2, dtype=jnp.float32) / dim)
            t = jnp.arange(T, dtype=jnp.float32)
            freqs = jnp.outer(t, inv_freq)
            emb = jnp.concatenate([freqs, freqs], axis=-1)
            return (jnp.cos(emb).astype(dtype), jnp.sin(emb).astype(dtype))

        def _rotate_half(x):
            d = x.shape[-1] // 2
            return jnp.concatenate([-x[..., d:], x[..., :d]], axis=-1)

        def _apply_rope(q, k, cos, sin):
            c = cos[None, :, None, :]
            s = sin[None, :, None, :]
            q = q * c + _rotate_half(q) * s
            k = k * c + _rotate_half(k) * s
            return (q, k)
        key = jax.random.key(seed)
        ks = jax.random.split(key, 6)
        sc = 1.0 / np.sqrt(D_MODEL)
        kv_out = KV_HEADS * HEAD_DIM
        return {'x': jax.random.normal(ks[0], (BATCH, SEQ, D_MODEL), dtype=jnp.float32), 'Wq': jax.random.normal(ks[1], (D_MODEL, D_MODEL), dtype=jnp.float32) * sc, 'Wk': jax.random.normal(ks[2], (D_MODEL, kv_out), dtype=jnp.float32) * sc, 'Wv': jax.random.normal(ks[3], (D_MODEL, kv_out), dtype=jnp.float32) * sc, 'Wo': jax.random.normal(ks[4], (D_MODEL, D_MODEL), dtype=jnp.float32) * sc, 'bo': jax.random.normal(ks[5], (D_MODEL,), dtype=jnp.float32) * 0.01}
    _L0_attn_all = _L0_attn_setup()
    _L0_attn_in = {k: v for k, v in _L0_attn_all.items() if k in ('Wq', 'Wk', 'Wv', 'Wo', 'bo')}
    del _L0_attn_all

    def _L0_xattn_setup():
        import jax, jax.numpy as jnp
        import numpy as np
        B, Lq, Lk = (2, 512, 128)
        Q_DIM, KV_DIM = (256, 256)
        H, HD = (16, 128)
        KVC, QC, R = (64, 96, 64)
        LOOKBACK = 8
        NEG = -1e+30

        def _rope(x, L):
            half = x.shape[-1] // 2
            inv_freq = 1.0 / 10000.0 ** (jnp.arange(half, dtype=jnp.float32) / half)
            ang = jnp.arange(L, dtype=jnp.float32)[:, None] * inv_freq
            cos, sin = (jnp.cos(ang), jnp.sin(ang))
            x1, x2 = (x[..., :half], x[..., half:])
            return jnp.concatenate([x1 * cos - x2 * sin, x1 * sin + x2 * cos], axis=-1)
        key = jax.random.key(seed)
        ks = jax.random.split(key, 11)

        def w(k, shape, fan_in):
            return jax.random.normal(k, shape, jnp.float32) / np.sqrt(fan_in).astype(np.float32)
        return {'q': jax.random.normal(ks[0], (B, Lq, Q_DIM), jnp.float32), 'kv': jax.random.normal(ks[1], (B, Lk, KV_DIM), jnp.float32), 'seg_id': jnp.sort(jax.random.randint(ks[2], (B, Lq), 0, Lk), axis=-1), 'W_kvc': w(ks[3], (KV_DIM, KVC), KV_DIM), 'W_dq': w(ks[4], (Q_DIM, QC), Q_DIM), 'W_uq': w(ks[5], (QC, H * HD), QC), 'W_qr': w(ks[6], (QC, H * R), QC), 'W_uk': w(ks[7], (KVC, H * HD), KVC), 'W_kr': w(ks[8], (KVC, R), KVC), 'W_uv': w(ks[9], (KVC, H * HD), KVC), 'W_o': w(ks[10], (H * HD, Q_DIM), H * HD)}
    _L0_xattn_all = _L0_xattn_setup()
    _L0_xattn_in = {k: v for k, v in _L0_xattn_all.items() if k in ('W_kvc', 'W_dq', 'W_uq', 'W_qr', 'W_uk', 'W_kr', 'W_uv', 'W_o')}
    del _L0_xattn_all

    def _L0_ffn_setup():
        import jax, jax.numpy as jnp
        import numpy as np
        H = 256
        E = 16
        K = 4
        I = 176
        SH_I = 2 * I
        B, S = (1, 128)
        key = jax.random.key(seed)
        ks = jax.random.split(key, 9)
        sc_h = 1.0 / np.sqrt(H)
        sc_i = 1.0 / np.sqrt(I)
        return {'hidden_states': jax.random.normal(ks[0], (B, S, H), dtype=jnp.float32), 'w_gate': jax.random.normal(ks[1], (E, H), dtype=jnp.float32) * sc_h, 'wg': jax.random.normal(ks[2], (E, H, I), dtype=jnp.float32) * sc_h, 'wu': jax.random.normal(ks[3], (E, H, I), dtype=jnp.float32) * sc_h, 'wd': jax.random.normal(ks[4], (E, I, H), dtype=jnp.float32) * sc_i, 'sg': jax.random.normal(ks[5], (H, SH_I), dtype=jnp.float32) * sc_h, 'su': jax.random.normal(ks[6], (H, SH_I), dtype=jnp.float32) * sc_h, 'sd': jax.random.normal(ks[7], (SH_I, H), dtype=jnp.float32) * (1.0 / np.sqrt(SH_I))}
    _L0_ffn_all = _L0_ffn_setup()
    _L0_ffn_in = {k: v for k, v in _L0_ffn_all.items() if k in ('w_gate', 'wg', 'wu', 'wd', 'sg', 'su', 'sd')}
    del _L0_ffn_all

    def _L1_attn_setup():
        import jax, jax.numpy as jnp
        import numpy as np
        B, S, HID = (2, 256, 256)
        NK, NV, DK, DV = (16, 32, 128, 128)
        KCONV, CHUNK, EPS = (4, 64, 1e-06)
        KEY_DIM = NK * DK
        VAL_DIM = NV * DV
        CONV_DIM = 2 * KEY_DIM + VAL_DIM

        def _forward(x, W_qkv, W_z, W_b, W_a, W_out, conv_w, dt_bias, A_log, norm_w):
            Bs, Ss, _ = x.shape
            mixed = jnp.einsum('bsh,ch->bsc', x, W_qkv)
            z = jnp.einsum('bsh,vh->bsv', x, W_z)
            b = jnp.einsum('bsh,nh->bsn', x, W_b)
            a = jnp.einsum('bsh,nh->bsn', x, W_a)
            xp = jnp.pad(mixed, ((0, 0), (KCONV - 1, 0), (0, 0)))
            conv = sum((xp[:, k:k + Ss, :] * conv_w[:, k] for k in range(KCONV)))
            mixed = jax.nn.silu(conv)
            q, k, v = jnp.split(mixed, [KEY_DIM, 2 * KEY_DIM], axis=-1)
            q = q.reshape(Bs, Ss, NK, DK)
            k = k.reshape(Bs, Ss, NK, DK)
            v = v.reshape(Bs, Ss, NV, DV)
            rep = NV // NK
            q = jnp.repeat(q, rep, axis=2)
            k = jnp.repeat(k, rep, axis=2)
            beta = jax.nn.sigmoid(b)
            g = -jnp.exp(A_log) * jax.nn.softplus(a + dt_bias)
            l2n = lambda t: t / jnp.maximum(jnp.linalg.norm(t, axis=-1, keepdims=True), 1e-12)
            q, k = (l2n(q), l2n(k))
            qT = jnp.swapaxes(q, 1, 2) * DK ** (-0.5)
            kT = jnp.swapaxes(k, 1, 2)
            vT = jnp.swapaxes(v, 1, 2)
            bT = jnp.swapaxes(beta, 1, 2)
            gT = jnp.swapaxes(g, 1, 2)
            N = Ss // CHUNK
            qc = qT.reshape(Bs, NV, N, CHUNK, DK)
            kc = kT.reshape(Bs, NV, N, CHUNK, DK)
            vc = vT.reshape(Bs, NV, N, CHUNK, DV)
            bc = bT.reshape(Bs, NV, N, CHUNK)
            gc = jnp.cumsum(gT.reshape(Bs, NV, N, CHUNK), axis=-1)
            v_beta = vc * bc[..., None]
            k_beta = kc * bc[..., None]
            tril = jnp.tril(jnp.ones((CHUNK, CHUNK), bool))
            strict = jnp.tril(jnp.ones((CHUNK, CHUNK), bool), -1)
            diff = gc[..., :, None] - gc[..., None, :]
            decay = jnp.exp(jnp.where(tril, diff, 0.0)) * tril
            A = -(jnp.einsum('bhnid,bhnjd->bhnij', k_beta, kc) * decay) * strict
            eye = jnp.eye(CHUNK, dtype=A.dtype)
            Tm = jax.scipy.linalg.solve_triangular(eye - A, jnp.broadcast_to(eye, A.shape), lower=True, unit_diagonal=True)
            u = jnp.einsum('bhnij,bhnjv->bhniv', Tm, v_beta)
            kcd = jnp.einsum('bhnij,bhnjd->bhnid', Tm, k_beta * jnp.exp(gc)[..., None])
            front = lambda t: jnp.moveaxis(t, 2, 0)
            xs = (front(qc), front(kc), front(u), front(kcd), front(decay), front(gc))
            S0 = jnp.zeros((Bs, NV, DK, DV), jnp.float32)

            def step(St, inp):
                q_i, k_i, u_i, kcd_i, dec_i, g_i = inp
                attn = jnp.einsum('bhid,bhjd->bhij', q_i, k_i) * dec_i
                v_new = u_i - jnp.einsum('bhid,bhdv->bhiv', kcd_i, St)
                inter = jnp.einsum('bhid,bhdv->bhiv', q_i * jnp.exp(g_i)[..., None], St)
                out_i = inter + jnp.einsum('bhij,bhjv->bhiv', attn, v_new)
                g_last = g_i[..., -1]
                St_new = St * jnp.exp(g_last)[..., None, None] + jnp.einsum('bhid,bhiv->bhdv', k_i * jnp.exp(g_last[..., None] - g_i)[..., None], v_new)
                return (St_new, out_i)
            _, outs = jax.lax.scan(step, S0, xs)
            core = jnp.moveaxis(outs, 0, 2).reshape(Bs, NV, Ss, DV)
            core = jnp.swapaxes(core, 1, 2)
            zr = z.reshape(Bs, Ss, NV, DV)
            var = jnp.mean(core * core, axis=-1, keepdims=True)
            normed = core * jax.lax.rsqrt(var + EPS) * norm_w * jax.nn.silu(zr)
            return jnp.einsum('bsv,hv->bsh', normed.reshape(Bs, Ss, VAL_DIM), W_out)
        key = jax.random.key(seed)
        ks = jax.random.split(key, 10)
        n = lambda k, shape, s: jax.random.normal(k, shape, jnp.float32) * s
        return {'x': n(ks[0], (B, S, HID), 1.0), 'W_qkv': n(ks[1], (CONV_DIM, HID), HID ** (-0.5)), 'W_z': n(ks[2], (VAL_DIM, HID), HID ** (-0.5)), 'W_b': n(ks[3], (NV, HID), HID ** (-0.5)), 'W_a': n(ks[4], (NV, HID), HID ** (-0.5)), 'W_out': n(ks[5], (HID, VAL_DIM), VAL_DIM ** (-0.5)), 'conv_w': n(ks[6], (CONV_DIM, KCONV), 0.5), 'dt_bias': n(ks[7], (NV,), 0.5), 'A_log': n(ks[8], (NV,), 0.5), 'norm_w': jnp.ones((DV,), jnp.float32)}
    _L1_attn_all = _L1_attn_setup()
    _L1_attn_in = {k: v for k, v in _L1_attn_all.items() if k in ('W_qkv', 'W_z', 'W_b', 'W_a', 'W_out', 'conv_w', 'dt_bias', 'A_log', 'norm_w')}
    del _L1_attn_all

    def _L1_xattn_setup():
        import jax, jax.numpy as jnp
        import numpy as np
        NUM_HEADS = 16
        EPS = 1e-08

        def _dyn_quant(x):
            s = jnp.maximum(jnp.max(jnp.abs(x), axis=-1, keepdims=True) / 127.0, EPS)
            q = jnp.clip(jnp.round(x / s), -127.0, 127.0)
            return (q, s)

        def _quant_weight(w):
            s = jnp.maximum(jnp.max(jnp.abs(w), axis=1, keepdims=True) / 127.0, EPS)
            q = jnp.clip(jnp.round(w / s), -127.0, 127.0)
            return (q, s)

        def _w8a8_linear(x, w, b):
            qx, sx = _dyn_quant(x)
            qw, sw = _quant_weight(w)
            y = jnp.einsum('bnc,oc->bno', qx, qw) * (sx * sw[:, 0])
            return y + b
        key = jax.random.key(seed)
        ks = jax.random.split(key, 9)
        B, N, L, C = (2, 512, 64, 256)
        sc = 0.02
        return {'x': jax.random.normal(ks[0], (B, N, C), jnp.float32), 'cond': jax.random.normal(ks[1], (B, L, C), jnp.float32), 'mask': jnp.zeros((B, N, L), jnp.float32), 'wq': jax.random.normal(ks[2], (C, C), jnp.float32) * sc, 'bq': jnp.zeros((C,), jnp.float32), 'wk': jax.random.normal(ks[3], (C, C), jnp.float32) * sc, 'bk': jnp.zeros((C,), jnp.float32), 'wv': jax.random.normal(ks[4], (C, C), jnp.float32) * sc, 'bv': jnp.zeros((C,), jnp.float32), 'wo': jax.random.normal(ks[5], (C, C), jnp.float32) * sc, 'bo': jnp.zeros((C,), jnp.float32)}
    _L1_xattn_all = _L1_xattn_setup()
    _L1_xattn_in = {k: v for k, v in _L1_xattn_all.items() if k in ('wq', 'bq', 'wk', 'bk', 'wv', 'bv', 'wo', 'bo')}
    del _L1_xattn_all

    def _L1_ffn_setup():
        import jax, jax.numpy as jnp
        import numpy as np
        import math
        N_EMBD = 256
        N_HEAD = 16
        HEAD_DIM = N_EMBD // N_HEAD
        B, T = (2, 256)
        key = jax.random.key(seed)
        k1, k2, k3 = jax.random.split(key, 3)
        x = jax.random.normal(k1, (B, T, N_EMBD), dtype=jnp.float32)
        W_gate = jax.random.normal(k2, (N_HEAD, N_EMBD), dtype=jnp.float32) * 0.02
        W_qkv = jax.random.normal(k3, (3 * N_EMBD, N_EMBD), dtype=jnp.float32) * 0.02
        return {'x': x, 'W_gate': W_gate, 'W_qkv': W_qkv}
    _L1_ffn_all = _L1_ffn_setup()
    _L1_ffn_in = {k: v for k, v in _L1_ffn_all.items() if k in ('W_gate', 'W_qkv')}
    del _L1_ffn_all
    return {'x': x, 'ctx_2048': ctx_2048, 'itok_BxS_0_1023': itok_BxS_0_1023, 'mask_BxSxS2_ff0': mask_BxSxS2_ff0, 'L0_attn_Wq': _L0_attn_in['Wq'], 'L0_attn_Wk': _L0_attn_in['Wk'], 'L0_attn_Wv': _L0_attn_in['Wv'], 'L0_attn_Wo': _L0_attn_in['Wo'], 'L0_attn_bo': _L0_attn_in['bo'], 'L0_xattn_W_kvc': _L0_xattn_in['W_kvc'], 'L0_xattn_W_dq': _L0_xattn_in['W_dq'], 'L0_xattn_W_uq': _L0_xattn_in['W_uq'], 'L0_xattn_W_qr': _L0_xattn_in['W_qr'], 'L0_xattn_W_uk': _L0_xattn_in['W_uk'], 'L0_xattn_W_kr': _L0_xattn_in['W_kr'], 'L0_xattn_W_uv': _L0_xattn_in['W_uv'], 'L0_xattn_W_o': _L0_xattn_in['W_o'], 'L0_ffn_w_gate': _L0_ffn_in['w_gate'], 'L0_ffn_wg': _L0_ffn_in['wg'], 'L0_ffn_wu': _L0_ffn_in['wu'], 'L0_ffn_wd': _L0_ffn_in['wd'], 'L0_ffn_sg': _L0_ffn_in['sg'], 'L0_ffn_su': _L0_ffn_in['su'], 'L0_ffn_sd': _L0_ffn_in['sd'], 'L1_attn_W_qkv': _L1_attn_in['W_qkv'], 'L1_attn_W_z': _L1_attn_in['W_z'], 'L1_attn_W_b': _L1_attn_in['W_b'], 'L1_attn_W_a': _L1_attn_in['W_a'], 'L1_attn_W_out': _L1_attn_in['W_out'], 'L1_attn_conv_w': _L1_attn_in['conv_w'], 'L1_attn_dt_bias': _L1_attn_in['dt_bias'], 'L1_attn_A_log': _L1_attn_in['A_log'], 'L1_attn_norm_w': _L1_attn_in['norm_w'], 'L1_xattn_wq': _L1_xattn_in['wq'], 'L1_xattn_bq': _L1_xattn_in['bq'], 'L1_xattn_wk': _L1_xattn_in['wk'], 'L1_xattn_bk': _L1_xattn_in['bk'], 'L1_xattn_wv': _L1_xattn_in['wv'], 'L1_xattn_bv': _L1_xattn_in['bv'], 'L1_xattn_wo': _L1_xattn_in['wo'], 'L1_xattn_bo': _L1_xattn_in['bo'], 'L1_ffn_W_gate': _L1_ffn_in['W_gate'], 'L1_ffn_W_qkv': _L1_ffn_in['W_qkv']}

def reference(x, ctx_2048, itok_BxS_0_1023, mask_BxSxS2_ff0, L0_attn_Wq, L0_attn_Wk, L0_attn_Wv, L0_attn_Wo, L0_attn_bo, L0_xattn_W_kvc, L0_xattn_W_dq, L0_xattn_W_uq, L0_xattn_W_qr, L0_xattn_W_uk, L0_xattn_W_kr, L0_xattn_W_uv, L0_xattn_W_o, L0_ffn_w_gate, L0_ffn_wg, L0_ffn_wu, L0_ffn_wd, L0_ffn_sg, L0_ffn_su, L0_ffn_sd, L1_attn_W_qkv, L1_attn_W_z, L1_attn_W_b, L1_attn_W_a, L1_attn_W_out, L1_attn_conv_w, L1_attn_dt_bias, L1_attn_A_log, L1_attn_norm_w, L1_xattn_wq, L1_xattn_bq, L1_xattn_wk, L1_xattn_bk, L1_xattn_wv, L1_xattn_bv, L1_xattn_wo, L1_xattn_bo, L1_ffn_W_gate, L1_ffn_W_qkv):
    import jax
    import jax.numpy as jnp

    def _L0_attn_ref(x, Wq, Wk, Wv, Wo, bo):
        import jax, jax.numpy as jnp
        import numpy as np
        D_MODEL = 256
        NUM_HEADS = 16
        KV_HEADS = 4
        HEAD_DIM = D_MODEL // NUM_HEADS
        SEQ = 512
        BATCH = 1
        ROPE_THETA = 10000.0

        def _rope_cache(T, dim, base, dtype):
            inv_freq = 1.0 / base ** (jnp.arange(0, dim, 2, dtype=jnp.float32) / dim)
            t = jnp.arange(T, dtype=jnp.float32)
            freqs = jnp.outer(t, inv_freq)
            emb = jnp.concatenate([freqs, freqs], axis=-1)
            return (jnp.cos(emb).astype(dtype), jnp.sin(emb).astype(dtype))

        def _rotate_half(x):
            d = x.shape[-1] // 2
            return jnp.concatenate([-x[..., d:], x[..., :d]], axis=-1)

        def _apply_rope(q, k, cos, sin):
            c = cos[None, :, None, :]
            s = sin[None, :, None, :]
            q = q * c + _rotate_half(q) * s
            k = k * c + _rotate_half(k) * s
            return (q, k)
        B, T, _ = x.shape
        q = (x @ Wq).reshape(B, T, NUM_HEADS, HEAD_DIM)
        k = (x @ Wk).reshape(B, T, KV_HEADS, HEAD_DIM)
        v = (x @ Wv).reshape(B, T, KV_HEADS, HEAD_DIM)
        cos, sin = _rope_cache(T, HEAD_DIM, ROPE_THETA, x.dtype)
        q, k = _apply_rope(q, k, cos, sin)
        reps = NUM_HEADS // KV_HEADS
        k = jnp.repeat(k, reps, axis=2)
        v = jnp.repeat(v, reps, axis=2)
        q = q.transpose(0, 2, 1, 3)
        k = k.transpose(0, 2, 1, 3)
        v = v.transpose(0, 2, 1, 3)
        scores = jnp.einsum('bhqd,bhkd->bhqk', q, k)
        causal = jnp.triu(jnp.ones((T, T), dtype=bool), k=1)
        scores = jnp.where(causal[None, None], -jnp.inf, scores)
        attn = jax.nn.softmax(scores / jnp.sqrt(jnp.asarray(HEAD_DIM, x.dtype)), axis=-1)
        ctx = jnp.einsum('bhqk,bhkd->bhqd', attn, v)
        ctx = ctx.transpose(0, 2, 1, 3).reshape(B, T, D_MODEL)
        return ctx @ Wo + bo

    def _L0_xattn_ref(q, kv, seg_id, W_kvc, W_dq, W_uq, W_qr, W_uk, W_kr, W_uv, W_o):
        import jax, jax.numpy as jnp
        import numpy as np
        B, Lq, Lk = (2, 512, 128)
        Q_DIM, KV_DIM = (256, 256)
        H, HD = (16, 128)
        KVC, QC, R = (64, 96, 64)
        LOOKBACK = 8
        NEG = -1e+30

        def _rope(x, L):
            half = x.shape[-1] // 2
            inv_freq = 1.0 / 10000.0 ** (jnp.arange(half, dtype=jnp.float32) / half)
            ang = jnp.arange(L, dtype=jnp.float32)[:, None] * inv_freq
            cos, sin = (jnp.cos(ang), jnp.sin(ang))
            x1, x2 = (x[..., :half], x[..., half:])
            return jnp.concatenate([x1 * cos - x2 * sin, x1 * sin + x2 * cos], axis=-1)
        b, lq, _ = q.shape
        lk = kv.shape[1]
        kv_c = kv @ W_kvc
        q_c = q @ W_dq
        q_nope = (q_c @ W_uq).reshape(b, lq, H, HD).transpose(0, 2, 1, 3)
        q_rope = (q_c @ W_qr).reshape(b, lq, H, R).transpose(0, 2, 1, 3)
        k_nope = (kv_c @ W_uk).reshape(b, lk, H, HD)
        v = (kv_c @ W_uv).reshape(b, lk, H, HD)
        k_rope = kv_c @ W_kr
        q_rope = _rope(q_rope, lq)
        k_rope = _rope(k_rope, lk)
        scale = 1.0 / np.sqrt(HD + R).astype(np.float32)
        scores = (jnp.einsum('bhqd,bkhd->bhqk', q_nope, k_nope) + jnp.einsum('bhqr,bkr->bhqk', q_rope, k_rope)) * scale
        k_ids = jnp.arange(lk)[None, None, :]
        qs = seg_id[:, :, None]
        good = (k_ids <= qs) & (k_ids >= qs - LOOKBACK)
        scores = jnp.where(good[:, None, :, :], scores, NEG)
        attn = jax.nn.softmax(scores, axis=-1)
        out = jnp.einsum('bhqk,bkhd->bqhd', attn, v).reshape(b, lq, H * HD)
        return out @ W_o

    def _L0_ffn_ref(hidden_states, w_gate, wg, wu, wd, sg, su, sd):
        import jax, jax.numpy as jnp
        import numpy as np
        H = 256
        E = 16
        K = 4
        I = 176
        SH_I = 2 * I
        B, S = (1, 128)
        b, s, h = hidden_states.shape
        x = hidden_states.reshape(-1, h)
        T = x.shape[0]
        logits = x @ w_gate.T
        probs = jax.nn.softmax(logits.astype(jnp.float32), axis=-1)
        top_w, top_i = jax.lax.top_k(probs, K)
        routing_weight = jnp.zeros((T, E), dtype=probs.dtype)
        routing_weight = routing_weight.at[jnp.arange(T)[:, None], top_i].add(top_w)
        g = jnp.einsum('th,ehi->tei', x, wg)
        u = jnp.einsum('th,ehi->tei', x, wu)
        act = jax.nn.silu(g) * u
        routed = jnp.einsum('te,tei,eih->th', routing_weight, act, wd)
        shared = jax.nn.silu(x @ sg) * (x @ su) @ sd
        out = (routed + shared).astype(hidden_states.dtype)
        return out.reshape(b, s, h)

    def _L1_attn_ref(x, W_qkv, W_z, W_b, W_a, W_out, conv_w, dt_bias, A_log, norm_w):
        import jax, jax.numpy as jnp
        import numpy as np
        B, S, HID = (2, 256, 256)
        NK, NV, DK, DV = (16, 32, 128, 128)
        KCONV, CHUNK, EPS = (4, 64, 1e-06)
        KEY_DIM = NK * DK
        VAL_DIM = NV * DV
        CONV_DIM = 2 * KEY_DIM + VAL_DIM

        def _forward(x, W_qkv, W_z, W_b, W_a, W_out, conv_w, dt_bias, A_log, norm_w):
            Bs, Ss, _ = x.shape
            mixed = jnp.einsum('bsh,ch->bsc', x, W_qkv)
            z = jnp.einsum('bsh,vh->bsv', x, W_z)
            b = jnp.einsum('bsh,nh->bsn', x, W_b)
            a = jnp.einsum('bsh,nh->bsn', x, W_a)
            xp = jnp.pad(mixed, ((0, 0), (KCONV - 1, 0), (0, 0)))
            conv = sum((xp[:, k:k + Ss, :] * conv_w[:, k] for k in range(KCONV)))
            mixed = jax.nn.silu(conv)
            q, k, v = jnp.split(mixed, [KEY_DIM, 2 * KEY_DIM], axis=-1)
            q = q.reshape(Bs, Ss, NK, DK)
            k = k.reshape(Bs, Ss, NK, DK)
            v = v.reshape(Bs, Ss, NV, DV)
            rep = NV // NK
            q = jnp.repeat(q, rep, axis=2)
            k = jnp.repeat(k, rep, axis=2)
            beta = jax.nn.sigmoid(b)
            g = -jnp.exp(A_log) * jax.nn.softplus(a + dt_bias)
            l2n = lambda t: t / jnp.maximum(jnp.linalg.norm(t, axis=-1, keepdims=True), 1e-12)
            q, k = (l2n(q), l2n(k))
            qT = jnp.swapaxes(q, 1, 2) * DK ** (-0.5)
            kT = jnp.swapaxes(k, 1, 2)
            vT = jnp.swapaxes(v, 1, 2)
            bT = jnp.swapaxes(beta, 1, 2)
            gT = jnp.swapaxes(g, 1, 2)
            N = Ss // CHUNK
            qc = qT.reshape(Bs, NV, N, CHUNK, DK)
            kc = kT.reshape(Bs, NV, N, CHUNK, DK)
            vc = vT.reshape(Bs, NV, N, CHUNK, DV)
            bc = bT.reshape(Bs, NV, N, CHUNK)
            gc = jnp.cumsum(gT.reshape(Bs, NV, N, CHUNK), axis=-1)
            v_beta = vc * bc[..., None]
            k_beta = kc * bc[..., None]
            tril = jnp.tril(jnp.ones((CHUNK, CHUNK), bool))
            strict = jnp.tril(jnp.ones((CHUNK, CHUNK), bool), -1)
            diff = gc[..., :, None] - gc[..., None, :]
            decay = jnp.exp(jnp.where(tril, diff, 0.0)) * tril
            A = -(jnp.einsum('bhnid,bhnjd->bhnij', k_beta, kc) * decay) * strict
            eye = jnp.eye(CHUNK, dtype=A.dtype)
            Tm = jax.scipy.linalg.solve_triangular(eye - A, jnp.broadcast_to(eye, A.shape), lower=True, unit_diagonal=True)
            u = jnp.einsum('bhnij,bhnjv->bhniv', Tm, v_beta)
            kcd = jnp.einsum('bhnij,bhnjd->bhnid', Tm, k_beta * jnp.exp(gc)[..., None])
            front = lambda t: jnp.moveaxis(t, 2, 0)
            xs = (front(qc), front(kc), front(u), front(kcd), front(decay), front(gc))
            S0 = jnp.zeros((Bs, NV, DK, DV), jnp.float32)

            def step(St, inp):
                q_i, k_i, u_i, kcd_i, dec_i, g_i = inp
                attn = jnp.einsum('bhid,bhjd->bhij', q_i, k_i) * dec_i
                v_new = u_i - jnp.einsum('bhid,bhdv->bhiv', kcd_i, St)
                inter = jnp.einsum('bhid,bhdv->bhiv', q_i * jnp.exp(g_i)[..., None], St)
                out_i = inter + jnp.einsum('bhij,bhjv->bhiv', attn, v_new)
                g_last = g_i[..., -1]
                St_new = St * jnp.exp(g_last)[..., None, None] + jnp.einsum('bhid,bhiv->bhdv', k_i * jnp.exp(g_last[..., None] - g_i)[..., None], v_new)
                return (St_new, out_i)
            _, outs = jax.lax.scan(step, S0, xs)
            core = jnp.moveaxis(outs, 0, 2).reshape(Bs, NV, Ss, DV)
            core = jnp.swapaxes(core, 1, 2)
            zr = z.reshape(Bs, Ss, NV, DV)
            var = jnp.mean(core * core, axis=-1, keepdims=True)
            normed = core * jax.lax.rsqrt(var + EPS) * norm_w * jax.nn.silu(zr)
            return jnp.einsum('bsv,hv->bsh', normed.reshape(Bs, Ss, VAL_DIM), W_out)
        return _forward(x, W_qkv, W_z, W_b, W_a, W_out, conv_w, dt_bias, A_log, norm_w)

    def _L1_xattn_ref(x, cond, mask, wq, bq, wk, bk, wv, bv, wo, bo):
        import jax, jax.numpy as jnp
        import numpy as np
        NUM_HEADS = 16
        EPS = 1e-08

        def _dyn_quant(x):
            s = jnp.maximum(jnp.max(jnp.abs(x), axis=-1, keepdims=True) / 127.0, EPS)
            q = jnp.clip(jnp.round(x / s), -127.0, 127.0)
            return (q, s)

        def _quant_weight(w):
            s = jnp.maximum(jnp.max(jnp.abs(w), axis=1, keepdims=True) / 127.0, EPS)
            q = jnp.clip(jnp.round(w / s), -127.0, 127.0)
            return (q, s)

        def _w8a8_linear(x, w, b):
            qx, sx = _dyn_quant(x)
            qw, sw = _quant_weight(w)
            y = jnp.einsum('bnc,oc->bno', qx, qw) * (sx * sw[:, 0])
            return y + b
        B, N, C = x.shape
        L = cond.shape[1]
        H = NUM_HEADS
        D = C // H
        inv_sqrt_d = np.float32(1.0 / np.sqrt(D))
        q = _w8a8_linear(x, wq, bq).reshape(B, N, H, D).transpose(0, 2, 1, 3)
        k = (cond @ wk.T + bk).reshape(B, L, H, D).transpose(0, 2, 1, 3)
        v = (cond @ wv.T + bv).reshape(B, L, H, D).transpose(0, 2, 1, 3)
        scores = jnp.einsum('bhnd,bhld->bhnl', q, k) * inv_sqrt_d + mask[:, None]
        attn = jax.nn.softmax(scores, axis=-1)
        o = jnp.einsum('bhnl,bhld->bhnd', attn, v)
        o = o.transpose(0, 2, 1, 3).reshape(B, N, C)
        return _w8a8_linear(o, wo, bo)

    def _L1_ffn_ref(x, W_gate, W_qkv):
        import jax, jax.numpy as jnp
        import numpy as np
        import math
        N_EMBD = 256
        N_HEAD = 16
        HEAD_DIM = N_EMBD // N_HEAD
        B, T = (2, 256)
        Bb, Tt, C = x.shape
        H, hd = (N_HEAD, HEAD_DIM)
        gating = jax.nn.softmax(x @ W_gate.T, axis=-1)
        idx = jnp.argmax(gating, axis=-1)
        indicator = jax.nn.one_hot(idx, H, dtype=gating.dtype)
        top1_val = jnp.max(gating, axis=-1, keepdims=True)
        gating_top1 = indicator * top1_val
        qkv = x @ W_qkv.T
        q, k, v = jnp.split(qkv, 3, axis=-1)
        k = k.reshape(Bb, Tt, H, hd)
        v = v.reshape(Bb, Tt, H, hd)
        k_shared = jnp.einsum('bth,bthd->btd', indicator, k)
        v_shared = jnp.einsum('bth,bthd->btd', gating_top1, v)
        q = q.reshape(Bb, Tt, H, hd).transpose(0, 2, 1, 3)
        att = jnp.einsum('bhqd,bkd->bhqk', q, k_shared) * (1.0 / math.sqrt(hd))
        causal = jnp.tril(jnp.ones((Tt, Tt), dtype=bool))
        att = jnp.where(causal[None, None, :, :], att, -jnp.inf)
        att = jax.nn.softmax(att, axis=-1)
        y = jnp.einsum('bhqk,bkd->bhqd', att, v_shared)
        y = y.transpose(0, 2, 1, 3).reshape(Bb, Tt, C)
        return y
    x = _layernorm(x + _L0_attn_ref(x, L0_attn_Wq, L0_attn_Wk, L0_attn_Wv, L0_attn_Wo, L0_attn_bo), axis=-1)
    x = _layernorm(x + _L0_xattn_ref(x, ctx_2048, itok_BxS_0_1023, L0_xattn_W_kvc, L0_xattn_W_dq, L0_xattn_W_uq, L0_xattn_W_qr, L0_xattn_W_uk, L0_xattn_W_kr, L0_xattn_W_uv, L0_xattn_W_o), axis=-1)
    x = _layernorm(x + _L0_ffn_ref(x, L0_ffn_w_gate, L0_ffn_wg, L0_ffn_wu, L0_ffn_wd, L0_ffn_sg, L0_ffn_su, L0_ffn_sd), axis=-1)
    x = _layernorm(x + _L1_attn_ref(x, L1_attn_W_qkv, L1_attn_W_z, L1_attn_W_b, L1_attn_W_a, L1_attn_W_out, L1_attn_conv_w, L1_attn_dt_bias, L1_attn_A_log, L1_attn_norm_w), axis=-1)
    x = _layernorm(x + _L1_xattn_ref(x, ctx_2048, mask_BxSxS2_ff0, L1_xattn_wq, L1_xattn_bq, L1_xattn_wk, L1_xattn_bk, L1_xattn_wv, L1_xattn_bv, L1_xattn_wo, L1_xattn_bo), axis=-1)
    x = _layernorm(x + _L1_ffn_ref(x, L1_ffn_W_gate, L1_ffn_W_qkv), axis=-1)
    return x

_drawn_inputs = setup_inputs


def setup_inputs(seed=0):
    import zlib

    import numpy as np

    out = dict(_drawn_inputs(seed))
    spreads = {'L1_attn_norm_w': (1.0, 0.2),
     'L1_xattn_bq': (0.0, 0.8),
     'L1_xattn_bk': (0.0, 0.8),
     'L1_xattn_bv': (0.0, 0.274),
     'L1_xattn_bo': (0.0, 0.1)}
    factors = {'L0_attn_bo': 3.64,
     'L1_xattn_wq': 8.0,
     'L1_xattn_wk': 8.0,
     'L1_ffn_W_gate': 5.82,
     'L1_ffn_W_qkv': 4.465}
    for name, (base, spread) in spreads.items():
        noise = np.random.default_rng([zlib.crc32(name.encode()), seed]).standard_normal(out[name].shape)
        drawn = base * np.exp(spread * noise) if base else spread * noise
        out[name] = jnp.asarray(drawn.astype(out[name].dtype))
    for name, factor in factors.items():
        out[name] = (out[name] * factor).astype(out[name].dtype)
    return out
```

```python
from contextlib import ExitStack

import numpy as np

import concourse.bass as bass
from concourse import mybir

F32 = mybir.dt.float32
BF16 = mybir.dt.bfloat16
I32 = mybir.dt.int32
ALU = mybir.AluOpType
ACT = mybir.ActivationFunctionType
AX = mybir.AxisListType

B, S, D = 8, 128, 256
P = 128
DC = D // P
H = 16
QUADS = H // 4
HD = D // H
MASKED = -1e30
LN_EPS = 1e-5


def at(i, per, n):
    return i * per + n


class Linked:

    def __init__(self, eng, sem, per=0, i=0):
        self.eng, self.sem, self.per, self.i, self.n = eng, sem, per, i, 0

    def __call__(self, *together):
        for ins in together:
            ins.then_inc(self.sem, 1)
            self.n += 1
        self.eng.wait_ge(self.sem, at(self.i, self.per, self.n))

    def close(self):
        assert self.n == self.per, self.n


class Phase:

    def __init__(self, nc, tag, ctx, sems):
        self.nc, self.tag, self.ctx, self.sems = nc, tag, ctx, sems

    def sb(self, name, shape, dt=F32):
        return self.ctx.enter_context(self.nc.sbuf_tensor(f"{self.tag}_{name}", shape, dt))

    def bank(self, name, dt=F32):
        return self.ctx.enter_context(self.nc.psum_tensor(f"{self.tag}_{name}", [P, 2048 // mybir.dt.size(dt)], dt))

    def sem(self, name):
        self.sems.append(self.nc.alloc_semaphore(name=f"{self.tag}_{name}"))
        return self.sems[-1]


def four(ap):
    return ap.rearrange("p (h n) -> p h n", h=4)


def spread(ap, n):
    return ap.unsqueeze(1).broadcast_to([ap.shape[0], n, ap.shape[1]])


def along(ap, n):
    return ap.unsqueeze(2).broadcast_to([ap.shape[0], ap.shape[1], n])


def batch(t, b):
    return t[bass.ds(b, 1)].rearrange("a p c -> p (a c)")


def store_batch(sp, i, ready, out, dst, stored, free):
    sp.wait_ge(ready, at(i, 1, 1))
    sp.dma_start(batch(dst, i), out).then_inc(stored, 16)
    sp.wait_ge(stored, at(i, 16, 16))
    sp.sem_inc(free, 1)


def fill_identity(pool, link, tile):
    link(pool.memset(tile, 0.0))
    link(pool.affine_select(out=tile, in_=tile, compare_op=ALU.not_equal, fill=1.0, base=0,
                            pattern=[[-1, P]], channel_multiplier=1))


class Attention:

    def __init__(self, ph, name, width, banks, pbuf, ptbuf, stats, out, ident):
        self.width, self.out, self.ident = width, out, ident
        self.S, self.PT, self.O = banks
        self.p, self.pt, self.stats = pbuf, ptbuf, stats
        self.scores_ready = ph.sem(name + "_scores_ready")
        self.max_ready = ph.sem(name + "_max_ready")
        self.shifted = ph.sem(name + "_shifted")
        self.exp_ready = ph.sem(name + "_exp_ready")
        self.pt_ready = ph.sem(name + "_pt_ready")
        self.pt_copied = ph.sem(name + "_pt_copied")
        self.o_ready = ph.sem(name + "_o_ready")
        self.recip_ready = ph.sem(name + "_recip_ready")
        self.o_done = ph.sem(name + "_o_done")

    def on_tensor(self, pe, i, scores, values):
        w = self.width + 1
        for s in range(QUADS + 2):
            if s < QUADS:
                if s >= 2:
                    pe.wait_ge(self.shifted, at(i, QUADS, s - 1))
                scores(s, self.S[s % 2]).then_inc(self.scores_ready, 1)
            if 1 <= s <= QUADS:
                n = s - 1
                pe.wait_ge(self.exp_ready, at(i, QUADS, n + 1))
                if n >= 2:
                    pe.wait_ge(self.pt_copied, at(i, QUADS, n - 1))
                for h in range(4):
                    last = pe.transpose(self.PT[n % 2][:, h * P:(h + 1) * P], self.p[:, n % 2, h, :], self.ident)
                last.then_inc(self.pt_ready, 1)
            if s >= 2:
                n = s - 2
                pe.wait_ge(self.pt_copied, at(i, QUADS, n + 1))
                if n >= 2:
                    pe.wait_ge(self.o_done, at(i, QUADS, n - 1))
                for h in range(4):
                    last = pe.matmul(self.O[n % 2][:, h * w:(h + 1) * w], self.pt[:, n % 2, h, :],
                                     values(n, h), start=True, stop=True)
                last.then_inc(self.o_ready, 1)

    def on_scalar(self, act, i):
        for s in range(QUADS + 1):
            if s < QUADS:
                act.wait_ge(self.shifted, at(i, QUADS, s + 1))
                act.activation(self.p[:, s % 2], self.p[:, s % 2], ACT.Exp).then_inc(self.exp_ready, 1)
            if s >= 1:
                n = s - 1
                act.wait_ge(self.pt_ready, at(i, QUADS, n + 1))
                if n >= 2:
                    act.wait_ge(self.o_ready, at(i, QUADS, n - 1))
                act.activation(self.pt[:, n % 2], four(self.PT[n % 2][:, :]), ACT.Copy).then_inc(self.pt_copied, 1)

    def on_vector(self, dve, i):
        w = self.width + 1
        for s in range(QUADS + 2):
            if s < QUADS:
                dve.wait_ge(self.scores_ready, at(i, QUADS, s + 1))
                dve.tensor_reduce(self.stats[:, 4 * s:4 * s + 4], four(self.S[s % 2][:, :]), AX.X, ALU.max)\
                   .then_inc(self.max_ready, 1)
                dve.wait_ge(self.max_ready, at(i, QUADS, s + 1))
                if s >= 2:
                    dve.wait_ge(self.pt_ready, at(i, QUADS, s - 1))
                dve.tensor_tensor(self.p[:, s % 2], four(self.S[s % 2][:, :]), along(self.stats[:, 4 * s:4 * s + 4], P),
                                  ALU.subtract).then_inc(self.shifted, 1)
            if s >= 2:
                n = s - 2
                dve.wait_ge(self.o_ready, at(i, QUADS, n + 1))
                o = self.O[n % 2][:, 0:4 * w].rearrange("p (h w) -> p h w", h=4)
                dve.reciprocal(self.stats[:, 16 + 4 * n:20 + 4 * n].unsqueeze(2), o[:, :, self.width:w]).then_inc(self.recip_ready, 1)
                dve.wait_ge(self.recip_ready, at(i, QUADS, n + 1))
                dve.tensor_tensor(self.out[:, 4 * n:4 * n + 4, :], o[:, :, 0:self.width],
                                  along(self.stats[:, 16 + 4 * n:20 + 4 * n], self.width), ALU.mult).then_inc(self.o_done, 1)


class LayerNorm:

    DVE_STEPS = 9

    def __init__(self, ph, name):
        self.r = ph.sb(name + "_sum", [P, D])
        self.st = ph.sb(name + "_stats", [P, 6])
        self.c = ph.sb(name + "_cols", [P, 8])
        self.rstd = ph.sb(name + "_rstd", [P, 2])
        self.step = ph.sem(name + "_step")
        self.log_ready = ph.sem(name + "_log_ready")
        self.rstd_ready = ph.sem(name + "_rstd_ready")
        self.done = ph.sem(name + "_done")

    def on_vector(self, dve, i, out, x, y):
        link = Linked(dve, self.step, self.DVE_STEPS, i)
        col = lambda n: self.c[:, n:n + 1]
        link(dve.tensor_tensor(self.r[:, :], x, y, ALU.add))
        link(dve.bn_stats(self.st[:, :], self.r[:, :]))
        link(dve.tensor_tensor(col(0), self.st[:, 1:2], self.st[:, 4:5], ALU.subtract),
             dve.tensor_tensor(col(1), self.st[:, 1:2], self.st[:, 4:5], ALU.add),
             dve.tensor_tensor(col(2), self.st[:, 2:3], self.st[:, 5:6], ALU.add))
        link(dve.scalar_tensor_tensor(col(3), col(0), 0.25, col(0), ALU.mult, ALU.mult),
             dve.tensor_scalar(col(4), col(2), 1.0 / D, LN_EPS, ALU.mult, ALU.add),
             dve.tensor_scalar(col(5), col(1), 0.5, None, ALU.mult))
        link(dve.tensor_tensor(self.rstd[:, 0:1], col(3), col(4), ALU.add))
        link.close()
        dve.wait_ge(self.rstd_ready, at(i, 1, 1))
        dve.tensor_scalar(out, self.r[:, :], col(5), self.rstd[:, 1:2], ALU.subtract, ALU.mult).then_inc(self.done, 1)

    def on_scalar(self, act, i):
        act.wait_ge(self.step, at(i, self.DVE_STEPS, self.DVE_STEPS))
        act.activation(self.rstd[:, 1:2], self.rstd[:, 0:1], ACT.Ln).then_inc(self.log_ready, 1)
        act.wait_ge(self.log_ready, at(i, 1, 1))
        act.activation(self.rstd[:, 1:2], self.rstd[:, 1:2], ACT.Exp, scale=-0.5).then_inc(self.rstd_ready, 1)

KV = 4
LAT, QLAT, ROPE, XHD = 64, 96, 64, 128
LOOKBACK = 8
PAIRS = H // 2


def layer0_attention(nc, sems, d, x_src, x_dst):
    ctx = ExitStack()
    with ctx:
        ph = Phase(nc, "a", ctx, sems)
        sb, sem = ph.sb, ph.sem
        shapes = dict(wqk=[P, 2, DC, 4, P], wv=[P, DC, KV * HD], wo=[P, DC, D], bo=[1, D], rope=[P, 2, P],
                      wkvc2=[P, DC, 2 * LAT], wdq=[P, DC, QLAT], wuq=[P, H, QLAT], wuk=[P, H, LAT],
                      wqr=[QLAT, 2, PAIRS, P], wkr2=[LAT, 2, 2 * ROPE], wuv=[P, H, LAT], wxo=[P, H, D],
                      xrope=[P, 4, P], itok=[P, B])
        w = {k: sb(k, s, I32 if k == "itok" else F32) for k, s in shapes.items()}
        ident = sb("ident", [P, P])
        identb = sb("identb", [P, P], BF16)
        causal = sb("causal", [P, P])
        causalb = sb("causalb", [P, P], BF16)
        own_block = sb("own_block", [P, 8])
        key_id = sb("key_id", [P, 2, P])
        ones = sb("ones", [1, P])
        wabs = sb("wabs", [QLAT, PAIRS, P])
        wuvo = sb("wuvo", [P, PAIRS, D])
        xt = sb("xt", [P, D])
        ct = sb("ct", [P, D])
        xcT = sb("xcT", [P, 4, P])
        t1 = sb("t1", [P, 4, P])
        t2 = sb("t2", [P, 4, P])
        qk = sb("qk", [P, 4, P])
        kexp = sb("kexp", [P, DC, 8, P])
        vaug = sb("vaug", [P, KV, HD + 1])
        kvT = sb("kvT", [P, P])
        key = sb("key", [P, 2, P])
        kvaug = sb("kvaug", [P, LAT + 1])
        seg = sb("seg", [P, 1])
        near = sb("near", [P, 2, P])
        segb = sb("segb", [P, P], BF16)
        pbuf = sb("pbuf", [P, 2, 4, P])
        ptbuf = sb("ptbuf", [P, 2, 4, P])
        stats = sb("stats", [P, 32])
        osb = sb("osb", [P, H, HD])
        oT = sb("oT", [P, DC, P])
        x1 = sb("x1", [P, D])
        x1T = sb("x1T", [P, DC, P])
        qcT = sb("qcT", [QLAT, P])
        Q = sb("Q", [P, PAIRS, 2, P])
        lat = sb("lat", [P, H, LAT])
        latT = sb("latT", [P, PAIRS, P])
        x2 = sb("x2", [P, D])
        M0, M1, S0, S1, T0, T1, O0, O1 = (ph.bank(n) for n in ("M0", "M1", "S0", "S1", "T0", "T1", "O0", "O1"))
        banks = ((S0, S1), (T0, T1), (O0, O1))
        self_att = Attention(ph, "self", HD, banks, pbuf, ptbuf, stats, osb, ident[:, :])
        cross_att = Attention(ph, "cross", LAT, banks, pbuf, ptbuf, stats, lat, ident[:, :])
        ln1, ln2 = LayerNorm(ph, "ln1"), LayerNorm(ph, "ln2")
        weights = sem("weights")
        pool_step, consts = sem("pool_step"), sem("consts")
        products_ready, products_copied = sem("products_ready"), sem("products_copied")
        x_loaded, ctx_loaded, x2_stored, x2_free = (sem(n) for n in ("x_loaded", "ctx_loaded", "x2_stored", "x2_free"))
        xcT_ps, xcT_ready, v_ps, v_ready, qk_ps, rope_step, qk_ready, kexp_ready = (sem(n) for n in (
            "xcT_ps", "xcT_ready", "v_ps", "v_ready", "qk_ps", "rope_step", "qk_ready", "kexp_ready"))
        kr_ps, kr_ready, seg_step = (sem(n) for n in ("kr_ps", "kr_ready", "seg_step"))
        oT_ps, oT_ready, y1_ps, x1T_ps, x1T_ready = (sem(n) for n in ("oT_ps", "oT_ready", "y1_ps", "x1T_ps", "x1T_ready"))
        qc_ps, qc_ready, Q_ps, Qa_ready, Qr_ready = (sem(n) for n in ("qc_ps", "qc_ready", "Q_ps", "Qa_ready", "Qr_ready"))
        latT_ps, latT_ready, y2_ps = (sem(n) for n in ("latT_ps", "latT_ready", "y2_ps"))
        xscale = float(np.float32(1.0) / np.sqrt(np.float32(XHD + ROPE)))
        block = ctx.enter_context(nc.Block())

        @block.sync
        def _(sp):
            for k in shapes:
                sp.dma_start(w[k][:], d[k]).then_inc(weights, 16)
            sp.dma_start(xt[:, :], batch(x_src, 0)).then_inc(x_loaded, 16)
            sp.dma_start(ct[:, :], batch(d["ctx"], 0)).then_inc(ctx_loaded, 16)
            sp.sem_inc(x2_free, 1)
            with sp.Fori(0, B - 1) as i:
                sp.wait_ge(xcT_ps, i + 1)
                sp.dma_start(ct[:, :], batch(d["ctx"], i + 1)).then_inc(ctx_loaded, 16)
                sp.wait_ge(ln1.step, at(i, ln1.DVE_STEPS, 1))
                sp.dma_start(xt[:, :], batch(x_src, i + 1)).then_inc(x_loaded, 16)
                store_batch(sp, i, ln2.done, x2[:, :], x_dst, x2_stored, x2_free)
            store_batch(sp, B - 1, ln2.done, x2[:, :], x_dst, x2_stored, x2_free)

        @block.gpsimd
        def _(pool):
            link = Linked(pool, pool_step)
            fill_identity(pool, link, ident[:, :])
            link(pool.tensor_copy(identb[:, :], ident[:, :]))
            link(pool.memset(causal[:, :], 0.0))
            link(pool.affine_select(out=causal[:, :], in_=causal[:, :], compare_op=ALU.is_ge, fill=MASKED,
                                    base=0, pattern=[[-1, P]], channel_multiplier=1))
            link(pool.tensor_copy(causalb[:, :], causal[:, :]))
            link(pool.memset(own_block[:, :], 1.0))
            link(pool.affine_select(out=own_block[:, :], in_=own_block[:, :], compare_op=ALU.is_ge, fill=0.0,
                                    base=0, pattern=[[-HD, 8]], channel_multiplier=1))
            link(pool.affine_select(out=own_block[:, :], in_=own_block[:, :], compare_op=ALU.is_ge, fill=0.0,
                                    base=HD - 1, pattern=[[HD, 8]], channel_multiplier=-1))
            link(pool.iota(key_id[:, :, :], pattern=[[LOOKBACK, 2], [1, P]], base=0, channel_multiplier=0,
                           allow_small_or_imprecise_dtypes=True))
            link(pool.memset(ones[:, :], 1.0))
            link(pool.memset(vaug[:, :, :], 1.0))
            pool.memset(kvaug[:, :], 1.0).then_inc(consts, 1)
            with pool.Fori(0, B) as i:
                for c in range(DC):
                    if c == 0:
                        pool.wait_ge(qk_ready, i + 1)
                    pool.tensor_tensor(kexp[:, c], spread(qk[:, 2 + c, :], 8), along(own_block[:, :], P), ALU.mult)\
                        .then_inc(kexp_ready, 1)

        @block.tensor
        def _(pe):
            pe.wait_ge(weights, 16 * len(shapes))
            pe.wait_ge(consts, 1)
            for h in range(H):
                bank, at0 = (M0, M1)[h // 8], (h % 8) * LAT
                pe.matmul(bank[0:QLAT, at0:at0 + LAT], w["wuq"][:, h, :], w["wuk"][:, h, :], start=True, stop=True)
            for h in range(H):
                bank, row, col = (S0, S1, T0, T1)[h // 4], LAT * (h % 2), (h // 2 % 2) * D
                last = pe.matmul(bank[row:row + LAT, col:col + D], w["wuv"][:, h, :], w["wxo"][:, h, :],
                                 start=True, stop=True)
            last.then_inc(products_ready, 1)
            pe.wait_ge(products_copied, 6)
            with pe.Fori(0, B) as i:
                pe.wait_ge(x_loaded, at(i, 16, 16))
                pe.wait_ge(ctx_loaded, at(i, 16, 16))
                for c in range(DC):
                    pe.transpose(M0[:, c * P:(c + 1) * P], xt[:, c * P:(c + 1) * P], ident[:, :])
                for c in range(DC):
                    last = pe.transpose(M0[:, (2 + c) * P:(3 + c) * P], ct[:, c * P:(c + 1) * P], ident[:, :])
                last.then_inc(xcT_ps, 1)
                pe.wait_ge(xcT_ready, i + 1)
                for c in range(DC):
                    pe.matmul(O0[:, 0:KV * HD], xcT[:, c, :], w["wv"][:, c, :], start=c == 0, stop=c == DC - 1)
                for c in range(DC):
                    pe.matmul(O0[:, 64:192], w["wkvc2"][:, c, :], xcT[:, 2 + c, :], start=c == 0, stop=c == DC - 1)
                for c in range(DC):
                    last = pe.matmul(O0[:, 192:256], xcT[:, 2 + c, :], w["wkvc2"][:, c, 0:LAT],
                                     start=c == 0, stop=c == DC - 1)
                last.then_inc(v_ps, 1)
                for r, bank in enumerate((M0, M1)):
                    for n in range(4):
                        for c in range(DC):
                            last = pe.matmul(bank[:, n * P:(n + 1) * P], w["wqk"][:, r, c, n, :], xcT[:, c, :],
                                             start=c == 0, stop=c == DC - 1)
                last.then_inc(qk_ps, 1)
                pe.wait_ge(v_ready, at(i, 5, 5))
                for r in range(2):
                    last = pe.matmul(O1[:, r * P:(r + 1) * P], w["wkr2"][:, r, :], kvT[0:LAT, :], start=True, stop=True)
                last.then_inc(kr_ps, 1)
                pe.wait_ge(kr_ready, at(i, 2, 2))
                mask4 = spread(causalb[:, :], 4)

                def self_scores(n, bank):
                    if n % 2 == 0:
                        pe.wait_ge(kexp_ready, at(i, 2, n // 2 + 1))
                    pe.matmul(four(bank[:, :]), identb[:, :], mask4, start=True, stop=False)
                    return pe.matmul(four(bank[:, :]), qk[:, n // 2, :], kexp[:, n // 2, 4 * (n % 2):4 * (n % 2) + 4, :],
                                     start=False, stop=True)

                self_att.on_tensor(pe, i, self_scores, lambda n, h: vaug[:, n, :])
                pe.wait_ge(self_att.o_done, at(i, QUADS, QUADS))
                for c in range(DC):
                    last = pe.transpose(M0[:, c * P:(c + 1) * P], osb[:, 8 * c:8 * c + 8, :].rearrange("p h d -> p (h d)"),
                                        ident[:, :])
                last.then_inc(oT_ps, 1)
                pe.wait_ge(oT_ready, i + 1)
                pe.matmul(M1[:, 0:D], ones[:, :], w["bo"][:, :], start=True, stop=False)
                for c in range(DC):
                    last = pe.matmul(M1[:, 0:D], oT[:, c, :], w["wo"][:, c, :], start=False, stop=c == DC - 1)
                last.then_inc(y1_ps, 1)
                pe.wait_ge(ln1.done, i + 1)
                for c in range(DC):
                    last = pe.transpose(M0[:, c * P:(c + 1) * P], x1[:, c * P:(c + 1) * P], ident[:, :])
                last.then_inc(x1T_ps, 1)
                pe.wait_ge(x1T_ready, i + 1)
                for c in range(DC):
                    last = pe.matmul(M0[0:QLAT, 2 * P:3 * P], w["wdq"][:, c, :], x1T[:, c, :], start=c == 0, stop=c == DC - 1)
                last.then_inc(qc_ps, 1)
                pe.wait_ge(qc_ready, i + 1)
                for half, trio in enumerate(((M0, M1, T0), (T1, O0, O1))):
                    for bank, wt in zip(trio, (wabs[:, :, :], w["wqr"][:, 0], w["wqr"][:, 1])):
                        for n in range(4):
                            last = pe.matmul(bank[:, n * P:(n + 1) * P], wt[:, 4 * half + n, :], qcT[:, :],
                                             start=True, stop=True)
                    last.then_inc(Q_ps, 1)
                pe.wait_ge(seg_step, at(i, 4, 4))
                seg4 = spread(segb[:, :], 4)

                def cross_scores(n, bank):
                    if n % 2 == 0:
                        pe.wait_ge(Qa_ready, at(i, 4, 4))
                        pe.wait_ge(Qr_ready, at(i, 4, 4))
                    pe.matmul(four(bank[:, :]), identb[:, :], seg4, start=True, stop=False)
                    for h in range(4):
                        last = pe.matmul(bank[:, h * P:(h + 1) * P], Q[:, (4 * n + h) // 2, h % 2, :], key[:, h % 2, :],
                                         start=False, stop=h == 3)
                    return last

                cross_att.on_tensor(pe, i, cross_scores, lambda n, h: kvaug[:, :])
                pe.wait_ge(cross_att.o_done, at(i, QUADS, QUADS))
                for half, bank in enumerate((M0, M1)):
                    for n in range(4):
                        pair = 4 * half + n
                        last = pe.transpose(bank[:, n * P:(n + 1) * P],
                                            lat[:, 2 * pair:2 * pair + 2, :].rearrange("p h d -> p (h d)"), ident[:, :])
                    last.then_inc(latT_ps, 1)
                for pair in range(PAIRS):
                    if pair % 4 == 0:
                        pe.wait_ge(latT_ready, at(i, 2, pair // 4 + 1))
                    last = pe.matmul(T0[:, 0:D], latT[:, pair, :], wuvo[:, pair, :], start=pair == 0, stop=pair == PAIRS - 1)
                last.then_inc(y2_ps, 1)

        @block.scalar
        def _(act):
            act.wait_ge(products_ready, 1)
            for k, bank in enumerate((M0, M1)):
                act.activation(wabs[:, 4 * k:4 * k + 4, :], four(bank[0:QLAT, :]), ACT.Copy).then_inc(products_copied, 1)
            for k, bank in enumerate((S0, S1, T0, T1)):
                act.activation(wuvo[:, 2 * k:2 * k + 2, :], bank[:, :].rearrange("p (a n) -> p a n", a=2), ACT.Copy)\
                   .then_inc(products_copied, 1)
            with act.Fori(0, B) as i:
                act.wait_ge(xcT_ps, i + 1)
                act.activation(xcT[:, :, :], four(M0[:, :]), ACT.Copy).then_inc(xcT_ready, 1)
                act.wait_ge(v_ps, i + 1)
                act.activation(vaug[:, :, 0:HD], O0[:, 0:64].rearrange("p (g d) -> p g d", g=KV), ACT.Copy).then_inc(v_ready, 1)
                act.activation(kvT[:, :], O0[:, 64:192], ACT.Copy).then_inc(v_ready, 1)
                for parity in range(2):
                    rows = slice(LAT * parity, LAT * parity + LAT)
                    act.activation(key[rows, parity, :], O0[rows, 64:192], ACT.Copy).then_inc(v_ready, 1)
                act.activation(kvaug[:, 0:LAT], O0[:, 192:256], ACT.Copy).then_inc(v_ready, 1)
                self_att.on_scalar(act, i)
                act.wait_ge(oT_ps, i + 1)
                act.activation(oT[:, :, :], M0[:, 0:D].rearrange("p (c n) -> p c n", c=DC), ACT.Copy).then_inc(oT_ready, 1)
                ln1.on_scalar(act, i)
                act.wait_ge(x1T_ps, i + 1)
                act.activation(x1T[:, :, :], M0[:, 0:D].rearrange("p (c n) -> p c n", c=DC), ACT.Copy).then_inc(x1T_ready, 1)
                act.wait_ge(qc_ps, i + 1)
                act.activation(qcT[:, :], M0[0:QLAT, 2 * P:3 * P], ACT.Copy).then_inc(qc_ready, 1)
                for half, bank in enumerate((M0, T1)):
                    act.wait_ge(Q_ps, at(i, 2, half + 1))
                    for parity in range(2):
                        rows = slice(LAT * parity, LAT * parity + LAT)
                        act.activation(Q[rows, 4 * half:4 * half + 4, parity, :], four(bank[rows, :]), ACT.Copy,
                                       scale=xscale).then_inc(Qa_ready, 1)
                cross_att.on_scalar(act, i)
                for half, bank in enumerate((M0, M1)):
                    act.wait_ge(latT_ps, at(i, 2, half + 1))
                    act.activation(latT[:, 4 * half:4 * half + 4, :], four(bank[:, :]), ACT.Copy).then_inc(latT_ready, 1)
                ln2.on_scalar(act, i)

        @block.vector
        def _(dve):
            dve.wait_ge(weights, 16 * len(shapes))
            dve.wait_ge(consts, 1)

            ALL = slice(0, P)
            OTHER = (slice(LAT, P), slice(0, LAT))

            def rotate(link, done, out, plain, swapped, cos, sin, n):
                link(dve.tensor_tensor(t1[:, 0:n, :], plain, spread(cos, n), ALU.mult))
                link(dve.tensor_tensor(t2[:, 0:n, :], swapped, spread(sin, n), ALU.mult))
                for rows, part in out:
                    dve.tensor_tensor(part, t1[rows, 0:n, :], t2[rows, 0:n, :], ALU.add).then_inc(done, 1)

            with dve.Fori(0, B) as i:
                link = Linked(dve, seg_step, 4, i)
                link(dve.tensor_copy(seg[:, :], w["itok"][:, bass.ds(i, 1)]))
                link(dve.tensor_scalar(near[:, 0, :], key_id[:, 0, :], seg[:, :], MASKED, ALU.is_gt, ALU.mult))
                link(dve.tensor_scalar(near[:, 1, :], key_id[:, 1, :], seg[:, :], MASKED, ALU.is_lt, ALU.mult))
                link(dve.tensor_tensor(segb[:, :], near[:, 0, :], near[:, 1, :], ALU.add))
                link.close()
                link = Linked(dve, rope_step, 8, i)
                dve.wait_ge(qk_ps, i + 1)
                rotate(link, qk_ready, [(ALL, qk[:, :, :])], four(M0[:, :]), four(M1[:, :]), w["rope"][:, 0, :], w["rope"][:, 1, :], 4)
                dve.wait_ge(kr_ps, i + 1)
                dve.wait_ge(qk_ready, i + 1)
                rotate(link, kr_ready, [(r, key[r, q, :].unsqueeze(1)) for q, r in enumerate(OTHER)], O1[:, 0:P].unsqueeze(1), O1[:, P:2 * P].unsqueeze(1),
                       w["xrope"][:, 0, :], w["xrope"][:, 1, :], 1)
                self_att.on_vector(dve, i)
                dve.wait_ge(y1_ps, i + 1)
                ln1.on_vector(dve, i, x1[:, :], xt[:, :], M1[:, 0:D])
                dve.wait_ge(kr_ready, at(i, 2, 2))
                for half, (plain, swapped) in enumerate(((M1, T0), (O0, O1))):
                    dve.wait_ge(Q_ps, at(i, 2, half + 1))
                    if half:
                        dve.wait_ge(Qr_ready, at(i, 4, 2))
                    rotate(link, Qr_ready, [(r, Q[r, 4 * half:4 * half + 4, q, :]) for q, r in enumerate(OTHER)], four(plain[:, :]), four(swapped[:, :]),
                           w["xrope"][:, 2, :], w["xrope"][:, 3, :], 4)
                link.close()
                cross_att.on_vector(dve, i)
                dve.wait_ge(y2_ps, i + 1)
                dve.wait_ge(x2_free, i + 1)
                ln2.on_vector(dve, i, x2[:, :], x1[:, :], T0[:, 0:D])


def layout_layer0_attention(inp):
    f = np.float32
    by_chunk = lambda a: np.ascontiguousarray(a.reshape(DC, P, -1).transpose(1, 0, 2))
    half = HD // 2
    Wq = inp["L0_attn_Wq"].reshape(D, DC, P)
    Wk = inp["L0_attn_Wk"].reshape(D, DC, 2, HD).repeat(4, axis=2).reshape(D, DC, P)
    plain = np.concatenate([Wq, Wk], axis=1)
    swap = plain.reshape(D, 4, 8, 2, half)[:, :, :, ::-1].reshape(D, 4, P)
    wqk = np.stack([plain, swap]).reshape(2, DC, P, 4, P).transpose(2, 0, 1, 3, 4)
    inv = (1.0 / f(10000.0) ** (np.arange(0, HD, 2, dtype=f) / f(HD))).astype(f)
    ang = np.outer(np.arange(S, dtype=f), inv).astype(f)
    row = np.arange(P)
    sign = np.where(row % HD < half, -1, 1).astype(f)[:, None]
    root = f(0.5)
    rope = np.stack([root * np.cos(ang).T[row % half], root * sign * np.sin(ang).T[row % half]], axis=1)
    xh = ROPE // 2
    xinv = (1.0 / f(10000.0) ** (np.arange(xh, dtype=f) / f(xh))).astype(f)
    xang = (np.arange(S, dtype=f)[:, None] * xinv).astype(f)
    xsign = np.where(row % ROPE < xh, -1, 1).astype(f)[:, None]
    xc, xs = np.cos(xang).T[row % xh], xsign * np.sin(xang).T[row % xh]
    scale = f(1.0) / np.sqrt(f(XHD + ROPE))
    xrope = np.stack([xc, xs, xc * scale, xs * scale], axis=1)
    Wkvc = inp["L0_xattn_W_kvc"]
    Wqr = inp["L0_xattn_W_qr"].reshape(QLAT, PAIRS, 2, ROPE)[:, :, ::-1]
    Wqr_s = Wqr.reshape(QLAT, PAIRS, 2, 2, xh)[:, :, :, ::-1]
    Wkr = inp["L0_xattn_W_kr"]
    Wkr_s = Wkr.reshape(LAT, 2, xh)[:, ::-1].reshape(LAT, ROPE)
    head_d = lambda a, n: a.reshape(n, H, XHD).transpose(2, 1, 0)
    out = dict(
        ctx=inp["ctx_2048"], wqk=wqk, wv=by_chunk(inp["L0_attn_Wv"]), wo=by_chunk(inp["L0_attn_Wo"]),
        bo=inp["L0_attn_bo"].reshape(1, D), rope=rope, wkvc2=by_chunk(np.concatenate([Wkvc, Wkvc], axis=1)),
        wdq=by_chunk(inp["L0_xattn_W_dq"]), wuq=head_d(inp["L0_xattn_W_uq"], QLAT), wuk=head_d(inp["L0_xattn_W_uk"], LAT),
        wqr=np.stack([Wqr.reshape(QLAT, PAIRS, P), Wqr_s.reshape(QLAT, PAIRS, P)], axis=1),
        wkr2=np.stack([np.concatenate([a, a], axis=1) for a in (Wkr, Wkr_s)], axis=1),
        wuv=head_d(inp["L0_xattn_W_uv"], LAT), wxo=inp["L0_xattn_W_o"].reshape(H, XHD, D).transpose(1, 0, 2),
        xrope=xrope, itok=inp["itok_BxS_0_1023"].T)
    return out


EXPERTS, TOP, INNER = 16, 4, 176
EPAIR = 2 * INNER
EP = EXPERTS // 2 + 1
ECH = 3
EREST = EPAIR - 2 * P


def layer0_experts(nc, sems, d, x_src, x_dst):
    ctx = ExitStack()
    with ctx:
        ph = Phase(nc, "b", ctx, sems)
        sb, sem = ph.sb, ph.sem
        wgate = sb("wgate", [P, DC, EXPERTS])
        wup = sb("wup", [P, EP, 2, DC, EPAIR])
        wdown = sb("wdown", [P, EP, ECH, D])
        ident = sb("ident", [P, P])
        before = sb("before", [P, EXPERTS, EXPERTS])
        xt = sb("xt", [P, D])
        xT = sb("xT", [P, DC, P])
        col = sb("col", [P, 4])
        prob = sb("prob", [P, 2, EXPERTS])
        cmp_ = sb("cmp", [P, 2, EXPERTS, EXPERTS])
        rank = sb("rank", [P, EXPERTS])
        route = sb("route", [P, 2 * EP])
        sg = sb("sg", [P, 2, EPAIR])
        act_ = sb("act", [P, 2, ECH * P])
        aT = sb("aT", [P, 2, ECH, P])
        xo = sb("xo", [P, D])
        G0, G1, U0, U1, T0, T1, Y, M = (ph.bank(n) for n in ("G0", "G1", "U0", "U1", "T0", "T1", "Y", "M"))
        G, U, T = (G0, G1), (U0, U1), (T0, T1)
        ln = LayerNorm(ph, "ln")
        weights, pool_step, consts, x_loaded, stored = (sem(n) for n in ("weights", "pool_step", "consts", "x_loaded", "stored"))
        xo_free = sem("xo_free")
        pair_loaded = [sem(f"pair{e}_loaded") for e in range(EP)]
        xT_ps, xT_ready, logits_ready, route_step, exp_ready, route_ready = (sem(n) for n in (
            "xT_ps", "xT_ready", "logits_ready", "route_step", "exp_ready", "route_ready"))
        up_ready, silu_ready, act_ready, aT_ps, aT_ready, y_ready = (sem(n) for n in (
            "up_ready", "silu_ready", "act_ready", "aT_ps", "aT_ready", "y_ready"))
        ROUTE = 11
        block = ctx.enter_context(nc.Block())

        @block.sync
        def _(sp):
            sp.dma_start(xt[:, :], batch(x_src, 0)).then_inc(x_loaded, 16)
            sp.dma_start(wgate[:], d["wgate"]).then_inc(weights, 16)
            for e in range(EP):
                sp.dma_start(wup[:, e], d["wup"][:, e]).then_inc(pair_loaded[e], 16)
                sp.dma_start(wdown[:, e], d["wdown"][:, e]).then_inc(pair_loaded[e], 16)
            sp.sem_inc(xo_free, 1)
            with sp.Fori(0, B - 1) as i:
                sp.wait_ge(ln.step, at(i, ln.DVE_STEPS, 1))
                sp.dma_start(xt[:, :], batch(x_src, i + 1)).then_inc(x_loaded, 16)
                store_batch(sp, i, ln.done, xo[:, :], x_dst, stored, xo_free)
            store_batch(sp, B - 1, ln.done, xo[:, :], x_dst, stored, xo_free)

        @block.gpsimd
        def _(pool):
            link = Linked(pool, pool_step)
            fill_identity(pool, link, ident[:, :])
            link(pool.memset(before[:, :, :], 1.0))
            link(pool.affine_select(out=before[:, :, :], in_=before[:, :, :], compare_op=ALU.is_ge, fill=0.0, base=-1,
                                    pattern=[[1, EXPERTS], [-1, EXPERTS]], channel_multiplier=0))
            link(pool.memset(act_[:, :, :], 0.0))
            pool.memset(route[:, :], 1.0).then_inc(consts, 1)

        @block.tensor
        def _(pe):
            pe.wait_ge(weights, 16)
            pe.wait_ge(consts, 1)
            with pe.Fori(0, B) as i:
                pe.wait_ge(x_loaded, at(i, 16, 16))
                for c in range(DC):
                    last = pe.transpose(M[:, c * P:(c + 1) * P], xt[:, c * P:(c + 1) * P], ident[:, :])
                last.then_inc(xT_ps, 1)
                pe.wait_ge(xT_ready, i + 1)
                for c in range(DC):
                    last = pe.matmul(M[:, D:D + EXPERTS], xT[:, c, :], wgate[:, c, :], start=c == 0, stop=c == DC - 1)
                last.then_inc(logits_ready, 1)
                for s in range(EP + 2):
                    if s < EP:
                        pe.wait_ge(pair_loaded[s], 32)
                        if s >= 2:
                            pe.wait_ge(act_ready, at(i, 2 * EP, 2 * s - 2))
                        for k, bank in enumerate((G[s % 2], U[s % 2])):
                            for c in range(DC):
                                last = pe.matmul(bank[:, 0:EPAIR], xT[:, c, :], wup[:, s, k, c, :], start=c == 0, stop=c == DC - 1)
                        last.then_inc(up_ready, 1)
                    if 1 <= s <= EP:
                        n = s - 1
                        pe.wait_ge(act_ready, at(i, 2 * EP, 2 * n + 2))
                        if n >= 2:
                            pe.wait_ge(aT_ready, at(i, EP, n - 1))
                        for c in range(ECH):
                            last = pe.transpose(T[n % 2][:, c * P:(c + 1) * P], act_[:, n % 2, c * P:(c + 1) * P], ident[:, :])
                        last.then_inc(aT_ps, 1)
                    if s >= 2:
                        n = s - 2
                        pe.wait_ge(aT_ready, at(i, EP, n + 1))
                        for c in range(ECH):
                            rows = P if c < 2 else EREST
                            last = pe.matmul(Y[:, 0:D], aT[0:rows, n % 2, c, :], wdown[0:rows, n, c, :],
                                             start=n == 0 and c == 0, stop=n == EP - 1 and c == ECH - 1)
                        last.then_inc(y_ready, 1)

        @block.scalar
        def _(act):
            with act.Fori(0, B) as i:
                act.wait_ge(xT_ps, i + 1)
                act.activation(xT[:, :, :], M[:, 0:D].rearrange("p (c n) -> p c n", c=DC), ACT.Copy).then_inc(xT_ready, 1)
                act.wait_ge(route_step, at(i, ROUTE, 2))
                act.activation(prob[:, 0, :], prob[:, 0, :], ACT.Exp).then_inc(exp_ready, 1)
                for s in range(EP + 1):
                    if s < EP:
                        act.wait_ge(up_ready, at(i, EP, s + 1))
                        if s >= 2:
                            act.wait_ge(act_ready, at(i, 2 * EP, 2 * s - 2))
                        act.activation(sg[:, s % 2, :], G[s % 2][:, 0:EPAIR], ACT.Silu).then_inc(silu_ready, 1)
                    if s >= 1:
                        n = s - 1
                        act.wait_ge(aT_ps, at(i, EP, n + 1))
                        if n >= 2:
                            act.wait_ge(y_ready, at(i, EP, n - 1))
                        act.activation(aT[:, n % 2], T[n % 2][:, 0:ECH * P].rearrange("p (c n) -> p c n", c=ECH), ACT.Copy)\
                           .then_inc(aT_ready, 1)
                ln.on_scalar(act, i)

        @block.vector
        def _(dve):
            dve.wait_ge(consts, 1)
            with dve.Fori(0, B) as i:
                link = Linked(dve, route_step, ROUTE, i)
                dve.wait_ge(logits_ready, i + 1)
                logits = M[:, D:D + EXPERTS]
                link(dve.tensor_reduce(col[:, 0:1], logits, AX.X, ALU.max))
                link(dve.tensor_scalar(prob[:, 0, :], logits, col[:, 0:1], None, ALU.subtract))
                dve.wait_ge(exp_ready, i + 1)
                link(dve.tensor_reduce(col[:, 1:2], prob[:, 0, :], AX.X, ALU.add))
                link(dve.reciprocal(col[:, 2:3], col[:, 1:2]))
                link(dve.tensor_scalar(prob[:, 1, :], prob[:, 0, :], col[:, 2:3], None, ALU.mult))
                pj, pi = spread(prob[:, 1, :], EXPERTS), along(prob[:, 1, :], EXPERTS)
                link(dve.tensor_tensor(cmp_[:, 0], pj, pi, ALU.is_gt))
                link(dve.tensor_tensor(cmp_[:, 1], pj, pi, ALU.is_equal))
                link(dve.tensor_tensor(cmp_[:, 1], cmp_[:, 1], before[:, :, :], ALU.mult))
                link(dve.tensor_tensor(cmp_[:, 0], cmp_[:, 0], cmp_[:, 1], ALU.add))
                link(dve.tensor_reduce(rank[:, :], cmp_[:, 0], AX.X, ALU.add))
                link(dve.scalar_tensor_tensor(route[:, 0:EXPERTS], rank[:, :], TOP - 0.5, prob[:, 1, :], ALU.is_lt, ALU.mult))
                link.close()
                for s in range(EP):
                    dve.wait_ge(silu_ready, at(i, EP, s + 1))
                    if s >= 2:
                        dve.wait_ge(aT_ps, at(i, EP, s - 1))
                    for j in range(2):
                        cols = slice(j * INNER, (j + 1) * INNER)
                        dve.scalar_tensor_tensor(act_[:, s % 2, cols], sg[:, s % 2, cols], route[:, 2 * s + j:2 * s + j + 1],
                                                 U[s % 2][:, cols], ALU.mult, ALU.mult).then_inc(act_ready, 1)
                dve.wait_ge(y_ready, at(i, EP, EP))
                dve.wait_ge(xo_free, i + 1)
                ln.on_vector(dve, i, xo[:, :], xt[:, :], Y[:, 0:D])


def layout_layer0_experts(inp):
    def up(routed, shared):
        pairs = inp[routed].reshape(EP - 1, 2, D, INNER).transpose(0, 2, 1, 3).reshape(EP - 1, D, EPAIR)
        return np.concatenate([pairs, inp[shared][None]]).reshape(EP, DC, P, EPAIR)
    wup = np.stack([up("L0_ffn_wg", "L0_ffn_sg"), up("L0_ffn_wu", "L0_ffn_su")]).transpose(3, 1, 0, 2, 4)
    down = np.concatenate([inp["L0_ffn_wd"].reshape(EP - 1, EPAIR, D), inp["L0_ffn_sd"][None]])
    down = np.concatenate([down, np.zeros((EP, ECH * P - EPAIR, D), np.float32)], axis=1)
    return dict(wgate=inp["L0_ffn_w_gate"].T.reshape(DC, P, EXPERTS).transpose(1, 0, 2), wup=wup,
                wdown=down.reshape(EP, ECH, P, D).transpose(2, 0, 1, 3))


KEY_HEADS, VAL_HEADS, DK, TAPS = 16, 32, 128, 4
HB = 4
KB = HB // 2
ROUNDS = VAL_HEADS // HB
ITEMS = HB * B
QK = 2 * KB
CHUNKS = QK + HB
BL = 32
NBL = S // BL
RMS_EPS = 1e-6
TINY = 1e-12


def layer1_delta_rule(nc, sems, d, x_src, x_dst):
    ctx = ExitStack()
    with ctx:
        ph = Phase(nc, "c", ctx, sems)
        sb, sem = ph.sb, ph.sem
        ident = sb("ident", [P, P])
        identb = sb("identb", [P, P], BF16)
        tri = sb("tri", [P, P])
        hidden = sb("hidden", [P, P])
        hiddenb = sb("hiddenb", [P, P], BF16)
        ones = sb("ones", [P, 1])
        zero = sb("zero", [P, 1])
        wba = sb("wba", [P, DC, 2 * VAL_HEADS])
        bias = sb("bias", [P, 2, VAL_HEADS])
        normw = sb("normw", [P, 1])
        wqkv = sb("wqkv", [P, CHUNKS, DC * P])
        wconv = sb("wconv", [P, CHUNKS, TAPS])
        wz = sb("wz", [P, DC, HB * P])
        wout = sb("wout", [P, HB, D])
        acc = sb("acc", [P, B, D])
        xT = sb("xT", [P, DC, B, P])
        sm = sb("sm", [P, 4, B, VAL_HEADS])
        beta = sb("beta", [P, B, VAL_HEADS])
        g = sb("g", [P, B, VAL_HEADS])
        gcn = sb("gcn", [P, B, VAL_HEADS])
        gR, gcnR, betaR = (sb(n, [P, HB, B]) for n in ("gR", "gcnR", "betaR"))
        pad = sb("pad", [P, 2, B, TAPS - 1 + S])
        cv = sb("cv", [P, 2, B, S])
        qkT = sb("qkT", [P, KB, 2, B, S])
        sq = sb("sq", [P, 2, B, S])
        nrm = sb("nrm", [P, 3, KB, 2, B])
        cj = sb("cj", [P, HB, B])
        V = sb("V", [P, HB, B, S])
        NP = sb("NP", [P, HB, B, 2, S])
        A = sb("A", [P, BL, BL])
        T = sb("T", [P, BL, BL])
        T0 = sb("T0", [P, BL, BL])
        tmp = sb("tmp", [P, 256])
        Tb = sb("Tb", [P, ITEMS, P])
        TbT = sb("TbT", [P, ITEMS, P])
        Y = sb("Y", [P, HB, B, S])
        zs = qkT[:, :, :, :, :].rearrange("p k q b s -> p (k q b s)").rearrange("p (b n) -> p b n", b=B)
        s2 = sb("s2", [P, HB, B])
        f = sb("f", [P, 3, HB, B])
        yT = sb("yT", [P, 2, HB, S])
        banks = [ph.bank(f"bank{n}") for n in range(8)]
        blocks = nc.dram_tensor("diagonal_blocks", (3, NBL, ITEMS, BL, BL), F32, kind="Internal").ap()
        names = """blocks_out inverse_out weights consts pool_step x_loaded xT_ps xT_copied ba_ps gate_step gate_act gc_ps gates_ready
            round_loaded round_copied gates_used proj_ready pad_ready tap0_ready conv_step cv_ready silu_ready sq_ready norms_ps
            root_ready norm_step gcrow_ps E_ready GP_ps NP_ready gathered elim_step scattered diag_cleared
            vt_ps V_ready z_ps z_ready MT_ps MT_ready apply_ps y_ready W_ps W_ready C_ps C_ready csq_ready s2_ready
            wout_ready var_ready rstd_log rstd_ready f_step y_scaled yT_ps yT_ready out_ps acc_step
            ln_step ln_log ln_rstd xo_ready stored""".split()
        s = {n: sem(n) for n in names}
        quads = [(h, q) for h in range(HB) for q in range(2)]
        flat = lambda ap: ap.rearrange("p a b -> p (a b)")
        ELIM = 2 * (BL - 1) + 2
        block = ctx.enter_context(nc.Block())

        def rr(t, h, q):
            return t[:, h, 4 * q:4 * q + 4]

        @block.sync
        def _(sp):
            for dst, k in ((wba, "wba"), (bias, "bias"), (normw, "normw")):
                sp.dma_start(dst[:], d[k]).then_inc(s["weights"], 16)
            sp.dma_start(acc[:, :, :], x_src.rearrange("b p c -> p b c")).then_inc(s["x_loaded"], 16)

            def load(dst, name, i):
                sp.dma_start(dst[:], d[name][bass.ds(i, 1)].rearrange("a p m n -> (a p) m n")).then_inc(s["round_loaded"], 16)

            def invert(i):
                sp.wait_ge(s["NP_ready"], at(i, ITEMS, ITEMS))
                for r in range(NBL):
                    rows = slice(BL * r, BL * r + BL)
                    sp.dma_start(blocks[0, r].rearrange("t j i -> j t i"), NP[rows, :, :, 0, rows].rearrange("p h b i -> p (h b) i"))\
                        .then_inc(s["blocks_out"], 16)
                sp.wait_ge(s["blocks_out"], at(i, 16 * NBL, 16 * NBL))
                sp.dma_start(A[:, :, :], blocks[0].rearrange("r t j i -> (r t) j i")).then_inc(s["gathered"], 16)
                for n, src in ((1, T), (2, A)):
                    sp.wait_ge(s["elim_step"], at(i, ELIM, ELIM - 2 + n))
                    sp.dma_start(blocks[n].rearrange("r t i k -> (r t) i k"), src[:, :, :]).then_inc(s["inverse_out"], 16)
                for n, dst in ((1, Tb), (2, TbT)):
                    if n == 1:
                        sp.wait_ge(s["inverse_out"], at(i, 32, 32))
                    for r in range(NBL):
                        rows = slice(BL * r, BL * r + BL)
                        sp.dma_start(dst[rows, :, rows], blocks[n, r].rearrange("t i k -> i t k")).then_inc(s["scattered"], 16)

            for dst, name in ((wqkv, "wqkv"), (wconv, "wconv"), (wz, "wz"), (wout, "wout")):
                load(dst, name, 0)
            with sp.Fori(0, ROUNDS - 1) as i:
                invert(i)
                sp.wait_ge(s["proj_ready"], at(i, CHUNKS, CHUNKS))
                load(wqkv, "wqkv", i + 1)
                sp.wait_ge(s["cv_ready"], at(i, CHUNKS, CHUNKS))
                load(wconv, "wconv", i + 1)
                sp.wait_ge(s["z_ps"], at(i, B, B))
                load(wz, "wz", i + 1)
                sp.wait_ge(s["out_ps"], at(i, B, B))
                load(wout, "wout", i + 1)
            invert(ROUNDS - 1)
            with sp.Fori(0, B) as b:
                sp.wait_ge(s["xo_ready"], b + 1)
                sp.dma_start(x_dst[bass.ds(b, 1)].rearrange("a p c -> p a c"), acc[:, bass.ds(b, 1), :]).then_inc(s["stored"], 16)
            sp.wait_ge(s["stored"], 16 * B)

        @block.gpsimd
        def _(pool):
            link = Linked(pool, s["pool_step"])
            fill_identity(pool, link, ident[:, :])
            link(pool.tensor_copy(identb[:, :], ident[:, :]))
            link(pool.memset(tri[:, :], 1.0))
            link(pool.affine_select(out=tri[:, :], in_=tri[:, :], compare_op=ALU.is_ge, fill=0.0, base=0,
                                    pattern=[[1, P]], channel_multiplier=-1))
            link(pool.memset(hidden[:, :], 0.0))
            link(pool.affine_select(out=hidden[:, :], in_=hidden[:, :], compare_op=ALU.is_ge, fill=MASKED, base=0,
                                    pattern=[[1, P]], channel_multiplier=-1))
            link(pool.tensor_copy(hiddenb[:, :], hidden[:, :]))
            link(pool.memset(T0[:, :, :], 0.0))
            link(pool.affine_select(out=T0[:, :, :], in_=T0[:, :, :], compare_op=ALU.not_equal, fill=1.0, base=0,
                                    pattern=[[1, BL], [-1, BL]], channel_multiplier=0))
            link(pool.memset(zero[:, :], 0.0))
            link(pool.memset(Tb[:, :, :], 0.0))
            link(pool.memset(TbT[:, :, :], 0.0))
            link(pool.memset(pad[:, :, :, :], 0.0))
            pool.memset(ones[:, :], 1.0).then_inc(s["consts"], 1)
            with pool.Fori(0, ROUNDS) as i:
                pool.wait_ge(s["round_loaded"], at(i, 64, 64))
                pool.wait_ge(s["weights"], 48)
                pool.tensor_tensor(flat(wout[:, :, :]), flat(wout[:, :, :]), normw[:, 0:1].broadcast_to([P, HB * D]), ALU.mult).then_inc(s["wout_ready"], 1)

                def tap0(m):
                    pool.wait_ge(s["pad_ready"], at(i, 2 * CHUNKS, 2 * m + 2))
                    if m >= 2:
                        pool.wait_ge(s["silu_ready"], at(i, CHUNKS, m - 1))
                    if m >= QK + 2:
                        pool.wait_ge(s["vt_ps"], at(i, 2 * HB, 2 * (m - QK - 1)))
                    pool.tensor_tensor(cv[:, m % 2], pad[:, m % 2, :, 0:S], along(wconv[:, m, 0:1].broadcast_to([P, B]), S), ALU.mult)\
                        .then_inc(s["tap0_ready"], 1)

                def square(m):
                    pool.wait_ge(s["silu_ready"], at(i, CHUNKS, m + 1))
                    if m >= 2:
                        pool.wait_ge(s["norms_ps"], at(i, QK, m - 1))
                    src = qkT[:, m // 2, m % 2]
                    pool.tensor_tensor(sq[:, m % 2], src, src, ALU.mult).then_inc(s["sq_ready"], 1)

                for m in range(QK + 2):
                    if m < QK + 1:
                        tap0(m)
                    if 1 <= m <= QK:
                        square(m - 1)
                for m in range(QK + 1, CHUNKS):
                    tap0(m)
                pool.wait_ge(s["blocks_out"], at(i, 16 * NBL, 16 * NBL))
                pool.wait_ge(s["tap0_ready"], at(i, CHUNKS, CHUNKS))
                for r in range(NBL):
                    rows = slice(BL * r, BL * r + BL)
                    if r:
                        pool.wait_ge(s["diag_cleared"], at(i, NBL, r))
                    none = along(zero[rows, 0:1].broadcast_to([BL, ITEMS]), BL)
                    pool.tensor_tensor(NP[rows, :, :, 0, rows].rearrange("p h b i -> p (h b) i"), none, none, ALU.add)\
                        .then_inc(s["diag_cleared"], 1)
                pool.wait_ge(s["diag_cleared"], at(i, NBL, NBL))
                for n, (h, q) in enumerate(quads):
                    pool.wait_ge(s["C_ready"], at(i, 8, n + 1))
                    pool.tensor_tensor(rr(V, h, q), rr(Y, h, q), rr(Y, h, q), ALU.mult).then_inc(s["csq_ready"], 1)

        @block.tensor
        def _(pe):
            pe.wait_ge(s["consts"], 1)
            pe.wait_ge(s["x_loaded"], 16)
            for b in range(B):
                bank = banks[b // 2]
                for c in range(DC):
                    last = pe.transpose(bank[:, (2 * (b % 2) + c) * P:(2 * (b % 2) + c + 1) * P], acc[:, b, c * P:(c + 1) * P],
                                        ident[:, :])
                last.then_inc(s["xT_ps"], 1)
            pe.wait_ge(s["weights"], 48)
            pe.wait_ge(s["xT_copied"], 4)
            for b in range(B):
                for c in range(DC):
                    last = pe.matmul(banks[4][:, 64 * b:64 * b + 64], xT[:, c, b, :], wba[:, c, :], start=c == 0, stop=c == DC - 1)
            last.then_inc(s["ba_ps"], 1)
            pe.wait_ge(s["gate_step"], 6)
            pe.matmul(banks[5][:, 0:B * VAL_HEADS], tri[:, :], flat(g[:, :, :]), start=True, stop=True).then_inc(s["gc_ps"], 1)
            with pe.Fori(0, ROUNDS) as i:
                pe.wait_ge(s["round_loaded"], at(i, 64, 64))

                def project(m):
                    if m >= 2:
                        pe.wait_ge(s["pad_ready"], at(i, 2 * CHUNKS, 2 * (m - 1)))
                    for q in range(2):
                        bank = banks[2 * (m % 2) + q]
                        for c in range(DC):
                            last = pe.matmul(four(bank[:, :]), wqkv[:, m, c * P:(c + 1) * P], xT[:, c, 4 * q:4 * q + 4, :],
                                             start=c == 0, stop=c == DC - 1)
                    last.then_inc(s["proj_ready"], 1)

                def norms(m):
                    pe.wait_ge(s["sq_ready"], at(i, QK, m + 1))
                    for b in range(B):
                        last = pe.matmul(banks[7][:, m * B + b:m * B + b + 1], sq[:, m % 2, b, :], ones[:, :], start=True, stop=True)
                    last.then_inc(s["norms_ps"], 1)

                def gcrow(n):
                    h, q = order[n]
                    bank = banks[4 + n % 2]
                    if n >= 2:
                        pe.wait_ge(s["E_ready"], at(i, ITEMS, 4 * (n - 1)))
                    pe.matmul(four(bank[:, :]), identb[:, :], spread(hiddenb[:, :], 4), start=True, stop=False)
                    for b in range(4):
                        last = pe.matmul(bank[:, b * P:(b + 1) * P], gR[:, h, 4 * q + b:4 * q + b + 1].broadcast_to([P, P]), tri[:, :],
                                         start=False, stop=b == 3)
                    last.then_inc(s["gcrow_ps"], 1)

                def gram(u):
                    k, b0 = u // 4, 2 * (u % 4)
                    bank = banks[6 + u % 2]
                    if u == 0:
                        pe.wait_ge(s["silu_ready"], at(i, CHUNKS, QK))
                        pe.wait_ge(s["root_ready"], i + 1)
                    if u >= 2:
                        pe.wait_ge(s["NP_ready"], at(i, ITEMS, 8 * ((u - 2) // 2) + 8))
                    for b in range(2):
                        last = pe.matmul(bank[:, b * 2 * P:(b + 1) * 2 * P].rearrange("p (a n) -> p a n", a=2),
                                         qkT[:, k, 0, b0 + b, :], qkT[:, k, :, b0 + b, :], start=True, stop=True)
                    last.then_inc(s["GP_ps"], 1)

                for m in range(QK + 1):
                    project(m)
                    if m >= 2:
                        norms(m - 2)
                norms(QK - 1)
                order = [(2 * k + e, q) for k in range(KB) for q in range(2) for e in range(2)]
                pe.wait_ge(s["gates_used"], at(i, 3, 3))
                for grp in range(4):
                    gcrow(2 * grp)
                    gcrow(2 * grp + 1)
                    gram(2 * grp)
                    gram(2 * grp + 1)

                def values(n):
                    pe.wait_ge(s["silu_ready"], at(i, CHUNKS, QK + n + 1))
                    if n == 0:
                        pe.wait_ge(s["E_ready"], at(i, ITEMS, ITEMS))
                    for q in range(2):
                        bank = banks[4 + q]
                        if n >= 1:
                            pe.wait_ge(s["V_ready"], at(i, 2 * HB, 2 * n - 1 + q))
                        for b in range(4):
                            last = pe.transpose(bank[:, b * P:(b + 1) * P], cv[:, (QK + n) % 2, 4 * q + b, :], ident[:, :])
                        last.then_inc(s["vt_ps"], 1)

                for n in range(HB):
                    if n + 1 < HB:
                        project(QK + n + 1)
                    values(n)
                for b in range(B):
                    bank = banks[4 + b % 2]
                    if b == 0:
                        pe.wait_ge(s["NP_ready"], at(i, ITEMS, ITEMS))
                    pe.wait_ge(s["V_ready"], at(i, 2 * HB, 2 * HB))
                    if b >= 2:
                        pe.wait_ge(s["z_ready"], at(i, B, b - 1))
                    for c in range(DC):
                        last = pe.matmul(bank[:, :], xT[:, c, b, :], wz[:, c, :], start=c == 0, stop=c == DC - 1)
                    last.then_inc(s["z_ps"], 1)
                pe.wait_ge(s["scattered"], at(i, 128, 128))
                pe.wait_ge(s["diag_cleared"], at(i, NBL, NBL))
                pe.wait_ge(s["pad_ready"], at(i, 2 * CHUNKS, 2 * CHUNKS))
                for n, (h, q) in enumerate(quads):
                    bank = banks[n % 4]
                    if n >= 4:
                        pe.wait_ge(s["MT_ready"], at(i, 8, n - 3))
                    for b in range(4):
                        last = pe.matmul(bank[:, b * P:(b + 1) * P], Tb[:, h * B + 4 * q + b, :], NP[:, h, 4 * q + b, 0, :],
                                         start=True, stop=True)
                    last.then_inc(s["MT_ps"], 1)
                for rep in range(3):
                    for n, (h, q) in enumerate(quads):
                        bank = banks[n % 4]
                        if rep == 0:
                            pe.wait_ge(s["MT_ready"], at(i, 8, min(n + 5, 8)))
                        else:
                            pe.wait_ge(s["y_ready"], at(i, 24, 8 * (rep - 1) + n + 1))
                        if n >= 4 or rep:
                            pe.wait_ge(s["y_ready"], at(i, 24, 8 * rep + n - 3))
                        for b in range(4):
                            y = V if rep == 0 else Y
                            last = pe.matmul(bank[:, b * P:(b + 1) * P], NP[:, h, 4 * q + b, 0, :], y[:, h, 4 * q + b, :],
                                             start=True, stop=True)
                        last.then_inc(s["apply_ps"], 1)
                for n, (h, q) in enumerate(quads):
                    bank = banks[n % 4]
                    pe.wait_ge(s["y_ready"], at(i, 24, 16 + max(n + 1, min(n + 5, 8))))
                    if n >= 4:
                        pe.wait_ge(s["W_ready"], at(i, 8, n - 3))
                    for b in range(4):
                        last = pe.matmul(bank[:, b * P:(b + 1) * P], TbT[:, h * B + 4 * q + b, :], Y[:, h, 4 * q + b, :],
                                         start=True, stop=True)
                    last.then_inc(s["W_ps"], 1)
                for n, (h, q) in enumerate(quads):
                    bank = banks[n % 4]
                    pe.wait_ge(s["W_ready"], at(i, 8, min(n + 5, 8)))
                    if n >= 4:
                        pe.wait_ge(s["C_ready"], at(i, 8, n - 3))
                    for b in range(4):
                        last = pe.matmul(bank[:, b * P:(b + 1) * P], NP[:, h, 4 * q + b, 1, :], Y[:, h, 4 * q + b, :],
                                         start=True, stop=True)
                    last.then_inc(s["C_ps"], 1)
                pe.wait_ge(s["z_ready"], at(i, B, B))
                pe.wait_ge(s["wout_ready"], i + 1)
                for b in range(B + 1):
                    if b < B:
                        bank = banks[6 + b % 2]
                        if b >= 2:
                            pe.wait_ge(s["yT_ready"], at(i, B, b - 1))
                        pe.wait_ge(s["y_scaled"], at(i, ITEMS, HB * (b + 1)))
                        for h in range(HB):
                            last = pe.transpose(bank[:, h * P:(h + 1) * P], Y[:, h, b, :], ident[:, :])
                        last.then_inc(s["yT_ps"], 1)
                    if b >= 1:
                        m = b - 1
                        bank = banks[4 + m % 2]
                        pe.wait_ge(s["yT_ready"], at(i, B, m + 1))
                        if m >= 2:
                            pe.wait_ge(s["acc_step"], at(i, B, m - 1))
                        for h in range(HB):
                            last = pe.matmul(bank[:, 0:D], yT[:, m % 2, h, :], wout[:, h, :], start=h == 0, stop=h == HB - 1)
                        last.then_inc(s["out_ps"], 1)
                pe.wait_ge(s["acc_step"], at(i, B, B))

        @block.scalar
        def _(act):
            for n in range(4):
                act.wait_ge(s["xT_ps"], 2 * n + 2)
                act.activation(xT[:, :, 2 * n:2 * n + 2, :], banks[n][:, :].rearrange("p (b c n) -> p c b n", b=2, c=DC), ACT.Copy)\
                    .then_inc(s["xT_copied"], 1)
            ba = banks[4][:, :].rearrange("p (b k h) -> p b k h", b=B, k=2)
            act.wait_ge(s["ba_ps"], 1)
            act.activation(sm[:, 0], ba[:, :, 0, :], ACT.Exp, scale=-1.0).then_inc(s["gate_act"], 1)
            act.wait_ge(s["gate_step"], 2)
            act.activation(sm[:, 2], sm[:, 2], ACT.Exp, scale=-1.0).then_inc(s["gate_act"], 1)
            act.wait_ge(s["gate_step"], 3)
            act.activation(sm[:, 2], sm[:, 3], ACT.Ln).then_inc(s["gate_act"], 1)
            act.wait_ge(s["weights"], 48)
            act.activation(bias[:, 1, :], bias[:, 1, :], ACT.Exp).then_inc(s["gate_act"], 1)
            with act.Fori(0, ROUNDS) as i:
                def copy_in(m):
                    act.wait_ge(s["proj_ready"], at(i, CHUNKS, m + 1))
                    if m >= 2:
                        act.wait_ge(s["cv_ready"], at(i, CHUNKS, m - 1))
                    if m >= 2:
                        act.wait_ge(s["tap0_ready"], at(i, CHUNKS, m - 1))
                    for q in range(2):
                        act.activation(pad[:, m % 2, 4 * q:4 * q + 4, TAPS - 1:], four(banks[2 * (m % 2) + q][:, :]), ACT.Copy)\
                            .then_inc(s["pad_ready"], 1)

                def silu(m):
                    act.wait_ge(s["cv_ready"], at(i, CHUNKS, m + 1))
                    dst = qkT[:, m // 2, m % 2] if m < QK else cv[:, m % 2]
                    act.activation(dst, cv[:, m % 2], ACT.Silu).then_inc(s["silu_ready"], 1)

                for m in range(QK + 2):
                    if m < QK + 1:
                        copy_in(m)
                    if m >= 1:
                        silu(m - 1)
                act.wait_ge(s["norms_ps"], at(i, QK, QK))
                act.activation(nrm[:, 0].rearrange("p k q b -> p (k q b)"), banks[7][:, 0:QK * B], ACT.Sqrt).then_inc(s["root_ready"], 1)
                order = [(2 * k + e, q) for k in range(KB) for q in range(2) for e in range(2)]
                for n, (h, q) in enumerate(order):
                    act.wait_ge(s["gcrow_ps"], at(i, 8, n + 1))
                    for b in range(4):
                        act.activation(NP[:, h, 4 * q + b, 1, :], banks[4 + n % 2][:, b * P:(b + 1) * P], ACT.Exp,
                                       bias=gcnR[:, h, 4 * q + b:4 * q + b + 1]).then_inc(s["E_ready"], 1)
                for m in range(QK + 1, CHUNKS):
                    copy_in(m)
                    silu(m)
                for b in range(B):
                    act.wait_ge(s["z_ps"], at(i, B, b + 1))
                    act.activation(zs[:, b, :], banks[4 + b % 2][:, :], ACT.Silu).then_inc(s["z_ready"], 1)
                for n, (h, q) in enumerate(quads):
                    act.wait_ge(s["MT_ps"], at(i, 8, n + 1))
                    act.activation(NP[:, h, 4 * q:4 * q + 4, 0, :], four(banks[n % 4][:, :]), ACT.Copy).then_inc(s["MT_ready"], 1)
                for n, (h, q) in enumerate(quads):
                    act.wait_ge(s["W_ps"], at(i, 8, n + 1))
                    act.activation(rr(Y, h, q), four(banks[n % 4][:, :]), ACT.Copy).then_inc(s["W_ready"], 1)
                for n, (h, q) in enumerate(quads):
                    act.wait_ge(s["C_ps"], at(i, 8, n + 1))
                    act.activation(rr(Y, h, q), four(banks[n % 4][:, :]), ACT.Copy).then_inc(s["C_ready"], 1)
                act.wait_ge(s["var_ready"], at(i, 2, 2))
                act.activation(f[:, 1], f[:, 0], ACT.Ln).then_inc(s["rstd_log"], 1)
                act.wait_ge(s["rstd_log"], i + 1)
                act.activation(f[:, 1], f[:, 1], ACT.Exp, scale=-0.5).then_inc(s["rstd_ready"], 1)
                for b in range(B):
                    act.wait_ge(s["yT_ps"], at(i, B, b + 1))
                    if b >= 2:
                        act.wait_ge(s["out_ps"], at(i, B, b - 1))
                    act.activation(yT[:, b % 2], four(banks[6 + b % 2][:, :]), ACT.Copy).then_inc(s["yT_ready"], 1)
            act.wait_ge(s["ln_step"], 3 * B + 1)
            act.activation(f[:, 1, 0, :], f[:, 0, 0, :], ACT.Ln).then_inc(s["ln_log"], 1)
            act.wait_ge(s["ln_log"], 1)
            act.activation(f[:, 1, 0, :], f[:, 1, 0, :], ACT.Exp, scale=-0.5).then_inc(s["ln_rstd"], 1)

        @block.vector
        def _(dve):
            link = Linked(dve, s["gate_step"])
            ba = banks[4][:, :].rearrange("p (b k h) -> p b k h", b=B, k=2)
            dve.wait_ge(s["weights"], 48)
            dve.wait_ge(s["gate_act"], 1)
            link(dve.tensor_tensor(sm[:, 1], ba[:, :, 1, :], spread(bias[:, 0, :], B), ALU.add))
            link(dve.scalar_tensor_tensor(sm[:, 2], sm[:, 1], -1.0, sm[:, 1], ALU.mult, ALU.max))
            dve.wait_ge(s["gate_act"], 2)
            link(dve.tensor_scalar(sm[:, 3], sm[:, 2], 1.0, None, ALU.add))
            dve.wait_ge(s["gate_act"], 4)
            link(dve.scalar_tensor_tensor(sm[:, 1], sm[:, 1], 0.0, sm[:, 2], ALU.max, ALU.add))
            link(dve.tensor_scalar(sm[:, 0], sm[:, 0], 1.0, None, ALU.add))
            link(dve.scalar_tensor_tensor(g[:, :, :], sm[:, 1], -1.0, spread(bias[:, 1, :], B), ALU.mult, ALU.mult))
            link(dve.reciprocal(beta[:, :, :], sm[:, 0]))
            dve.wait_ge(s["gc_ps"], 1)
            link(dve.tensor_scalar(flat(gcn[:, :, :]), banks[5][:, 0:B * VAL_HEADS], -1.0, None, ALU.mult))
            dve.wait_ge(s["consts"], 1)
            with dve.Fori(0, ROUNDS) as i:
                for dst, src in ((gR, g), (gcnR, gcn), (betaR, beta)):
                    dve.tensor_copy(dst[:, :, :], src[:, :, bass.ds(i * HB, HB)].rearrange("p b h -> p h b"))\
                        .then_inc(s["gates_used"], 1)

                def conv(m):
                    dve.wait_ge(s["tap0_ready"], at(i, CHUNKS, m + 1))
                    for t in range(1, TAPS):
                        ins = dve.scalar_tensor_tensor(cv[:, m % 2], pad[:, m % 2, :, t:t + S], wconv[:, m, t:t + 1], cv[:, m % 2],
                                                       ALU.mult, ALU.add)
                        if t < TAPS - 1:
                            ins.then_inc(s["conv_step"], 1)
                            dve.wait_ge(s["conv_step"], at(i, 2 * CHUNKS, 2 * m + t))
                    ins.then_inc(s["cv_ready"], 1)

                for m in range(QK + 1):
                    conv(m)
                link = Linked(dve, s["norm_step"], 3 + KB, i)
                dve.wait_ge(s["root_ready"], i + 1)
                link(dve.tensor_scalar(nrm[:, 0], nrm[:, 0], TINY, None, ALU.max))
                link(dve.reciprocal(nrm[:, 1], nrm[:, 0]))
                link(dve.tensor_tensor(nrm[:, 2], nrm[:, 1], nrm[:, 1], ALU.mult))
                dve.wait_ge(s["gates_used"], at(i, 3, 3))
                for k in range(KB):
                    link(dve.tensor_tensor(cj[:, 2 * k:2 * k + 2, :], betaR[:, 2 * k:2 * k + 2, :], spread(nrm[:, 2, k, 0, :], 2), ALU.mult))
                link.close()
                for grp in range(4):
                    k, q = grp // 2, grp % 2
                    dve.wait_ge(s["E_ready"], at(i, ITEMS, 8 * grp + 8))
                    for u in range(2):
                        dve.wait_ge(s["GP_ps"], at(i, 8, 2 * grp + u + 1))
                        for b in range(2):
                            gp = banks[6 + u][:, b * 2 * P:(b + 1) * 2 * P].rearrange("p (a n) -> p a n", a=2)
                            for e in range(2):
                                h, bb = 2 * k + e, 4 * q + 2 * u + b
                                dve.scalar_tensor_tensor(NP[:, h, bb, :, :], spread(NP[:, h, bb, 1, :], 2), cj[:, h, bb:bb + 1], gp,
                                                         ALU.mult, ALU.mult).then_inc(s["NP_ready"], 1)
                conv(QK + 1)
                elim = Linked(dve, s["elim_step"], ELIM, i)
                elim(dve.tensor_copy(T[:, :, :], T0[:, :, :]))
                dve.wait_ge(s["gathered"], at(i, 16, 16))
                for j in range(BL - 1):
                    n, w = BL - 1 - j, j + 1
                    part = tmp[:, 0:n * w].rearrange("p (n w) -> p n w", n=n)
                    elim(dve.tensor_tensor(part, along(A[:, j, j + 1:BL], w), spread(T[:, j, 0:w], n), ALU.mult))
                    elim(dve.tensor_tensor(T[:, j + 1:BL, 0:w], T[:, j + 1:BL, 0:w], part, ALU.subtract))
                elim(dve.tensor_copy(A[:, :, :], T[:, :, :].rearrange("p i k -> p k i")))
                elim.close()

                def values(n):
                    for q in range(2):
                        dve.wait_ge(s["vt_ps"], at(i, 2 * HB, 2 * n + q + 1))
                        dve.tensor_tensor(rr(V, n, q), four(banks[4 + q][:, :]), along(nrm[:, 0, n // 2, 0, 4 * q:4 * q + 4], P), ALU.mult)\
                            .then_inc(s["V_ready"], 1)

                values(0)
                values(1)
                for n in range(2, HB):
                    conv(QK + n)
                    values(n)
                for rep in range(3):
                    for n, (h, q) in enumerate(quads):
                        dve.wait_ge(s["apply_ps"], at(i, 24, 8 * rep + n + 1))
                        dve.tensor_tensor(rr(Y, h, q), rr(V, h, q), four(banks[n % 4][:, :]), ALU.subtract).then_inc(s["y_ready"], 1)
                for n, (h, q) in enumerate(quads):
                    dve.wait_ge(s["csq_ready"], at(i, 8, n + 1))
                    dve.tensor_reduce(s2[:, h, 4 * q:4 * q + 4], rr(V, h, q), AX.X, ALU.add).then_inc(s["s2_ready"], 1)
                dve.wait_ge(s["s2_ready"], at(i, 8, 8))
                for k in range(KB):
                    dve.tensor_tensor(f[:, 0, 2 * k:2 * k + 2, :], s2[:, 2 * k:2 * k + 2, :], spread(nrm[:, 2, k, 1, :], 2), ALU.mult)\
                        .then_inc(s["f_step"], 1)
                dve.wait_ge(s["f_step"], at(i, 2 * KB, KB))
                dve.tensor_scalar(f[:, 0], f[:, 0], 1.0 / (DK * DK), RMS_EPS, ALU.mult, ALU.add).then_inc(s["var_ready"], 2)
                dve.wait_ge(s["rstd_ready"], i + 1)
                for k in range(KB):
                    dve.scalar_tensor_tensor(f[:, 2, 2 * k:2 * k + 2, :], f[:, 1, 2 * k:2 * k + 2, :], DK ** -0.5, spread(nrm[:, 1, k, 1, :], 2),
                                             ALU.mult, ALU.mult).then_inc(s["f_step"], 1)
                dve.wait_ge(s["f_step"], at(i, 2 * KB, 2 * KB))
                dve.wait_ge(s["z_ready"], at(i, B, B))

                def add_out(b):
                    dve.wait_ge(s["out_ps"], at(i, B, b + 1))
                    dve.tensor_tensor(acc[:, b, :], acc[:, b, :], banks[4 + b % 2][:, 0:D], ALU.add).then_inc(s["acc_step"], 1)

                for b in range(B):
                    for h in range(HB):
                        dve.scalar_tensor_tensor(Y[:, h, b, :], Y[:, h, b, :], f[:, 2, h, b:b + 1], zs[:, b, h * P:(h + 1) * P],
                                                 ALU.mult, ALU.mult).then_inc(s["y_scaled"], 1)
                    if b >= 2:
                        add_out(b - 2)
                add_out(B - 2)
                add_out(B - 1)
            dve.wait_ge(s["acc_step"], ROUNDS * B)
            link = Linked(dve, s["ln_step"])
            for b in range(B):
                dve.bn_stats(cj[:, 0, 0:6], acc[:, b, :]).then_inc(s["ln_step"], 1)
                dve.wait_ge(s["ln_step"], 3 * b + 1)
                dve.bn_aggr(gR[:, 0, 0:2], cj[:, 0, 0:6]).then_inc(s["ln_step"], 1)
                dve.wait_ge(s["ln_step"], 3 * b + 2)
                dve.tensor_copy(f[:, 2, 0:2, b], gR[:, 0, 0:2]).then_inc(s["ln_step"], 1)
                dve.wait_ge(s["ln_step"], 3 * b + 3)
            dve.tensor_scalar(f[:, 0, 0, :], f[:, 2, 1, :], LN_EPS, None, ALU.add).then_inc(s["ln_step"], 1)
            dve.wait_ge(s["ln_rstd"], 1)
            for b in range(B):
                dve.tensor_scalar(acc[:, b, :], acc[:, b, :], f[:, 2, 0, b:b + 1], f[:, 1, 0, b:b + 1], ALU.subtract, ALU.mult)\
                    .then_inc(s["xo_ready"], 1)


def layout_layer1_delta_rule(inp):
    W = inp["L1_attn_W_qkv"]
    q, k, v = (a.reshape(-1, P, D) for a in np.split(W, [KEY_HEADS * DK, 2 * KEY_HEADS * DK]))
    cw = inp["L1_attn_conv_w"]
    cq, ck, cvv = (a.reshape(-1, P, TAPS) for a in np.split(cw, [KEY_HEADS * DK, 2 * KEY_HEADS * DK]))

    def rounds(k, q, v):
        kq = np.stack([k, q], axis=1).reshape(ROUNDS, QK, *k.shape[1:])
        return np.concatenate([kq, v.reshape(ROUNDS, HB, *v.shape[1:])], axis=1)
    wqkv = rounds(k, q, v).reshape(ROUNDS, CHUNKS, P, DC, P).transpose(0, 4, 1, 3, 2)
    wconv = rounds(ck, cq, cvv).transpose(0, 2, 1, 3)
    wz = inp["L1_attn_W_z"].reshape(ROUNDS, HB * P, DC, P).transpose(0, 3, 2, 1)
    wout = inp["L1_attn_W_out"].T.reshape(ROUNDS, HB, P, D).transpose(0, 2, 1, 3)
    wba = np.concatenate([inp["L1_attn_W_b"], inp["L1_attn_W_a"]]).T.reshape(DC, P, 2 * VAL_HEADS).transpose(1, 0, 2)
    bias = np.broadcast_to(np.stack([inp["L1_attn_dt_bias"], inp["L1_attn_A_log"]])[None], (P, 2, VAL_HEADS))
    return dict(wqkv=wqkv.reshape(ROUNDS, P, CHUNKS, DC * P), wconv=wconv, wz=wz, wout=wout, wba=wba, bias=bias, normw=inp["L1_attn_norm_w"].reshape(P, 1))


LEVELS, QUANT_EPS = 127.0, 1e-8
MAGIC = 1.5 * 2.0 ** 23


class Quantizer:

    STEPS = 5

    def __init__(self, ph, name, per):
        self.col = ph.sb(name + "_col", [P, 2])
        self.t = ph.sb(name + "_t", [P, 2, D])
        self.step = ph.sem(name + "_step")
        self.done = ph.sem(name + "_done")
        self.per = per

    def on_vector(self, dve, i, n, src, out, step_out):
        link = Linked(dve, self.step, self.STEPS * self.per, i)
        link.n = self.STEPS * n
        link(dve.tensor_reduce(self.col[:, 0:1], src, AX.X, ALU.max, apply_absolute_value=True))
        link(dve.tensor_scalar(step_out, self.col[:, 0:1], 1.0 / LEVELS, QUANT_EPS, ALU.mult, ALU.max))
        link(dve.reciprocal(self.col[:, 1:2], step_out))
        link(dve.tensor_scalar(self.t[:, 0, :], src, self.col[:, 1:2], LEVELS, ALU.mult, ALU.min))
        link(dve.tensor_scalar(self.t[:, 1, :], self.t[:, 0, :], -LEVELS, MAGIC, ALU.max, ALU.add))
        dve.tensor_scalar(out, self.t[:, 1, :], MAGIC, None, ALU.subtract).then_inc(self.done, 1)
        dve.wait_ge(self.done, at(i, self.per, n + 1))


def layer1_attention(nc, sems, d, x_src, x_dst):
    ctx = ExitStack()
    with ctx:
        ph = Phase(nc, "d", ctx, sems)
        sb, sem = ph.sb, ph.sem
        shapes = dict(wq8=[P, DC, D], wo8=[P, DC, D], wk=[P, DC, D], wv=[P, DC, D], bk=[P, DC], bv=[1, D],
                      bqo=[P, 2, D], wtop=[P, DC, H], wqkv=[P, DC, 3 * D])
        w = {k: sb(k, s) for k, s in shapes.items()}
        ident = sb("ident", [P, P])
        identb = sb("identb", [P, P], BF16)
        causal = sb("causal", [P, P])
        causalb = sb("causalb", [P, P], BF16)
        own_block = sb("own_block", [P, 8])
        head_id = sb("head_id", [P, 2, H])
        ones = sb("ones", [1, P])
        w8 = sb("w8", [P, 2, DC, D], BF16)
        w8T = sb("w8T", [P, 2, DC, D], BF16)
        wstep = sb("wstep", [P, 2, DC])
        wstep_row = sb("wstep_row", [P, 2, D])
        xt = sb("xt", [P, D])
        ct = sb("ct", [P, D])
        mask = sb("mask", [P, P])
        cT = sb("cT", [P, DC, P])
        x8 = sb("x8", [P, 2, D], BF16)
        x8T = sb("x8T", [P, 2, DC, P], BF16)
        xstep = sb("xstep", [P, 2])
        y8 = sb("y8", [P, 2, D])
        yb = sb("yb", [P, 2, D])
        qT = sb("qT", [P, DC, P])
        kT = sb("kT", [P, DC, P])
        kexp = sb("kexp", [P, DC, 8, P])
        vaug = sb("vaug", [P, H, HD + 1])
        pbuf = sb("pbuf", [P, 2, 4, P])
        ptbuf = sb("ptbuf", [P, 2, 4, P])
        stats = sb("stats", [P, 32])
        osb = sb("osb", [P, H, HD])
        x5 = sb("x5", [P, D])
        x5T = sb("x5T", [P, DC, P])
        col = sb("col", [P, 6])
        prob = sb("prob", [P, 5, H])
        qT2 = sb("qT2", [P, DC, P])
        kv = sb("kv", [P, 2, H, HD])
        best = sb("best", [P, 2, HD])
        krep = sb("krep", [P, 8, HD])
        krepT = sb("krepT", [P, P])
        vaug2 = sb("vaug2", [P, HD + 1])
        osb2 = sb("osb2", [P, H, HD])
        xo = sb("xo", [P, D])
        M0, M1, S0, S1, T0, T1, O0, O1 = (ph.bank(n) for n in ("M0", "M1", "S0", "S1", "T0", "T1", "O0", "O1"))
        banks = ((S0, S1), (T0, T1), (O0, O1))
        cross_att = Attention(ph, "cross", HD, banks, pbuf, ptbuf, stats, osb, ident[:, :])
        self_att = Attention(ph, "self", HD, banks, pbuf, ptbuf, stats, osb2, ident[:, :])
        ln1, ln2 = LayerNorm(ph, "ln1"), LayerNorm(ph, "ln2")
        wquant = Quantizer(ph, "wquant", 2 * DC)
        xquant = Quantizer(ph, "xquant", 2)
        names = """weights pool_step consts w8T_ps w8T_ready wstep_ps wstep_ready x_loaded ctx_loaded mask_loaded stored xo_free
            cT_ps cT_ready kv_ps kT_ready v_ready kexp_ready x8T_ps x8T_ready y8_ps y8_step yb_ready qT_ps qT_ready
            x5T_ps x5T_ready logits_ps top_step exp_ready qkv_ps qT2_ready best_step krep_ready vaug2_ready
            krepT_ps krepT_ready kexp2_ready""".split()
        s = {n: sem(n) for n in names}
        TOP = 10
        half = lambda ap: ap.rearrange("p (c n) -> p c n", c=DC)
        M0b = M0[:, :].bitcast(BF16)
        block = ctx.enter_context(nc.Block())

        @block.sync
        def _(sp):
            for k in shapes:
                sp.dma_start(w[k][:], d[k]).then_inc(s["weights"], 16)
            sp.dma_start(ct[:, :], batch(d["ctx"], 0)).then_inc(s["ctx_loaded"], 16)
            sp.dma_start(xt[:, :], batch(x_src, 0)).then_inc(s["x_loaded"], 16)
            sp.dma_start(mask[:, :], batch(d["mask"], 0)).then_inc(s["mask_loaded"], 16)
            sp.sem_inc(s["xo_free"], 1)
            with sp.Fori(0, B - 1) as i:
                sp.wait_ge(s["cT_ps"], i + 1)
                sp.dma_start(ct[:, :], batch(d["ctx"], i + 1)).then_inc(s["ctx_loaded"], 16)
                sp.wait_ge(cross_att.scores_ready, at(i, QUADS, QUADS))
                sp.dma_start(mask[:, :], batch(d["mask"], i + 1)).then_inc(s["mask_loaded"], 16)
                sp.wait_ge(ln1.step, at(i, ln1.DVE_STEPS, 1))
                sp.dma_start(xt[:, :], batch(x_src, i + 1)).then_inc(s["x_loaded"], 16)
                store_batch(sp, i, ln2.done, xo[:, :], x_dst, s["stored"], s["xo_free"])
            store_batch(sp, B - 1, ln2.done, xo[:, :], x_dst, s["stored"], s["xo_free"])

        @block.gpsimd
        def _(pool):
            link = Linked(pool, s["pool_step"])
            fill_identity(pool, link, ident[:, :])
            link(pool.tensor_copy(identb[:, :], ident[:, :]))
            link(pool.memset(causal[:, :], 0.0))
            link(pool.affine_select(out=causal[:, :], in_=causal[:, :], compare_op=ALU.is_ge, fill=MASKED,
                                    base=0, pattern=[[-1, P]], channel_multiplier=1))
            link(pool.tensor_copy(causalb[:, :], causal[:, :]))
            link(pool.memset(own_block[:, :], 1.0))
            link(pool.affine_select(out=own_block[:, :], in_=own_block[:, :], compare_op=ALU.is_ge, fill=0.0,
                                    base=0, pattern=[[-HD, 8]], channel_multiplier=1))
            link(pool.affine_select(out=own_block[:, :], in_=own_block[:, :], compare_op=ALU.is_ge, fill=0.0,
                                    base=HD - 1, pattern=[[HD, 8]], channel_multiplier=-1))
            link(pool.iota(head_id[:, :, :], pattern=[[H, 2], [1, H]], base=0, channel_multiplier=0,
                           allow_small_or_imprecise_dtypes=True))
            link(pool.memset(ones[:, :], 1.0))
            link(pool.memset(vaug2[:, :], 1.0))
            pool.memset(vaug[:, :, :], 1.0).then_inc(s["consts"], 1)
            with pool.Fori(0, B) as i:
                pool.wait_ge(s["kT_ready"], at(i, DC, DC))
                for c in range(DC):
                    pool.tensor_tensor(kexp[:, c], spread(kT[:, c, :], 8), along(own_block[:, :], P), ALU.mult)\
                        .then_inc(s["kexp_ready"], 1)
                pool.wait_ge(s["krepT_ready"], i + 1)
                pool.tensor_tensor(kexp[:, 0], spread(krepT[:, :], 8), along(own_block[:, :], P), ALU.mult)\
                    .then_inc(s["kexp2_ready"], 1)

        @block.tensor
        def _(pe):
            pe.wait_ge(s["weights"], 16 * len(shapes))
            pe.wait_ge(s["consts"], 1)
            for k in range(2):
                for c in range(DC):
                    pe.wait_ge(wquant.done, 2 * k + c + 1)
                    for m in range(DC):
                        col0 = k * 2 * D + m * D + c * P
                        last = pe.transpose(M0b[:, col0:col0 + P] if k == 0 else M1[:, :].bitcast(BF16)[:, col0 - 2 * D:col0 - 2 * D + P],
                                            w8[:, k, c, m * P:(m + 1) * P], identb[:, :])
                last.then_inc(s["w8T_ps"], 1)
            for k in range(2):
                for c in range(DC):
                    last = pe.matmul(S0[:, (2 * k + c) * P:(2 * k + c + 1) * P], wstep[:, k, c:c + 1].broadcast_to([P, P]), ident[:, :],
                                     start=True, stop=True)
            last.then_inc(s["wstep_ps"], 1)
            pe.wait_ge(s["w8T_ready"], 2)
            pe.wait_ge(s["wstep_ready"], 1)
            with pe.Fori(0, B) as i:
                pe.wait_ge(s["ctx_loaded"], at(i, 16, 16))
                for c in range(DC):
                    last = pe.transpose(M1[:, c * P:(c + 1) * P], ct[:, c * P:(c + 1) * P], ident[:, :])
                last.then_inc(s["cT_ps"], 1)
                pe.wait_ge(s["cT_ready"], i + 1)
                for m in range(DC):
                    for c in range(DC):
                        pe.matmul(O0[:, m * P:(m + 1) * P], w["wk"][:, c, m * P:(m + 1) * P], cT[:, c, :], start=c == 0, stop=c == DC - 1)
                pe.matmul(O1[:, 0:D], ones[:, :], w["bv"][:, :], start=True, stop=False)
                for c in range(DC):
                    last = pe.matmul(O1[:, 0:D], cT[:, c, :], w["wv"][:, c, :], start=False, stop=c == DC - 1)
                last.then_inc(s["kv_ps"], 1)

                def project8(n, out):
                    pe.wait_ge(xquant.done, at(i, 2, n + 1))
                    for c in range(DC):
                        last = pe.transpose(M0b[:, c * P:(c + 1) * P], x8[:, n, c * P:(c + 1) * P], identb[:, :])
                    last.then_inc(s["x8T_ps"], 1)
                    pe.wait_ge(s["x8T_ready"], at(i, 2, n + 1))
                    for c in range(DC):
                        last = pe.matmul(out, x8T[:, n, c, :], w8T[:, n, c, :], start=c == 0, stop=c == DC - 1)
                    last.then_inc(s["y8_ps"], 1)

                project8(0, M1[:, D:2 * D])
                pe.wait_ge(s["yb_ready"], at(i, 2, 1))
                for c in range(DC):
                    last = pe.transpose(M0[:, D + c * P:D + (c + 1) * P], yb[:, 0, c * P:(c + 1) * P], ident[:, :])
                last.then_inc(s["qT_ps"], 1)
                pe.wait_ge(s["qT_ready"], i + 1)
                pe.wait_ge(s["v_ready"], i + 1)
                pe.wait_ge(s["mask_loaded"], at(i, 16, 16))

                def cross_scores(n, bank):
                    if n % 2 == 0:
                        pe.wait_ge(s["kexp_ready"], at(i, DC, n // 2 + 1))
                    pe.matmul(four(bank[:, :]), ident[:, :], spread(mask[:, :], 4), start=True, stop=False)
                    return pe.matmul(four(bank[:, :]), qT[:, n // 2, :], kexp[:, n // 2, 4 * (n % 2):4 * (n % 2) + 4, :],
                                     start=False, stop=True)

                cross_att.on_tensor(pe, i, cross_scores, lambda n, h: vaug[:, 4 * n + h, :])
                project8(1, M1[:, D:2 * D])
                pe.wait_ge(ln1.done, i + 1)
                for c in range(DC):
                    last = pe.transpose(M0[:, c * P:(c + 1) * P], x5[:, c * P:(c + 1) * P], ident[:, :])
                last.then_inc(s["x5T_ps"], 1)
                pe.wait_ge(s["x5T_ready"], i + 1)
                for c in range(DC):
                    last = pe.matmul(M0[:, D:D + H], x5T[:, c, :], w["wtop"][:, c, :], start=c == 0, stop=c == DC - 1)
                last.then_inc(s["logits_ps"], 1)
                for c in range(DC):
                    last = pe.matmul(O0[:, :], x5T[:, c, :], w["wqkv"][:, c, D:3 * D], start=c == 0, stop=c == DC - 1)
                for m in range(DC):
                    for c in range(DC):
                        last = pe.matmul(O1[:, m * P:(m + 1) * P], w["wqkv"][:, c, m * P:(m + 1) * P], x5T[:, c, :],
                                         start=c == 0, stop=c == DC - 1)
                last.then_inc(s["qkv_ps"], 1)
                pe.wait_ge(s["krep_ready"], i + 1)
                pe.transpose(M1[:, 0:P], krep[:, :, :].rearrange("p r d -> p (r d)"), ident[:, :]).then_inc(s["krepT_ps"], 1)
                pe.wait_ge(s["vaug2_ready"], i + 1)
                pe.wait_ge(s["qT2_ready"], i + 1)

                def self_scores(n, bank):
                    if n == 0:
                        pe.wait_ge(s["kexp2_ready"], i + 1)
                    pe.matmul(four(bank[:, :]), identb[:, :], spread(causalb[:, :], 4), start=True, stop=False)
                    return pe.matmul(four(bank[:, :]), qT2[:, n // 2, :], kexp[:, 0, 4 * (n % 2):4 * (n % 2) + 4, :],
                                     start=False, stop=True)

                self_att.on_tensor(pe, i, self_scores, lambda n, h: vaug2[:, :])

        @block.scalar
        def _(act):
            for k, bank in enumerate((M0, M1)):
                act.wait_ge(s["w8T_ps"], k + 1)
                act.activation(w8T[:, k], half(bank[:, :].bitcast(BF16)[:, 0:2 * D]), ACT.Copy).then_inc(s["w8T_ready"], 1)
            act.wait_ge(s["wstep_ps"], 1)
            act.activation(wstep_row[:, :, :], S0[:, :].rearrange("p (k n) -> p k n", k=2), ACT.Copy).then_inc(s["wstep_ready"], 1)
            with act.Fori(0, B) as i:
                act.wait_ge(s["cT_ps"], i + 1)
                act.activation(cT[:, :, :], half(M1[:, 0:D]), ACT.Copy).then_inc(s["cT_ready"], 1)
                act.wait_ge(s["kv_ps"], i + 1)
                act.activation(vaug[:, :, 0:HD], O1[:, 0:D].rearrange("p (h d) -> p h d", h=H), ACT.Copy).then_inc(s["v_ready"], 1)

                def copy8(n):
                    act.wait_ge(s["x8T_ps"], at(i, 2, n + 1))
                    act.activation(x8T[:, n], half(M0b[:, 0:D]), ACT.Copy).then_inc(s["x8T_ready"], 1)

                copy8(0)
                act.wait_ge(s["qT_ps"], i + 1)
                act.activation(qT[:, :, :], half(M0[:, D:2 * D]), ACT.Copy, scale=0.25).then_inc(s["qT_ready"], 1)
                cross_att.on_scalar(act, i)
                copy8(1)
                ln1.on_scalar(act, i)
                act.wait_ge(s["x5T_ps"], i + 1)
                act.activation(x5T[:, :, :], half(M0[:, 0:D]), ACT.Copy).then_inc(s["x5T_ready"], 1)
                act.wait_ge(s["top_step"], at(i, TOP, 2))
                act.activation(prob[:, 0, :], prob[:, 0, :], ACT.Exp).then_inc(s["exp_ready"], 1)
                act.wait_ge(s["qkv_ps"], i + 1)
                act.activation(qT2[:, :, :], half(O1[:, 0:D]), ACT.Copy, scale=0.25).then_inc(s["qT2_ready"], 1)
                act.wait_ge(s["krepT_ps"], i + 1)
                act.activation(krepT[:, :], M1[:, 0:P], ACT.Copy).then_inc(s["krepT_ready"], 1)
                self_att.on_scalar(act, i)
                ln2.on_scalar(act, i)

        @block.vector
        def _(dve):
            dve.wait_ge(s["weights"], 16 * len(shapes))
            dve.wait_ge(s["consts"], 1)
            for k, name in enumerate(("wq8", "wo8")):
                for c in range(DC):
                    wquant.on_vector(dve, 0, 2 * k + c, w[name][:, c, :], w8[:, k, c, :], wstep[:, k, c:c + 1])
            dve.wait_ge(s["wstep_ready"], 1)
            with dve.Fori(0, B) as i:
                def scale8(n):
                    dve.tensor_scalar(y8[:, 0, :], wstep_row[:, n, :], xstep[:, n:n + 1], None, ALU.mult).then_inc(s["y8_step"], 1)
                    dve.wait_ge(s["y8_step"], at(i, 4, 2 * n + 1))
                    dve.wait_ge(s["y8_ps"], at(i, 2, n + 1))
                    dve.tensor_tensor(y8[:, 1, :], y8[:, 0, :], M1[:, D:2 * D], ALU.mult).then_inc(s["y8_step"], 1)
                    dve.wait_ge(s["y8_step"], at(i, 4, 2 * n + 2))
                    dve.tensor_tensor(yb[:, n, :], y8[:, 1, :], w["bqo"][:, n, :], ALU.add).then_inc(s["yb_ready"], 1)

                dve.wait_ge(s["x_loaded"], at(i, 16, 16))
                xquant.on_vector(dve, i, 0, xt[:, :], x8[:, 0, :], xstep[:, 0:1])
                dve.wait_ge(s["kv_ps"], i + 1)
                for c in range(DC):
                    dve.tensor_scalar(kT[:, c, :], O0[:, c * P:(c + 1) * P], w["bk"][:, c:c + 1], None, ALU.add).then_inc(s["kT_ready"], 1)
                scale8(0)
                cross_att.on_vector(dve, i)
                dve.wait_ge(cross_att.o_done, at(i, QUADS, QUADS))
                xquant.on_vector(dve, i, 1, osb[:, :, :].rearrange("p h d -> p (h d)"), x8[:, 1, :], xstep[:, 1:2])
                scale8(1)
                dve.wait_ge(s["yb_ready"], at(i, 2, 2))
                ln1.on_vector(dve, i, x5[:, :], xt[:, :], yb[:, 1, :])
                link = Linked(dve, s["top_step"], TOP, i)
                dve.wait_ge(s["logits_ps"], i + 1)
                logits = M0[:, D:D + H]
                link(dve.tensor_reduce(col[:, 0:1], logits, AX.X, ALU.max))
                link(dve.tensor_scalar(prob[:, 0, :], logits, col[:, 0:1], None, ALU.subtract))
                dve.wait_ge(s["exp_ready"], i + 1)
                link(dve.tensor_reduce(col[:, 1:2], prob[:, 0, :], AX.X, ALU.add))
                link(dve.reciprocal(col[:, 2:3], col[:, 1:2]))
                link(dve.tensor_scalar(prob[:, 1, :], prob[:, 0, :], col[:, 2:3], None, ALU.mult))
                link(dve.tensor_reduce(col[:, 3:4], prob[:, 1, :], AX.X, ALU.max))
                link(dve.tensor_scalar(prob[:, 2, :], prob[:, 1, :], col[:, 3:4], -float(H), ALU.is_equal, ALU.mult))
                link(dve.tensor_tensor(prob[:, 3, :], prob[:, 2, :], head_id[:, 1, :], ALU.add))
                link(dve.tensor_reduce(col[:, 4:5], prob[:, 3, :], AX.X, ALU.min))
                link(dve.tensor_scalar(prob[:, 4, :], head_id[:, 0, :], col[:, 4:5], None, ALU.is_equal))
                link.close()
                dve.wait_ge(s["qkv_ps"], i + 1)
                kvp = O0[:, :].rearrange("p (a h d) -> p a h d", a=2, h=H)
                for a in range(2):
                    dve.tensor_tensor(kv[:, a], kvp[:, a], along(prob[:, 4, :], HD), ALU.mult).then_inc(s["best_step"], 1)
                for a in range(2):
                    dve.wait_ge(s["best_step"], at(i, 4, a + 1))
                    dve.tensor_reduce(best[:, a, :], kv[:, a].rearrange("p h d -> p d h"), AX.X, ALU.add).then_inc(s["best_step"], 1)
                dve.wait_ge(s["best_step"], at(i, 4, 4))
                dve.tensor_copy(krep[:, :, :], spread(best[:, 0, :], 8)).then_inc(s["krep_ready"], 1)
                dve.tensor_scalar(vaug2[:, 0:HD], best[:, 1, :], col[:, 3:4], None, ALU.mult).then_inc(s["vaug2_ready"], 1)
                self_att.on_vector(dve, i)
                dve.wait_ge(self_att.o_done, at(i, QUADS, QUADS))
                dve.wait_ge(s["xo_free"], i + 1)
                ln2.on_vector(dve, i, xo[:, :], x5[:, :], osb2[:, :, :].rearrange("p h d -> p (h d)"))


def layout_layer1_attention(inp):
    by_chunk = lambda a: a.reshape(DC, P, -1).transpose(1, 0, 2)
    bqo = np.broadcast_to(np.stack([inp["L1_xattn_bq"], inp["L1_xattn_bo"]])[None], (P, 2, D))
    return dict(ctx=inp["ctx_2048"], mask=inp["mask_BxSxS2_ff0"], wq8=by_chunk(inp["L1_xattn_wq"]), wo8=by_chunk(inp["L1_xattn_wo"]),
                wk=by_chunk(inp["L1_xattn_wk"].T), wv=by_chunk(inp["L1_xattn_wv"].T), bk=inp["L1_xattn_bk"].reshape(DC, P).T,
                bv=inp["L1_xattn_bv"].reshape(1, D), bqo=bqo, wtop=by_chunk(inp["L1_ffn_W_gate"].T),
                wqkv=by_chunk(inp["L1_ffn_W_qkv"].T))


PHASES = (("a", layout_layer0_attention, layer0_attention), ("b", layout_layer0_experts, layer0_experts),
          ("c", layout_layer1_delta_rule, layer1_delta_rule), ("d", layout_layer1_attention, layer1_attention))


def decoder(nc, x, weights, out):
    src = x
    for n, (tag, _, build) in enumerate(PHASES):
        last = n == len(PHASES) - 1
        dst = out if last else nc.dram_tensor(f"x_after_{tag}", (B, S, D), F32, kind="Internal").ap()
        sems = []
        build(nc, sems, weights[tag], src, dst)
        if not last:
            nc.all_engine_barrier()
            nc.clear_and_free_semaphores(sems)
            nc.all_engine_barrier()
        src = dst


def kernel(**inputs):
    import concourse.bacc as bacc
    from concourse.bass_utils import run_bass_kernel_spmd

    inputs = {k: np.asarray(v) for k, v in inputs.items()}
    nc = bacc.Bacc("TRN2", target_bir_lowering=False, num_devices=1)
    arrays = {"x": np.ascontiguousarray(inputs["x"])}
    handles = {"x": nc.dram_tensor("x", arrays["x"].shape, F32, kind="ExternalInput").ap()}
    weights = {}
    for tag, layout, _ in PHASES:
        weights[tag] = {}
        for name, a in layout(inputs).items():
            full = f"{tag}_in_{name}"
            arrays[full] = np.ascontiguousarray(a)
            weights[tag][name] = nc.dram_tensor(full, a.shape, mybir.dt.from_np(a.dtype), kind="ExternalInput").ap()
    out = nc.dram_tensor("out", (B, S, D), F32, kind="ExternalOutput").ap()
    decoder(nc, handles["x"], weights, out)
    return run_bass_kernel_spmd(nc, [arrays], core_ids=[0]).results[0]["out"]
```

```python
from contextlib import ExitStack

import numpy as np

import concourse.bass as bass
from concourse import mybir

F32 = mybir.dt.float32
BF16 = mybir.dt.bfloat16
I32 = mybir.dt.int32
ALU = mybir.AluOpType
ACT = mybir.ActivationFunctionType
AX = mybir.AxisListType

B, S, D = 8, 128, 256
P = 128
DC = D // P
H = 16
QUADS = H // 4
HD = D // H
MASKED = -1e30
LN_EPS = 1e-5


def at(i, per, n):
    return i * per + n


class Linked:

    def __init__(self, eng, sem, per=0, i=0):
        self.eng, self.sem, self.per, self.i, self.n = eng, sem, per, i, 0

    def __call__(self, *together):
        for ins in together:
            ins.then_inc(self.sem, 1)
            self.n += 1
        self.eng.wait_ge(self.sem, at(self.i, self.per, self.n))

    def close(self):
        assert self.n == self.per, self.n


LANES = 2


class Phase:

    def __init__(self, nc, tag, ctx, sems):
        self.nc, self.tag, self.ctx, self.sems = nc, tag, ctx, sems

    def sb(self, name, shape, dt=F32):
        return self.ctx.enter_context(self.nc.sbuf_tensor(f"{self.tag}_{name}", shape, dt))

    def bank(self, name, dt=F32):
        return self.ctx.enter_context(self.nc.psum_tensor(f"{self.tag}_{name}", [P, 2048 // mybir.dt.size(dt)], dt))

    def sem(self, name):
        self.sems.append(self.nc.alloc_semaphore(name=f"{self.tag}_{name}"))
        return self.sems[-1]


def four(ap):
    return ap.rearrange("p (h n) -> p h n", h=4)


def spread(ap, n):
    return ap.unsqueeze(1).broadcast_to([ap.shape[0], n, ap.shape[1]])


def along(ap, n):
    return ap.unsqueeze(2).broadcast_to([ap.shape[0], ap.shape[1], n])


def batch(t, b):
    return t[bass.ds(b, 1)].rearrange("a p c -> p (a c)")


def store_batch(sp, i, b, ready, out, dst, stored, free):
    sp.wait_ge(ready, at(i, 1, 1))
    sp.dma_start(batch(dst, b), out).then_inc(stored, 16)
    sp.wait_ge(stored, at(i, 16, 16))
    sp.sem_inc(free, 1)


def in_turns(programs):
    done = object()
    running = list(programs)
    while running:
        running = [p for p in running if next(p, done) is not done]


def fill_identity(pool, link, tile):
    link(pool.memset(tile, 0.0))
    link(pool.affine_select(out=tile, in_=tile, compare_op=ALU.not_equal, fill=1.0, base=0,
                            pattern=[[-1, P]], channel_multiplier=1))


class Attention:

    def __init__(self, ph, name, width, banks, pbuf, ptbuf, stats, out, ident):
        self.width, self.out, self.ident = width, out, ident
        self.S, self.PT, self.O = banks
        self.p, self.pt, self.stats = pbuf, ptbuf, stats
        self.scores_ready = ph.sem(name + "_scores_ready")
        self.max_ready = ph.sem(name + "_max_ready")
        self.shifted = ph.sem(name + "_shifted")
        self.exp_ready = ph.sem(name + "_exp_ready")
        self.pt_ready = ph.sem(name + "_pt_ready")
        self.pt_copied = ph.sem(name + "_pt_copied")
        self.o_ready = ph.sem(name + "_o_ready")
        self.recip_ready = ph.sem(name + "_recip_ready")
        self.o_done = ph.sem(name + "_o_done")

    def on_tensor(self, pe, i, scores, values):
        w = self.width + 1
        for s in range(QUADS + 2):
            if s < QUADS:
                if s >= 1:
                    pe.wait_ge(self.shifted, at(i, QUADS, s))
                scores(s, self.S).then_inc(self.scores_ready, 1)
            if 1 <= s <= QUADS:
                n = s - 1
                pe.wait_ge(self.exp_ready, at(i, QUADS, n + 1))
                if n >= 1:
                    pe.wait_ge(self.pt_copied, at(i, QUADS, n))
                for h in range(4):
                    last = pe.transpose(self.PT[:, h * P:(h + 1) * P], self.p[:, n % 2, h, :], self.ident)
                last.then_inc(self.pt_ready, 1)
            if s >= 2:
                n = s - 2
                pe.wait_ge(self.pt_copied, at(i, QUADS, n + 1))
                if n >= 1:
                    pe.wait_ge(self.o_done, at(i, QUADS, n))
                for h in range(4):
                    last = pe.matmul(self.O[:, h * w:(h + 1) * w], self.pt[:, n % 2, h, :],
                                     values(n, h), start=True, stop=True)
                last.then_inc(self.o_ready, 1)
            yield

    def on_scalar(self, act, i):
        for s in range(QUADS + 1):
            if s >= 1:
                n = s - 1
                act.wait_ge(self.pt_ready, at(i, QUADS, n + 1))
                if n >= 2:
                    act.wait_ge(self.o_ready, at(i, QUADS, n - 1))
                act.activation(self.pt[:, n % 2], four(self.PT[:, :]), ACT.Copy).then_inc(self.pt_copied, 1)
            if s < QUADS:
                act.wait_ge(self.shifted, at(i, QUADS, s + 1))
                act.activation(self.p[:, s % 2], self.p[:, s % 2], ACT.Exp).then_inc(self.exp_ready, 1)
            yield

    def on_vector(self, dve, i):
        w = self.width + 1
        for s in range(QUADS + 2):
            if s < QUADS:
                dve.wait_ge(self.scores_ready, at(i, QUADS, s + 1))
                dve.tensor_reduce(self.stats[:, 4 * s:4 * s + 4], four(self.S[:, :]), AX.X, ALU.max)\
                   .then_inc(self.max_ready, 1)
                dve.wait_ge(self.max_ready, at(i, QUADS, s + 1))
                if s >= 2:
                    dve.wait_ge(self.pt_ready, at(i, QUADS, s - 1))
                dve.tensor_tensor(self.p[:, s % 2], four(self.S[:, :]), along(self.stats[:, 4 * s:4 * s + 4], P),
                                  ALU.subtract).then_inc(self.shifted, 1)
            if s >= 2:
                n = s - 2
                dve.wait_ge(self.o_ready, at(i, QUADS, n + 1))
                o = self.O[:, 0:4 * w].rearrange("p (h w) -> p h w", h=4)
                dve.reciprocal(self.stats[:, 16 + 4 * n:20 + 4 * n].unsqueeze(2), o[:, :, self.width:w]).then_inc(self.recip_ready, 1)
                dve.wait_ge(self.recip_ready, at(i, QUADS, n + 1))
                dve.tensor_tensor(self.out[:, 4 * n:4 * n + 4, :], o[:, :, 0:self.width],
                                  along(self.stats[:, 16 + 4 * n:20 + 4 * n], self.width), ALU.mult).then_inc(self.o_done, 1)
            yield


class LayerNorm:

    DVE_STEPS = 9

    def __init__(self, ph, name):
        self.r = ph.sb(name + "_sum", [P, D])
        self.st = ph.sb(name + "_stats", [P, 6])
        self.c = ph.sb(name + "_cols", [P, 8])
        self.rstd = ph.sb(name + "_rstd", [P, 2])
        self.step = ph.sem(name + "_step")
        self.log_ready = ph.sem(name + "_log_ready")
        self.rstd_ready = ph.sem(name + "_rstd_ready")
        self.done = ph.sem(name + "_done")

    def on_vector(self, dve, i, out, x, y):
        link = Linked(dve, self.step, self.DVE_STEPS, i)
        col = lambda n: self.c[:, n:n + 1]
        link(dve.tensor_tensor(self.r[:, :], x, y, ALU.add))
        link(dve.bn_stats(self.st[:, :], self.r[:, :]))
        link(dve.tensor_tensor(col(0), self.st[:, 1:2], self.st[:, 4:5], ALU.subtract),
             dve.tensor_tensor(col(1), self.st[:, 1:2], self.st[:, 4:5], ALU.add),
             dve.tensor_tensor(col(2), self.st[:, 2:3], self.st[:, 5:6], ALU.add))
        link(dve.scalar_tensor_tensor(col(3), col(0), 0.25, col(0), ALU.mult, ALU.mult),
             dve.tensor_scalar(col(4), col(2), 1.0 / D, LN_EPS, ALU.mult, ALU.add),
             dve.tensor_scalar(col(5), col(1), 0.5, None, ALU.mult))
        link(dve.tensor_tensor(self.rstd[:, 0:1], col(3), col(4), ALU.add))
        link.close()
        yield
        dve.wait_ge(self.rstd_ready, at(i, 1, 1))
        dve.tensor_scalar(out, self.r[:, :], col(5), self.rstd[:, 1:2], ALU.subtract, ALU.mult).then_inc(self.done, 1)

    def on_scalar(self, act, i):
        act.wait_ge(self.step, at(i, self.DVE_STEPS, self.DVE_STEPS))
        act.activation(self.rstd[:, 1:2], self.rstd[:, 0:1], ACT.Ln).then_inc(self.log_ready, 1)
        yield
        act.wait_ge(self.log_ready, at(i, 1, 1))
        act.activation(self.rstd[:, 1:2], self.rstd[:, 1:2], ACT.Exp, scale=-0.5).then_inc(self.rstd_ready, 1)

KV = 4
LAT, QLAT, ROPE, XHD = 64, 96, 64, 128
LOOKBACK = 8
PAIRS = H // 2


class Layer0Lane:

    def __init__(self, nc, ctx, sems, n, ident):
        self.n = n
        ph = Phase(nc, f"a{n}", ctx, sems)
        sb = ph.sb
        self.xt = sb("xt", [P, D])
        self.ct = sb("ct", [P, D])
        self.xcT = sb("xcT", [P, 4, P])
        self.t1 = sb("t1", [P, 4, P])
        self.t2 = sb("t2", [P, 4, P])
        self.qk = sb("qk", [P, 4, P])
        self.kexp = sb("kexp", [P, DC, 8, P])
        self.vaug = sb("vaug", [P, KV, HD + 1])
        self.kvT = sb("kvT", [P, P])
        self.kvaug = sb("kvaug", [P, LAT + 1])
        self.seg = sb("seg", [P, 1])
        self.near = sb("near", [P, 2, P])
        self.key = sb("key", [P, 2, P])
        self.Q = sb("Q", [P, PAIRS, 2, P])
        self.pbuf = sb("pbuf", [P, 2, 4, P])
        self.ptbuf = sb("ptbuf", [P, 2, 4, P])
        self.stats = sb("stats", [P, 32])
        self.osb = sb("osb", [P, H, HD])
        self.oT = sb("oT", [P, DC, P])
        self.x1 = sb("x1", [P, D])
        self.x1T = sb("x1T", [P, DC, P])
        self.qcT = sb("qcT", [QLAT, P])
        self.lat = sb("lat", [P, H, LAT])
        self.latT = sb("latT", [P, PAIRS, P])
        self.x2 = sb("x2", [P, D])
        self.segb = sb("segb", [P, P], BF16)
        self.M, self.S, self.T, self.O = (ph.bank(k) for k in "MSTO")
        self.ln1, self.ln2 = LayerNorm(ph, "ln1"), LayerNorm(ph, "ln2")
        banks = (self.S, self.T, self.O)
        self.self_att = Attention(ph, "self", HD, banks, self.pbuf, self.ptbuf, self.stats, self.osb, ident)
        self.cross_att = Attention(ph, "cross", LAT, banks, self.pbuf, self.ptbuf, self.stats, self.lat, ident)
        self.x_loaded, self.ctx_loaded, self.x2_stored, self.x2_free = (
            ph.sem(k) for k in "x_loaded ctx_loaded x2_stored x2_free".split())
        self.xcT_ps, self.xcT_ready, self.v_ps, self.v_ready = (
            ph.sem(k) for k in "xcT_ps xcT_ready v_ps v_ready".split())
        self.qk_ps, self.rope_step, self.qk_ready, self.kexp_ready = (
            ph.sem(k) for k in "qk_ps rope_step qk_ready kexp_ready".split())
        self.kr_ps, self.kr_ready, self.seg_step, self.oT_ps = (
            ph.sem(k) for k in "kr_ps kr_ready seg_step oT_ps".split())
        self.oT_ready, self.y1_ps, self.x1T_ps, self.x1T_ready = (
            ph.sem(k) for k in "oT_ready y1_ps x1T_ps x1T_ready".split())
        self.qc_ps, self.qc_ready, self.Q_ps, self.Qa_ready = (
            ph.sem(k) for k in "qc_ps qc_ready Q_ps Qa_ready".split())
        self.Qr_ready, self.latT_ps, self.latT_ready, self.y2_ps = (
            ph.sem(k) for k in "Qr_ready latT_ps latT_ready y2_ps".split())


def layer0_attention(nc, sems, d, x_src, x_dst):
    ctx = ExitStack()
    with ctx:
        ph = Phase(nc, "a", ctx, sems)
        sb, sem = ph.sb, ph.sem
        shapes = dict(wqk=[P, 2, DC, 4, P], wv=[P, DC, KV * HD], wo=[P, DC, D], bo=[1, D], rope=[P, 2, P],
                      wkvc2=[P, DC, 2 * LAT], wdq=[P, DC, QLAT], wuq=[P, H, QLAT], wuk=[P, H, LAT],
                      wqr=[QLAT, 2, PAIRS, P], wkr2=[LAT, 2, 2 * ROPE], wuv=[P, H, LAT], wxo=[P, H, D],
                      xrope=[P, 4, P], itok=[P, B])
        w = {k: sb(k, s, I32 if k == "itok" else F32) for k, s in shapes.items()}
        ident = sb("ident", [P, P])
        identb = sb("identb", [P, P], BF16)
        causal = sb("causal", [P, P])
        causalb = sb("causalb", [P, P], BF16)
        own_block = sb("own_block", [P, 8])
        key_id = sb("key_id", [P, 2, P])
        ones = sb("ones", [1, P])
        wabs = sb("wabs", [QLAT, PAIRS, P])
        wuvo = sb("wuvo", [P, PAIRS, D])
        factors = ("wuq", "wuk", "wuv", "wxo")
        factors_loaded, weights = sem("factors_loaded"), sem("weights")
        pool_step, consts = sem("pool_step"), sem("consts")
        products_ready, products_copied = sem("products_ready"), sem("products_copied")

        lanes = [Layer0Lane(nc, ctx, sems, n, ident[:, :]) for n in range(LANES)]
        xscale = float(np.float32(1.0) / np.sqrt(np.float32(XHD + ROPE)))
        block = ctx.enter_context(nc.Block())

        @block.sync
        def _(sp):
            for k in factors:
                sp.dma_start(w[k][:], d[k]).then_inc(factors_loaded, 16)
            for k in shapes:
                if k not in factors:
                    sp.dma_start(w[k][:], d[k]).then_inc(weights, 16)
            for L in lanes:
                sp.dma_start(L.xt[:, :], batch(x_src, L.n)).then_inc(L.x_loaded, 16)
                sp.dma_start(L.ct[:, :], batch(d["ctx"], L.n)).then_inc(L.ctx_loaded, 16)
                sp.sem_inc(L.x2_free, 1)
            with sp.Fori(0, B // LANES - 1) as i:
                for L in lanes:
                    sp.wait_ge(L.xcT_ps, i + 1)
                    sp.dma_start(L.ct[:, :], batch(d["ctx"], (i + 1) * LANES + L.n)).then_inc(L.ctx_loaded, 16)
                for L in lanes:
                    sp.wait_ge(L.ln1.step, at(i, L.ln1.DVE_STEPS, 1))
                    sp.dma_start(L.xt[:, :], batch(x_src, (i + 1) * LANES + L.n)).then_inc(L.x_loaded, 16)
                for L in lanes:
                    store_batch(sp, i, i * LANES + L.n, L.ln2.done, L.x2[:, :], x_dst, L.x2_stored, L.x2_free)
            for L in lanes:
                store_batch(sp, B // LANES - 1, B - LANES + L.n, L.ln2.done, L.x2[:, :], x_dst, L.x2_stored, L.x2_free)

        @block.gpsimd
        def _(pool):
            link = Linked(pool, pool_step)
            fill_identity(pool, link, ident[:, :])
            link(pool.tensor_copy(identb[:, :], ident[:, :]))
            link(pool.memset(causal[:, :], 0.0))
            link(pool.affine_select(out=causal[:, :], in_=causal[:, :], compare_op=ALU.is_ge, fill=MASKED,
                                    base=0, pattern=[[-1, P]], channel_multiplier=1))
            link(pool.tensor_copy(causalb[:, :], causal[:, :]))
            link(pool.memset(own_block[:, :], 1.0))
            link(pool.affine_select(out=own_block[:, :], in_=own_block[:, :], compare_op=ALU.is_ge, fill=0.0,
                                    base=0, pattern=[[-HD, 8]], channel_multiplier=1))
            link(pool.affine_select(out=own_block[:, :], in_=own_block[:, :], compare_op=ALU.is_ge, fill=0.0,
                                    base=HD - 1, pattern=[[HD, 8]], channel_multiplier=-1))
            link(pool.iota(key_id[:, :, :], pattern=[[LOOKBACK, 2], [1, P]], base=0, channel_multiplier=0,
                           allow_small_or_imprecise_dtypes=True))
            link(pool.memset(ones[:, :], 1.0))
            for L in lanes:
                link(pool.memset(L.vaug[:, :, :], 1.0))
                link(pool.memset(L.kvaug[:, :], 1.0))
            pool.sem_inc(consts, 1)
            with pool.Fori(0, B // LANES) as i:
                for c in range(DC):
                    for L in lanes:
                        if c == 0:
                            pool.wait_ge(L.qk_ready, i + 1)
                        pool.tensor_tensor(L.kexp[:, c], spread(L.qk[:, 2 + c, :], 8), along(own_block[:, :], P), ALU.mult)\
                            .then_inc(L.kexp_ready, 1)

        @block.tensor
        def _(pe):
            pe.wait_ge(factors_loaded, 16 * len(factors))
            for h in range(H):
                bank, at0 = (lanes[0].M, lanes[1].M)[h // 8], (h % 8) * LAT
                pe.matmul(bank[0:QLAT, at0:at0 + LAT], w["wuq"][:, h, :], w["wuk"][:, h, :], start=True, stop=True)
            for h in range(H):
                bank, row, col = (lanes[0].S, lanes[1].S, lanes[0].T, lanes[1].T)[h // 4], LAT * (h % 2), (h // 2 % 2) * D
                last = pe.matmul(bank[row:row + LAT, col:col + D], w["wuv"][:, h, :], w["wxo"][:, h, :],
                                 start=True, stop=True)
            last.then_inc(products_ready, 1)
            pe.wait_ge(weights, 16 * (len(shapes) - len(factors)))
            pe.wait_ge(consts, 1)
            pe.wait_ge(products_copied, 6)

            def lane_program(i, L):
                pe.wait_ge(L.x_loaded, at(i, 16, 16))
                pe.wait_ge(L.ctx_loaded, at(i, 16, 16))
                for c in range(DC):
                    pe.transpose(L.M[:, c * P:(c + 1) * P], L.xt[:, c * P:(c + 1) * P], ident[:, :])
                for c in range(DC):
                    last = pe.transpose(L.M[:, (2 + c) * P:(3 + c) * P], L.ct[:, c * P:(c + 1) * P], ident[:, :])
                last.then_inc(L.xcT_ps, 1)
                yield
                pe.wait_ge(L.xcT_ready, i + 1)
                for c in range(DC):
                    pe.matmul(L.O[:, 0:KV * HD], L.xcT[:, c, :], w["wv"][:, c, :], start=c == 0, stop=c == DC - 1)
                for c in range(DC):
                    pe.matmul(L.O[:, 64:192], w["wkvc2"][:, c, :], L.xcT[:, 2 + c, :], start=c == 0, stop=c == DC - 1)
                for c in range(DC):
                    last = pe.matmul(L.O[:, 192:256], L.xcT[:, 2 + c, :], w["wkvc2"][:, c, 0:LAT],
                                     start=c == 0, stop=c == DC - 1)
                last.then_inc(L.v_ps, 1)
                for r, bank in enumerate((L.M, L.S)):
                    for n in range(4):
                        for c in range(DC):
                            last = pe.matmul(bank[:, n * P:(n + 1) * P], w["wqk"][:, r, c, n, :], L.xcT[:, c, :],
                                             start=c == 0, stop=c == DC - 1)
                last.then_inc(L.qk_ps, 1)
                yield
                pe.wait_ge(L.v_ready, at(i, 5, 5))
                for r in range(2):
                    last = pe.matmul(L.O[:, r * P:(r + 1) * P], w["wkr2"][:, r, :], L.kvT[0:LAT, :], start=True, stop=True)
                last.then_inc(L.kr_ps, 1)
                yield
                pe.wait_ge(L.kr_ready, at(i, 2, 2))
                mask4 = spread(causalb[:, :], 4)

                def self_scores(n, bank):
                    if n % 2 == 0:
                        pe.wait_ge(L.kexp_ready, at(i, 2, n // 2 + 1))
                    pe.matmul(four(bank[:, :]), identb[:, :], mask4, start=True, stop=False)
                    return pe.matmul(four(bank[:, :]), L.qk[:, n // 2, :], L.kexp[:, n // 2, 4 * (n % 2):4 * (n % 2) + 4, :],
                                     start=False, stop=True)

                yield from L.self_att.on_tensor(pe, i, self_scores, lambda n, h: L.vaug[:, n, :])
                pe.wait_ge(L.self_att.o_done, at(i, QUADS, QUADS))
                for c in range(DC):
                    last = pe.transpose(L.M[:, c * P:(c + 1) * P], L.osb[:, 8 * c:8 * c + 8, :].rearrange("p h d -> p (h d)"),
                                        ident[:, :])
                last.then_inc(L.oT_ps, 1)
                yield
                pe.wait_ge(L.oT_ready, i + 1)
                pe.matmul(L.M[:, D:2 * D], ones[:, :], w["bo"][:, :], start=True, stop=False)
                for c in range(DC):
                    last = pe.matmul(L.M[:, D:2 * D], L.oT[:, c, :], w["wo"][:, c, :], start=False, stop=c == DC - 1)
                last.then_inc(L.y1_ps, 1)
                yield
                yield
                pe.wait_ge(L.ln1.done, i + 1)
                for c in range(DC):
                    last = pe.transpose(L.M[:, c * P:(c + 1) * P], L.x1[:, c * P:(c + 1) * P], ident[:, :])
                last.then_inc(L.x1T_ps, 1)
                yield
                pe.wait_ge(L.x1T_ready, i + 1)
                for c in range(DC):
                    last = pe.matmul(L.M[0:QLAT, 2 * P:3 * P], w["wdq"][:, c, :], L.x1T[:, c, :], start=c == 0, stop=c == DC - 1)
                last.then_inc(L.qc_ps, 1)
                yield
                pe.wait_ge(L.qc_ready, i + 1)
                for half in range(2):
                    if half:
                        pe.wait_ge(L.Qa_ready, at(i, 4, 2))
                        pe.wait_ge(L.Qr_ready, at(i, 4, 2))
                    for bank, wt in zip((L.M, L.S, L.T), (wabs[:, :, :], w["wqr"][:, 0], w["wqr"][:, 1])):
                        for n in range(4):
                            last = pe.matmul(bank[:, n * P:(n + 1) * P], wt[:, 4 * half + n, :], L.qcT[:, :],
                                             start=True, stop=True)
                    last.then_inc(L.Q_ps, 1)
                    yield
                pe.wait_ge(L.seg_step, at(i, 4, 4))
                seg4 = spread(L.segb[:, :], 4)

                def cross_scores(n, bank):
                    if n % 2 == 0:
                        pe.wait_ge(L.Qa_ready, at(i, 4, 4))
                        pe.wait_ge(L.Qr_ready, at(i, 4, 4))
                    pe.matmul(four(bank[:, :]), identb[:, :], seg4, start=True, stop=False)
                    for h in range(4):
                        last = pe.matmul(bank[:, h * P:(h + 1) * P], L.Q[:, (4 * n + h) // 2, h % 2, :], L.key[:, h % 2, :],
                                         start=False, stop=h == 3)
                    return last

                yield from L.cross_att.on_tensor(pe, i, cross_scores, lambda n, h: L.kvaug[:, :])
                pe.wait_ge(L.cross_att.o_done, at(i, QUADS, QUADS))
                for half, bank in enumerate((L.M, L.S)):
                    for n in range(4):
                        pair = 4 * half + n
                        last = pe.transpose(bank[:, n * P:(n + 1) * P],
                                            L.lat[:, 2 * pair:2 * pair + 2, :].rearrange("p h d -> p (h d)"), ident[:, :])
                    last.then_inc(L.latT_ps, 1)
                yield
                for pair in range(PAIRS):
                    if pair % 4 == 0:
                        pe.wait_ge(L.latT_ready, at(i, 2, pair // 4 + 1))
                    last = pe.matmul(L.T[:, 0:D], L.latT[:, pair, :], wuvo[:, pair, :], start=pair == 0, stop=pair == PAIRS - 1)
                last.then_inc(L.y2_ps, 1)
                yield

            with pe.Fori(0, B // LANES) as i:
                in_turns([lane_program(i, L) for L in lanes])

        @block.scalar
        def _(act):
            act.wait_ge(products_ready, 1)
            for k, bank in enumerate((lanes[0].M, lanes[1].M)):
                act.activation(wabs[:, 4 * k:4 * k + 4, :], four(bank[0:QLAT, :]), ACT.Copy).then_inc(products_copied, 1)
            for k, bank in enumerate((lanes[0].S, lanes[1].S, lanes[0].T, lanes[1].T)):
                act.activation(wuvo[:, 2 * k:2 * k + 2, :], bank[:, :].rearrange("p (a n) -> p a n", a=2), ACT.Copy)\
                   .then_inc(products_copied, 1)

            def lane_program(i, L):
                act.wait_ge(L.xcT_ps, i + 1)
                act.activation(L.xcT[:, :, :], four(L.M[:, :]), ACT.Copy).then_inc(L.xcT_ready, 1)
                yield
                act.wait_ge(L.v_ps, i + 1)
                act.activation(L.vaug[:, :, 0:HD], L.O[:, 0:64].rearrange("p (g d) -> p g d", g=KV), ACT.Copy).then_inc(L.v_ready, 1)
                act.activation(L.kvT[:, :], L.O[:, 64:192], ACT.Copy).then_inc(L.v_ready, 1)
                for parity in range(2):
                    rows = slice(LAT * parity, LAT * parity + LAT)
                    act.activation(L.key[rows, parity, :], L.O[rows, 64:192], ACT.Copy).then_inc(L.v_ready, 1)
                act.activation(L.kvaug[:, 0:LAT], L.O[:, 192:256], ACT.Copy).then_inc(L.v_ready, 1)
                yield
                yield from L.self_att.on_scalar(act, i)
                act.wait_ge(L.oT_ps, i + 1)
                act.activation(L.oT[:, :, :], L.M[:, 0:D].rearrange("p (c n) -> p c n", c=DC), ACT.Copy).then_inc(L.oT_ready, 1)
                yield
                yield from L.ln1.on_scalar(act, i)
                yield
                act.wait_ge(L.x1T_ps, i + 1)
                act.activation(L.x1T[:, :, :], L.M[:, 0:D].rearrange("p (c n) -> p c n", c=DC), ACT.Copy).then_inc(L.x1T_ready, 1)
                yield
                act.wait_ge(L.qc_ps, i + 1)
                act.activation(L.qcT[:, :], L.M[0:QLAT, 2 * P:3 * P], ACT.Copy).then_inc(L.qc_ready, 1)
                yield
                for half in range(2):
                    act.wait_ge(L.Q_ps, at(i, 2, half + 1))
                    for parity in range(2):
                        rows = slice(LAT * parity, LAT * parity + LAT)
                        act.activation(L.Q[rows, 4 * half:4 * half + 4, parity, :], four(L.M[rows, :]), ACT.Copy,
                                       scale=xscale).then_inc(L.Qa_ready, 1)
                    yield
                yield
                yield from L.cross_att.on_scalar(act, i)
                for half, bank in enumerate((L.M, L.S)):
                    act.wait_ge(L.latT_ps, at(i, 2, half + 1))
                    act.activation(L.latT[:, 4 * half:4 * half + 4, :], four(bank[:, :]), ACT.Copy).then_inc(L.latT_ready, 1)
                yield
                yield from L.ln2.on_scalar(act, i)

            with act.Fori(0, B // LANES) as i:
                in_turns([lane_program(i, L) for L in lanes])

        @block.vector
        def _(dve):
            dve.wait_ge(weights, 16 * (len(shapes) - len(factors)))
            dve.wait_ge(consts, 1)

            ALL = slice(0, P)
            OTHER = (slice(LAT, P), slice(0, LAT))

            def rotate(L, link, done, out, plain, swapped, cos, sin, n):
                link(dve.tensor_tensor(L.t1[:, 0:n, :], plain, spread(cos, n), ALU.mult))
                link(dve.tensor_tensor(L.t2[:, 0:n, :], swapped, spread(sin, n), ALU.mult))
                for rows, part in out:
                    dve.tensor_tensor(part, L.t1[rows, 0:n, :], L.t2[rows, 0:n, :], ALU.add).then_inc(done, 1)


            def lane_program(i, L):
                link = Linked(dve, L.seg_step, 4, i)
                link(dve.tensor_copy(L.seg[:, :], w["itok"][:, bass.ds(i * LANES + L.n, 1)]))
                link(dve.tensor_scalar(L.near[:, 0, :], key_id[:, 0, :], L.seg[:, :], MASKED, ALU.is_gt, ALU.mult))
                link(dve.tensor_scalar(L.near[:, 1, :], key_id[:, 1, :], L.seg[:, :], MASKED, ALU.is_lt, ALU.mult))
                link(dve.tensor_tensor(L.segb[:, :], L.near[:, 0, :], L.near[:, 1, :], ALU.add))
                link.close()
                link = Linked(dve, L.rope_step, 8, i)
                dve.wait_ge(L.qk_ps, i + 1)
                rotate(L, link, L.qk_ready, [(ALL, L.qk[:, :, :])], four(L.M[:, :]), four(L.S[:, :]), w["rope"][:, 0, :], w["rope"][:, 1, :], 4)
                yield
                dve.wait_ge(L.kr_ps, i + 1)
                dve.wait_ge(L.qk_ready, i + 1)
                rotate(L, link, L.kr_ready, [(r, L.key[r, q, :].unsqueeze(1)) for q, r in enumerate(OTHER)], L.O[:, 0:P].unsqueeze(1), L.O[:, P:2 * P].unsqueeze(1),
                       w["xrope"][:, 0, :], w["xrope"][:, 1, :], 1)
                yield
                yield from L.self_att.on_vector(dve, i)
                dve.wait_ge(L.y1_ps, i + 1)
                yield from L.ln1.on_vector(dve, i, L.x1[:, :], L.xt[:, :], L.M[:, D:2 * D])
                yield
                dve.wait_ge(L.kr_ready, at(i, 2, 2))
                for half in range(2):
                    dve.wait_ge(L.Q_ps, at(i, 2, half + 1))
                    if half:
                        dve.wait_ge(L.Qr_ready, at(i, 4, 2))
                    rotate(L, link, L.Qr_ready, [(r, L.Q[r, 4 * half:4 * half + 4, q, :]) for q, r in enumerate(OTHER)], four(L.S[:, :]), four(L.T[:, :]),
                           w["xrope"][:, 2, :], w["xrope"][:, 3, :], 4)
                    yield
                link.close()
                yield
                yield from L.cross_att.on_vector(dve, i)
                dve.wait_ge(L.y2_ps, i + 1)
                dve.wait_ge(L.x2_free, i + 1)
                yield from L.ln2.on_vector(dve, i, L.x2[:, :], L.x1[:, :], L.T[:, 0:D])

            with dve.Fori(0, B // LANES) as i:
                in_turns([lane_program(i, L) for L in lanes])


def layout_layer0_attention(inp):
    f = np.float32
    by_chunk = lambda a: np.ascontiguousarray(a.reshape(DC, P, -1).transpose(1, 0, 2))
    half = HD // 2
    Wq = inp["L0_attn_Wq"].reshape(D, DC, P)
    Wk = inp["L0_attn_Wk"].reshape(D, DC, 2, HD).repeat(4, axis=2).reshape(D, DC, P)
    plain = np.concatenate([Wq, Wk], axis=1)
    swap = plain.reshape(D, 4, 8, 2, half)[:, :, :, ::-1].reshape(D, 4, P)
    wqk = np.stack([plain, swap]).reshape(2, DC, P, 4, P).transpose(2, 0, 1, 3, 4)
    inv = (1.0 / f(10000.0) ** (np.arange(0, HD, 2, dtype=f) / f(HD))).astype(f)
    ang = np.outer(np.arange(S, dtype=f), inv).astype(f)
    row = np.arange(P)
    sign = np.where(row % HD < half, -1, 1).astype(f)[:, None]
    root = f(0.5)
    rope = np.stack([root * np.cos(ang).T[row % half], root * sign * np.sin(ang).T[row % half]], axis=1)
    xh = ROPE // 2
    xinv = (1.0 / f(10000.0) ** (np.arange(xh, dtype=f) / f(xh))).astype(f)
    xang = (np.arange(S, dtype=f)[:, None] * xinv).astype(f)
    xsign = np.where(row % ROPE < xh, -1, 1).astype(f)[:, None]
    xc, xs = np.cos(xang).T[row % xh], xsign * np.sin(xang).T[row % xh]
    scale = f(1.0) / np.sqrt(f(XHD + ROPE))
    xrope = np.stack([xc, xs, xc * scale, xs * scale], axis=1)
    Wkvc = inp["L0_xattn_W_kvc"]
    Wqr = inp["L0_xattn_W_qr"].reshape(QLAT, PAIRS, 2, ROPE)[:, :, ::-1]
    Wqr_s = Wqr.reshape(QLAT, PAIRS, 2, 2, xh)[:, :, :, ::-1]
    Wkr = inp["L0_xattn_W_kr"]
    Wkr_s = Wkr.reshape(LAT, 2, xh)[:, ::-1].reshape(LAT, ROPE)
    head_d = lambda a, n: a.reshape(n, H, XHD).transpose(2, 1, 0)
    out = dict(
        ctx=inp["ctx_2048"], wqk=wqk, wv=by_chunk(inp["L0_attn_Wv"]), wo=by_chunk(inp["L0_attn_Wo"]),
        bo=inp["L0_attn_bo"].reshape(1, D), rope=rope, wkvc2=by_chunk(np.concatenate([Wkvc, Wkvc], axis=1)),
        wdq=by_chunk(inp["L0_xattn_W_dq"]), wuq=head_d(inp["L0_xattn_W_uq"], QLAT), wuk=head_d(inp["L0_xattn_W_uk"], LAT),
        wqr=np.stack([Wqr.reshape(QLAT, PAIRS, P), Wqr_s.reshape(QLAT, PAIRS, P)], axis=1),
        wkr2=np.stack([np.concatenate([a, a], axis=1) for a in (Wkr, Wkr_s)], axis=1),
        wuv=head_d(inp["L0_xattn_W_uv"], LAT), wxo=inp["L0_xattn_W_o"].reshape(H, XHD, D).transpose(1, 0, 2),
        xrope=xrope, itok=inp["itok_BxS_0_1023"].T)
    return out


EXPERTS, TOP, INNER = 16, 4, 176
EPAIR = 2 * INNER
EP = EXPERTS // 2 + 1
ECH = 3
EREST = EPAIR - 2 * P


def layer0_experts(nc, sems, d, x_src, x_dst):
    ctx = ExitStack()
    with ctx:
        ph = Phase(nc, "b", ctx, sems)
        sb, sem = ph.sb, ph.sem
        wgate = sb("wgate", [P, DC, EXPERTS])
        wup = sb("wup", [P, EP, 2, DC, EPAIR])
        wdown = sb("wdown", [P, EP, ECH, D])
        ident = sb("ident", [P, P])
        before = sb("before", [P, EXPERTS, EXPERTS])
        xt = sb("xt", [P, D])
        xT = sb("xT", [P, DC, P])
        col = sb("col", [P, 4])
        prob = sb("prob", [P, 2, EXPERTS])
        cmp_ = sb("cmp", [P, 2, EXPERTS, EXPERTS])
        rank = sb("rank", [P, EXPERTS])
        route = sb("route", [P, 2 * EP])
        sg = sb("sg", [P, 2, EPAIR])
        act_ = sb("act", [P, 2, ECH * P])
        aT = sb("aT", [P, 2, ECH, P])
        xo = sb("xo", [P, D])
        G0, G1, U0, U1, T0, T1, Y, M = (ph.bank(n) for n in ("G0", "G1", "U0", "U1", "T0", "T1", "Y", "M"))
        G, U, T = (G0, G1), (U0, U1), (T0, T1)
        ln = LayerNorm(ph, "ln")
        weights, pool_step, consts, x_loaded, stored = (sem(n) for n in ("weights", "pool_step", "consts", "x_loaded", "stored"))
        xo_free = sem("xo_free")
        pair_loaded = [sem(f"pair{e}_loaded") for e in range(EP)]
        xT_ps, xT_ready, logits_ready, route_step, exp_ready, route_ready = (sem(n) for n in (
            "xT_ps", "xT_ready", "logits_ready", "route_step", "exp_ready", "route_ready"))
        up_ready, silu_ready, act_ready, aT_ps, aT_ready, y_ready = (sem(n) for n in (
            "up_ready", "silu_ready", "act_ready", "aT_ps", "aT_ready", "y_ready"))
        ROUTE = 11
        block = ctx.enter_context(nc.Block())

        @block.sync
        def _(sp):
            sp.dma_start(xt[:, :], batch(x_src, 0)).then_inc(x_loaded, 16)
            sp.dma_start(wgate[:], d["wgate"]).then_inc(weights, 16)
            for e in range(EP):
                sp.dma_start(wup[:, e], d["wup"][:, e]).then_inc(pair_loaded[e], 16)
                sp.dma_start(wdown[:, e], d["wdown"][:, e]).then_inc(pair_loaded[e], 16)
            sp.sem_inc(xo_free, 1)
            with sp.Fori(0, B - 1) as i:
                sp.wait_ge(ln.step, at(i, ln.DVE_STEPS, 1))
                sp.dma_start(xt[:, :], batch(x_src, i + 1)).then_inc(x_loaded, 16)
                store_batch(sp, i, i, ln.done, xo[:, :], x_dst, stored, xo_free)
            store_batch(sp, B - 1, B - 1, ln.done, xo[:, :], x_dst, stored, xo_free)

        @block.gpsimd
        def _(pool):
            link = Linked(pool, pool_step)
            fill_identity(pool, link, ident[:, :])
            link(pool.memset(before[:, :, :], 1.0))
            link(pool.affine_select(out=before[:, :, :], in_=before[:, :, :], compare_op=ALU.is_ge, fill=0.0, base=-1,
                                    pattern=[[1, EXPERTS], [-1, EXPERTS]], channel_multiplier=0))
            link(pool.memset(act_[:, :, :], 0.0))
            pool.memset(route[:, :], 1.0).then_inc(consts, 1)

        @block.tensor
        def _(pe):
            pe.wait_ge(weights, 16)
            pe.wait_ge(consts, 1)
            with pe.Fori(0, B) as i:
                pe.wait_ge(x_loaded, at(i, 16, 16))
                for c in range(DC):
                    last = pe.transpose(M[:, c * P:(c + 1) * P], xt[:, c * P:(c + 1) * P], ident[:, :])
                last.then_inc(xT_ps, 1)
                pe.wait_ge(xT_ready, i + 1)
                for c in range(DC):
                    last = pe.matmul(M[:, D:D + EXPERTS], xT[:, c, :], wgate[:, c, :], start=c == 0, stop=c == DC - 1)
                last.then_inc(logits_ready, 1)
                for s in range(EP + 2):
                    if s < EP:
                        pe.wait_ge(pair_loaded[s], 32)
                        if s >= 2:
                            pe.wait_ge(act_ready, at(i, 2 * EP, 2 * s - 2))
                        for k, bank in enumerate((G[s % 2], U[s % 2])):
                            for c in range(DC):
                                last = pe.matmul(bank[:, 0:EPAIR], xT[:, c, :], wup[:, s, k, c, :], start=c == 0, stop=c == DC - 1)
                        last.then_inc(up_ready, 1)
                    if 1 <= s <= EP:
                        n = s - 1
                        pe.wait_ge(act_ready, at(i, 2 * EP, 2 * n + 2))
                        if n >= 2:
                            pe.wait_ge(aT_ready, at(i, EP, n - 1))
                        for c in range(ECH):
                            last = pe.transpose(T[n % 2][:, c * P:(c + 1) * P], act_[:, n % 2, c * P:(c + 1) * P], ident[:, :])
                        last.then_inc(aT_ps, 1)
                    if s >= 2:
                        n = s - 2
                        pe.wait_ge(aT_ready, at(i, EP, n + 1))
                        for c in range(ECH):
                            rows = P if c < 2 else EREST
                            last = pe.matmul(Y[:, 0:D], aT[0:rows, n % 2, c, :], wdown[0:rows, n, c, :],
                                             start=n == 0 and c == 0, stop=n == EP - 1 and c == ECH - 1)
                        last.then_inc(y_ready, 1)

        @block.scalar
        def _(act):
            with act.Fori(0, B) as i:
                act.wait_ge(xT_ps, i + 1)
                act.activation(xT[:, :, :], M[:, 0:D].rearrange("p (c n) -> p c n", c=DC), ACT.Copy).then_inc(xT_ready, 1)
                act.wait_ge(route_step, at(i, ROUTE, 2))
                act.activation(prob[:, 0, :], prob[:, 0, :], ACT.Exp).then_inc(exp_ready, 1)
                for s in range(EP + 1):
                    if s < EP:
                        act.wait_ge(up_ready, at(i, EP, s + 1))
                        if s >= 2:
                            act.wait_ge(act_ready, at(i, 2 * EP, 2 * s - 2))
                        act.activation(sg[:, s % 2, :], G[s % 2][:, 0:EPAIR], ACT.Silu).then_inc(silu_ready, 1)
                    if s >= 1:
                        n = s - 1
                        act.wait_ge(aT_ps, at(i, EP, n + 1))
                        if n >= 2:
                            act.wait_ge(y_ready, at(i, EP, n - 1))
                        act.activation(aT[:, n % 2], T[n % 2][:, 0:ECH * P].rearrange("p (c n) -> p c n", c=ECH), ACT.Copy)\
                           .then_inc(aT_ready, 1)
                in_turns([ln.on_scalar(act, i)])

        @block.vector
        def _(dve):
            dve.wait_ge(consts, 1)
            with dve.Fori(0, B) as i:
                link = Linked(dve, route_step, ROUTE, i)
                dve.wait_ge(logits_ready, i + 1)
                logits = M[:, D:D + EXPERTS]
                link(dve.tensor_reduce(col[:, 0:1], logits, AX.X, ALU.max))
                link(dve.tensor_scalar(prob[:, 0, :], logits, col[:, 0:1], None, ALU.subtract))
                dve.wait_ge(exp_ready, i + 1)
                link(dve.tensor_reduce(col[:, 1:2], prob[:, 0, :], AX.X, ALU.add))
                link(dve.reciprocal(col[:, 2:3], col[:, 1:2]))
                link(dve.tensor_scalar(prob[:, 1, :], prob[:, 0, :], col[:, 2:3], None, ALU.mult))
                pj, pi = spread(prob[:, 1, :], EXPERTS), along(prob[:, 1, :], EXPERTS)
                link(dve.tensor_tensor(cmp_[:, 0], pj, pi, ALU.is_gt))
                link(dve.tensor_tensor(cmp_[:, 1], pj, pi, ALU.is_equal))
                link(dve.tensor_tensor(cmp_[:, 1], cmp_[:, 1], before[:, :, :], ALU.mult))
                link(dve.tensor_tensor(cmp_[:, 0], cmp_[:, 0], cmp_[:, 1], ALU.add))
                link(dve.tensor_reduce(rank[:, :], cmp_[:, 0], AX.X, ALU.add))
                link(dve.scalar_tensor_tensor(route[:, 0:EXPERTS], rank[:, :], TOP - 0.5, prob[:, 1, :], ALU.is_lt, ALU.mult))
                link.close()
                for s in range(EP):
                    dve.wait_ge(silu_ready, at(i, EP, s + 1))
                    if s >= 2:
                        dve.wait_ge(aT_ps, at(i, EP, s - 1))
                    for j in range(2):
                        cols = slice(j * INNER, (j + 1) * INNER)
                        dve.scalar_tensor_tensor(act_[:, s % 2, cols], sg[:, s % 2, cols], route[:, 2 * s + j:2 * s + j + 1],
                                                 U[s % 2][:, cols], ALU.mult, ALU.mult).then_inc(act_ready, 1)
                dve.wait_ge(y_ready, at(i, EP, EP))
                dve.wait_ge(xo_free, i + 1)
                in_turns([ln.on_vector(dve, i, xo[:, :], xt[:, :], Y[:, 0:D])])


def layout_layer0_experts(inp):
    def up(routed, shared):
        pairs = inp[routed].reshape(EP - 1, 2, D, INNER).transpose(0, 2, 1, 3).reshape(EP - 1, D, EPAIR)
        return np.concatenate([pairs, inp[shared][None]]).reshape(EP, DC, P, EPAIR)
    wup = np.stack([up("L0_ffn_wg", "L0_ffn_sg"), up("L0_ffn_wu", "L0_ffn_su")]).transpose(3, 1, 0, 2, 4)
    down = np.concatenate([inp["L0_ffn_wd"].reshape(EP - 1, EPAIR, D), inp["L0_ffn_sd"][None]])
    down = np.concatenate([down, np.zeros((EP, ECH * P - EPAIR, D), np.float32)], axis=1)
    return dict(wgate=inp["L0_ffn_w_gate"].T.reshape(DC, P, EXPERTS).transpose(1, 0, 2), wup=wup,
                wdown=down.reshape(EP, ECH, P, D).transpose(2, 0, 1, 3))


KEY_HEADS, VAL_HEADS, DK, TAPS = 16, 32, 128, 4
HB = 4
KB = HB // 2
ROUNDS = VAL_HEADS // HB
ITEMS = HB * B
QK = 2 * KB
CHUNKS = QK + HB
BL = 32
NBL = S // BL
RMS_EPS = 1e-6
TINY = 1e-12


def layer1_delta_rule(nc, sems, d, x_src, x_dst):
    ctx = ExitStack()
    with ctx:
        ph = Phase(nc, "c", ctx, sems)
        sb, sem = ph.sb, ph.sem
        ident = sb("ident", [P, P])
        identb = sb("identb", [P, P], BF16)
        tri = sb("tri", [P, P])
        hidden = sb("hidden", [P, P])
        hiddenb = sb("hiddenb", [P, P], BF16)
        ones = sb("ones", [P, 1])
        zero = sb("zero", [P, 1])
        wba = sb("wba", [P, DC, 2 * VAL_HEADS])
        bias = sb("bias", [P, 2, VAL_HEADS])
        normw = sb("normw", [P, 1])
        wqk = sb("wqk", [P, QK, DC * P])
        wv = sb("wv", [P, HB, DC * P])
        wcqk = sb("wcqk", [P, QK, TAPS])
        wcv = sb("wcv", [P, HB, TAPS])
        wz = sb("wz", [P, DC, HB * P])
        wout = sb("wout", [P, HB, D])
        acc = sb("acc", [P, B, D])
        xT = sb("xT", [P, DC, B, P])
        beta = sb("beta", [P, B, VAL_HEADS])
        g = sb("g", [P, B, VAL_HEADS])
        gcn = sb("gcn", [P, B, VAL_HEADS])
        gR, gcnR, betaR = (sb(n, [P, HB, B]) for n in ("gR", "gcnR", "betaR"))
        pad = sb("pad", [P, 2, B, TAPS - 1 + S])
        cv = sb("cv", [P, 2, B, S])
        qkT = sb("qkT", [P, KB, 2, B, S])
        sq = sb("sq", [P, 2, B, S])
        root = sb("root", [P, KB, 2, B])
        nrm = sb("nrm", [P, 3, KB, 2, B])
        cj = sb("cj", [P, HB, B])
        V = sb("V", [P, HB, B, S])
        NP = sb("NP", [P, HB, B, 2, S])
        A = sb("A", [P, BL, BL])
        sm = A[:, :, :].rearrange("p a b -> p (a b)").rearrange("p (k b h) -> p k b h", k=4, b=B)
        T = sb("T", [P, BL, BL])
        T0 = sb("T0", [P, BL, BL], BF16)
        tmp = sb("tmp", [P, 256])
        Tb = sb("Tb", [P, ITEMS, P])
        TbT = sb("TbT", [P, ITEMS, P])
        Y = sb("Y", [P, HB, B, S])
        zs = sb("zs", [P, B, HB * P])
        s2 = sb("s2", [P, HB, B])
        f = sb("f", [P, 3, HB, B])
        yT = sb("yT", [P, 2, HB, S])
        banks = [ph.bank(f"bank{n}") for n in range(8)]
        blocks = nc.dram_tensor("diagonal_blocks", (3, NBL, ITEMS, BL, BL), F32, kind="Internal").ap()
        names = """blocks_out inverse_out weights consts pool_step x_loaded xT_ps xT_copied ba_ps gate_step gate_act gc_ps gates_ready
            qk_loaded v_loaded z_loaded out_loaded gates_used proj_ready pad_ready tap0_ready conv_step cv_ready silu_ready sq_ready norms_ps
            root_ready rms_ready csqa_ready norm_step gcrow_ps E_ready GP_ps NP_ready gathered elim_step scattered diag_cleared
            vt_ps V_ready z_ps z_ready MT_ps MT_ready apply_ps y_ready W_ps W_ready C_ps C_ready csq_ready s2_ready
            wout_ready var_ready f_step y_scaled yT_ps yT_ready out_ps acc_step
            ln_step ln_log ln_rstd xo_ready stored""".split()
        s = {n: sem(n) for n in names}
        quads = [(h, q) for h in range(HB) for q in range(2)]
        flat = lambda ap: ap.rearrange("p a b -> p (a b)")
        ELIM = 2 * (BL - 1) + 2
        F_STEPS = 2 * KB + 1
        order = [(2 * k + e, q) for k in range(KB) for q in range(2) for e in range(2)]
        block = ctx.enter_context(nc.Block())

        def project_banks(m):
            n = (0, 2, 6, 4)[m] if m < QK else 2 * (m % 2)
            return banks[n], banks[n + 1]

        def rr(t, h, q):
            return t[:, h, 4 * q:4 * q + 4]

        @block.sync
        def _(sp):
            for dst, k in ((wba, "wba"), (bias, "bias"), (normw, "normw")):
                sp.dma_start(dst[:], d[k]).then_inc(s["weights"], 16)
            sp.dma_start(acc[:, :, :], x_src.rearrange("b p c -> p b c")).then_inc(s["x_loaded"], 16)

            def load(dst, name, r, loaded):
                sp.dma_start(dst[:], d[name][bass.ds(r, 1)].rearrange("a p m n -> (a p) m n")).then_inc(s[loaded], 16)

            def load_qk(r):
                load(wqk, "wqk", r, "qk_loaded")
                load(wcqk, "wcqk", r, "qk_loaded")

            def load_v(r):
                load(wv, "wv", r, "v_loaded")
                load(wcv, "wcv", r, "v_loaded")

            def invert(i):
                sp.wait_ge(s["NP_ready"], at(i, ITEMS, ITEMS))
                for r in range(NBL):
                    rows = slice(BL * r, BL * r + BL)
                    sp.dma_start(blocks[0, r].rearrange("t j i -> j t i"), NP[rows, :, :, 0, rows].rearrange("p h b i -> p (h b) i"))\
                        .then_inc(s["blocks_out"], 16)
                sp.wait_ge(s["blocks_out"], at(i, 16 * NBL, 16 * NBL))
                sp.dma_start(A[:, :, :], blocks[0].rearrange("r t j i -> (r t) j i")).then_inc(s["gathered"], 16)
                for n, src in ((1, T), (2, A)):
                    sp.wait_ge(s["elim_step"], at(i, ELIM, ELIM - 2 + n))
                    sp.dma_start(blocks[n].rearrange("r t i k -> (r t) i k"), src[:, :, :]).then_inc(s["inverse_out"], 16)
                sp.wait_ge(s["inverse_out"], at(i, 32, 32))
                for n, dst in ((1, Tb), (2, TbT)):
                    for r in range(NBL):
                        rows = slice(BL * r, BL * r + BL)
                        sp.dma_start(dst[rows, :, rows], blocks[n, r].rearrange("t i k -> i t k")).then_inc(s["scattered"], 16)

            load_qk(0)
            load_v(0)
            load(wz, "wz", 0, "z_loaded")
            load(wout, "wout", 0, "out_loaded")
            sp.wait_ge(s["proj_ready"], QK)
            sp.wait_ge(s["cv_ready"], QK)
            load_qk(1)
            with sp.Fori(0, ROUNDS - 1) as i:
                invert(i)
                sp.wait_ge(s["cv_ready"], at(i, CHUNKS, CHUNKS))
                load_v(i + 1)
                sp.wait_ge(s["z_ps"], at(i, B, B))
                load(wz, "wz", i + 1, "z_loaded")
                sp.wait_ge(s["cv_ready"], at(i + 1, CHUNKS, QK))
                load_qk(i + 2)
                sp.wait_ge(s["out_ps"], at(i, B, B))
                load(wout, "wout", i + 1, "out_loaded")
            invert(ROUNDS - 1)
            with sp.Fori(0, B) as b:
                sp.wait_ge(s["xo_ready"], b + 1)
                sp.dma_start(x_dst[bass.ds(b, 1)].rearrange("a p c -> p a c"), acc[:, bass.ds(b, 1), :]).then_inc(s["stored"], 16)
            sp.wait_ge(s["stored"], 16 * B)

        @block.gpsimd
        def _(pool):
            link = Linked(pool, s["pool_step"])
            fill_identity(pool, link, ident[:, :])
            link(pool.tensor_copy(identb[:, :], ident[:, :]))
            link(pool.memset(tri[:, :], 1.0))
            link(pool.affine_select(out=tri[:, :], in_=tri[:, :], compare_op=ALU.is_ge, fill=0.0, base=0,
                                    pattern=[[1, P]], channel_multiplier=-1))
            link(pool.memset(hidden[:, :], 0.0))
            link(pool.affine_select(out=hidden[:, :], in_=hidden[:, :], compare_op=ALU.is_ge, fill=MASKED, base=0,
                                    pattern=[[1, P]], channel_multiplier=-1))
            link(pool.tensor_copy(hiddenb[:, :], hidden[:, :]))
            link(pool.memset(T0[:, :, :], 0.0))
            link(pool.affine_select(out=T0[:, :, :], in_=T0[:, :, :], compare_op=ALU.not_equal, fill=1.0, base=0,
                                    pattern=[[1, BL], [-1, BL]], channel_multiplier=0))
            link(pool.memset(zero[:, :], 0.0))
            link(pool.memset(Tb[:, :, :], 0.0))
            link(pool.memset(TbT[:, :, :], 0.0))
            link(pool.memset(pad[:, :, :, :], 0.0))
            pool.memset(ones[:, :], 1.0).then_inc(s["consts"], 1)

            def tap0(r, m, first=False):
                pool.wait_ge(s["pad_ready"], at(r, 2 * CHUNKS, 2 * m + 2))
                if m < 2 and not first:
                    pool.wait_ge(s["vt_ps"], at(r, 2 * HB, 2 * m - 2))
                elif 2 <= m < QK + 2:
                    pool.wait_ge(s["silu_ready"], at(r, CHUNKS, m - 1))
                elif m >= QK + 2:
                    pool.wait_ge(s["vt_ps"], at(r, 2 * HB, 2 * (m - QK - 1)))
                w = wcqk[:, m, 0:1] if m < QK else wcv[:, m - QK, 0:1]
                pool.tensor_tensor(cv[:, m % 2], pad[:, m % 2, :, 0:S], along(w.broadcast_to([P, B]), S), ALU.mult)\
                    .then_inc(s["tap0_ready"], 1)

            def square(r, m, first=False):
                pool.wait_ge(s["silu_ready"], at(r, CHUNKS, m + 1))
                if m >= 2 or not first:
                    pool.wait_ge(s["norms_ps"], at(r, QK, m - 1))
                src = qkT[:, m // 2, m % 2]
                pool.tensor_tensor(sq[:, m % 2], src, src, ALU.mult).then_inc(s["sq_ready"], 1)

            def round_(i, more):
                pool.wait_ge(s["out_loaded"], at(i, 16, 16))
                pool.wait_ge(s["weights"], 48)
                pool.tensor_tensor(flat(wout[:, :, :]), flat(wout[:, :, :]), normw[:, 0:1].broadcast_to([P, HB * D]), ALU.mult)\
                    .then_inc(s["wout_ready"], 1)
                tap0(i, QK)
                tap0(i, QK + 1)
                pool.wait_ge(s["blocks_out"], at(i, 16 * NBL, 16 * NBL))
                pool.wait_ge(s["tap0_ready"], at(i, CHUNKS, QK + 2))
                for r in range(NBL):
                    rows = slice(BL * r, BL * r + BL)
                    if r:
                        pool.wait_ge(s["diag_cleared"], at(i, NBL, r))
                    none = along(zero[rows, 0:1].broadcast_to([BL, ITEMS]), BL)
                    pool.tensor_tensor(NP[rows, :, :, 0, rows].rearrange("p h b i -> p (h b) i"), none, none, ALU.add)\
                        .then_inc(s["diag_cleared"], 1)
                pool.wait_ge(s["diag_cleared"], at(i, NBL, NBL))
                tap0(i, QK + 2)
                tap0(i, QK + 3)
                if more:
                    tap0(i + 1, 0)
                    tap0(i + 1, 1)
                    square(i + 1, 0)
                    tap0(i + 1, 2)
                    square(i + 1, 1)
                    tap0(i + 1, 3)
                    square(i + 1, 2)
                    square(i + 1, 3)
                for n in range(0, 8, 2):
                    h, q = quads[n]
                    pool.wait_ge(s["C_ready"], at(i, 8, n + 1))
                    pool.tensor_tensor(rr(V, h, q), rr(Y, h, q), rr(Y, h, q), ALU.mult).then_inc(s["csq_ready"], 1)

            for m in range(QK + 1):
                if m < QK:
                    tap0(0, m, first=True)
                if m >= 1:
                    square(0, m - 1, first=True)
            with pool.Fori(0, ROUNDS - 1) as i:
                round_(i, True)
            round_(ROUNDS - 1, False)

        @block.tensor
        def _(pe):
            pe.wait_ge(s["consts"], 1)
            pe.wait_ge(s["x_loaded"], 16)
            for b in range(B):
                bank = banks[b // 2]
                for c in range(DC):
                    last = pe.transpose(bank[:, (2 * (b % 2) + c) * P:(2 * (b % 2) + c + 1) * P], acc[:, b, c * P:(c + 1) * P],
                                        ident[:, :])
                last.then_inc(s["xT_ps"], 1)
            pe.wait_ge(s["weights"], 48)
            pe.wait_ge(s["xT_copied"], 4)
            for b in range(B):
                for c in range(DC):
                    last = pe.matmul(banks[4][:, 64 * b:64 * b + 64], xT[:, c, b, :], wba[:, c, :], start=c == 0, stop=c == DC - 1)
            last.then_inc(s["ba_ps"], 1)
            pe.wait_ge(s["gate_step"], 6)
            pe.matmul(banks[5][:, 0:B * VAL_HEADS], tri[:, :], flat(g[:, :, :]), start=True, stop=True).then_inc(s["gc_ps"], 1)

            def project(r, m, first=False):
                pair, w = project_banks(m), wqk[:, m] if m < QK else wv[:, m - QK]
                if m == 0:
                    pe.wait_ge(s["qk_loaded"], at(r, 32, 32))
                if m == QK:
                    pe.wait_ge(s["v_loaded"], at(r, 32, 32))
                if m >= QK + 2:
                    pe.wait_ge(s["pad_ready"], at(r, 2 * CHUNKS, 2 * (m - 1)))
                if m < QK and not first:
                    used, per, n = (("pad_ready", 2 * CHUNKS, -2), ("pad_ready", 2 * CHUNKS, 0),
                                    ("z_ready", B, 0), ("V_ready", 2 * HB, 0))[m]
                    pe.wait_ge(s[used], at(r, per, n))
                for q in range(2):
                    for c in range(DC):
                        last = pe.matmul(four(pair[q][:, :]), w[:, c * P:(c + 1) * P], xT[:, c, 4 * q:4 * q + 4, :],
                                         start=c == 0, stop=c == DC - 1)
                last.then_inc(s["proj_ready"], 1)

            def norms(r, m):
                if m == 0:
                    pe.wait_ge(s["pad_ready"], at(r, 2 * CHUNKS, 6))
                pe.wait_ge(s["sq_ready"], at(r, QK, m + 1))
                for b in range(B):
                    last = pe.matmul(banks[7][:, m * B + b:m * B + b + 1], sq[:, m % 2, b, :], ones[:, :], start=True, stop=True)
                last.then_inc(s["norms_ps"], 1)

            def gcrow(i, n):
                h, q = order[n]
                bank = banks[4 + n % 2]
                if n == 0:
                    pe.wait_ge(s["pad_ready"], at(i, 2 * CHUNKS, 2 * QK))
                if n >= 2:
                    pe.wait_ge(s["E_ready"], at(i, ITEMS, 4 * (n - 1)))
                pe.matmul(four(bank[:, :]), identb[:, :], spread(hiddenb[:, :], 4), start=True, stop=False)
                for b in range(4):
                    last = pe.matmul(bank[:, b * P:(b + 1) * P], gR[:, h, 4 * q + b:4 * q + b + 1].broadcast_to([P, P]), tri[:, :],
                                     start=False, stop=b == 3)
                last.then_inc(s["gcrow_ps"], 1)

            def gram(i, u):
                k, b0 = u // 4, 2 * (u % 4)
                bank = banks[6 + u % 2]
                if u == 0:
                    pe.wait_ge(s["root_ready"], at(i, 1, 1))
                if u >= 2:
                    pe.wait_ge(s["NP_ready"], at(i, ITEMS, 4 * (u - 1)))
                for b in range(2):
                    last = pe.matmul(bank[:, b * 2 * P:(b + 1) * 2 * P].rearrange("p (a n) -> p a n", a=2),
                                     qkT[:, k, 0, b0 + b, :], qkT[:, k, :, b0 + b, :], start=True, stop=True)
                last.then_inc(s["GP_ps"], 1)

            def values(i, n):
                pe.wait_ge(s["silu_ready"], at(i, CHUNKS, QK + n + 1))
                if n == 0:
                    pe.wait_ge(s["E_ready"], at(i, ITEMS, ITEMS))
                for q in range(2):
                    if n >= 1:
                        pe.wait_ge(s["V_ready"], at(i, 2 * HB, 2 * n - 1 + q))
                    for b in range(4):
                        last = pe.transpose(banks[4 + q][:, b * P:(b + 1) * P], cv[:, n % 2, 4 * q + b, :], ident[:, :])
                    last.then_inc(s["vt_ps"], 1)

            def out_gate(i, b):
                if b == 0:
                    pe.wait_ge(s["z_loaded"], at(i, 16, 16))
                    pe.wait_ge(s["NP_ready"], at(i, ITEMS, ITEMS))
                if b >= 2:
                    pe.wait_ge(s["z_ready"], at(i, B, b - 1))
                for c in range(DC):
                    last = pe.matmul(banks[6 + b % 2][:, :], xT[:, c, b, :], wz[:, c, :], start=c == 0, stop=c == DC - 1)
                last.then_inc(s["z_ps"], 1)

            def items(ps, n, lhsT, rhs):
                h, q = quads[n]
                for b in range(4):
                    last = pe.matmul(banks[n % 4][:, b * P:(b + 1) * P], lhsT(h, 4 * q + b), rhs(h, 4 * q + b), start=True, stop=True)
                last.then_inc(s[ps], 1)

            def apply(i, rep):
                y = V if rep == 0 else Y
                for n in range(8):
                    if rep == 0:
                        pe.wait_ge(s["MT_ready"], at(i, 8, min(n + 5, 8)))
                    else:
                        pe.wait_ge(s["y_ready"], at(i, 24, 8 * (rep - 1) + n + 1))
                    if n >= 4 or rep:
                        pe.wait_ge(s["y_ready"], at(i, 24, 8 * rep + n - 3))
                    items("apply_ps", n, lambda h, b: NP[:, h, b, 0, :], lambda h, b: y[:, h, b, :])

            def round_(i, more):
                project(i, QK)
                pe.wait_ge(s["gates_used"], at(i, 3, 3))
                gcrow(i, 0)
                gcrow(i, 1)
                project(i, QK + 1)
                for grp in range(4):
                    if grp:
                        gcrow(i, 2 * grp)
                        gcrow(i, 2 * grp + 1)
                    gram(i, 2 * grp)
                    gram(i, 2 * grp + 1)
                project(i, QK + 2)
                project(i, QK + 3)
                values(i, 0)
                for b in range(B):
                    out_gate(i, b)
                if more:
                    project(i + 1, 0)
                    project(i + 1, 1)
                    project(i + 1, 2)
                values(i, 1)
                values(i, 2)
                values(i, 3)
                pe.wait_ge(s["scattered"], at(i, 128, 128))
                pe.wait_ge(s["diag_cleared"], at(i, NBL, NBL))
                if more:
                    pe.wait_ge(s["pad_ready"], at(i + 1, 2 * CHUNKS, 4))
                for n in range(8):
                    if n >= 4:
                        pe.wait_ge(s["MT_ready"], at(i, 8, n - 3))
                    items("MT_ps", n, lambda h, b: Tb[:, h * B + b, :], lambda h, b: NP[:, h, b, 0, :])
                pe.wait_ge(s["V_ready"], at(i, 2 * HB, 2 * HB))
                if more:
                    project(i + 1, 3)
                    norms(i + 1, 0)
                apply(i, 0)
                if more:
                    norms(i + 1, 1)
                apply(i, 1)
                if more:
                    norms(i + 1, 2)
                apply(i, 2)
                if more:
                    norms(i + 1, 3)
                for n in range(8):
                    pe.wait_ge(s["y_ready"], at(i, 24, 16 + max(n + 1, min(n + 5, 8))))
                    if n >= 4:
                        pe.wait_ge(s["W_ready"], at(i, 8, n - 3))
                    items("W_ps", n, lambda h, b: TbT[:, h * B + b, :], lambda h, b: Y[:, h, b, :])
                for n in range(8):
                    pe.wait_ge(s["W_ready"], at(i, 8, min(n + 5, 8)))
                    if n >= 4:
                        pe.wait_ge(s["C_ready"], at(i, 8, n - 3))
                    items("C_ps", n, lambda h, b: NP[:, h, b, 1, :], lambda h, b: Y[:, h, b, :])
                pe.wait_ge(s["wout_ready"], at(i, 1, 1))
                pe.wait_ge(s["C_ready"], at(i, 8, 8))
                for b in range(B + 1):
                    if b < B:
                        if b >= 2:
                            pe.wait_ge(s["yT_ready"], at(i, B, b - 1))
                        pe.wait_ge(s["y_scaled"], at(i, ITEMS, HB * (b + 1)))
                        for h in range(HB):
                            last = pe.transpose(banks[b % 2][:, h * P:(h + 1) * P], Y[:, h, b, :], ident[:, :])
                        last.then_inc(s["yT_ps"], 1)
                    if b >= 1:
                        m = b - 1
                        pe.wait_ge(s["yT_ready"], at(i, B, m + 1))
                        if m >= 2:
                            pe.wait_ge(s["acc_step"], at(i, B, m - 1))
                        for h in range(HB):
                            last = pe.matmul(banks[2 + m % 2][:, 0:D], yT[:, m % 2, h, :], wout[:, h, :], start=h == 0, stop=h == HB - 1)
                        last.then_inc(s["out_ps"], 1)
                pe.wait_ge(s["acc_step"], at(i, B, B))

            pe.wait_ge(s["gate_step"], 8)
            for m in range(QK):
                project(0, m, first=True)
            for m in range(QK):
                norms(0, m)
            with pe.Fori(0, ROUNDS - 1) as i:
                round_(i, True)
            round_(ROUNDS - 1, False)

        @block.scalar
        def _(act):
            for n in range(4):
                act.wait_ge(s["xT_ps"], 2 * n + 2)
                act.activation(xT[:, :, 2 * n:2 * n + 2, :], banks[n][:, :].rearrange("p (b c n) -> p c b n", b=2, c=DC), ACT.Copy)\
                    .then_inc(s["xT_copied"], 1)
            ba = banks[4][:, :].rearrange("p (b k h) -> p b k h", b=B, k=2)
            act.wait_ge(s["ba_ps"], 1)
            act.activation(sm[:, 0], ba[:, :, 0, :], ACT.Exp, scale=-1.0).then_inc(s["gate_act"], 1)
            act.wait_ge(s["gate_step"], 2)
            act.activation(sm[:, 2], sm[:, 2], ACT.Exp, scale=-1.0).then_inc(s["gate_act"], 1)
            act.wait_ge(s["gate_step"], 3)
            act.activation(sm[:, 2], sm[:, 3], ACT.Ln).then_inc(s["gate_act"], 1)
            act.wait_ge(s["weights"], 48)
            act.activation(bias[:, 1, :], bias[:, 1, :], ACT.Exp).then_inc(s["gate_act"], 1)

            def copy_in(r, m, first=False):
                act.wait_ge(s["proj_ready"], at(r, CHUNKS, m + 1))
                if m >= 2 or not first:
                    act.wait_ge(s["cv_ready"], at(r, CHUNKS, m - 1))
                    act.wait_ge(s["tap0_ready"], at(r, CHUNKS, m - 1))
                pair = project_banks(m)
                for q in range(2):
                    act.activation(pad[:, m % 2, 4 * q:4 * q + 4, TAPS - 1:], four(pair[q][:, :]), ACT.Copy)\
                        .then_inc(s["pad_ready"], 1)

            def silu(r, m):
                act.wait_ge(s["cv_ready"], at(r, CHUNKS, m + 1))
                dst = qkT[:, m // 2, m % 2] if m < QK else cv[:, m % 2]
                act.activation(dst, cv[:, m % 2], ACT.Silu).then_inc(s["silu_ready"], 1)

            def take_root(r):
                act.wait_ge(s["norms_ps"], at(r, QK, QK))
                act.activation(root[:, :, :, :].rearrange("p k q b -> p (k q b)"), banks[7][:, 0:QK * B], ACT.Sqrt)\
                    .then_inc(s["root_ready"], 1)

            def out_gate(i, b):
                act.wait_ge(s["z_ps"], at(i, B, b + 1))
                act.activation(zs[:, b, :], banks[6 + b % 2][:, :], ACT.Silu).then_inc(s["z_ready"], 1)

            def copy_quad(i, ps, n, dst, ready):
                act.wait_ge(s[ps], at(i, 8, n + 1))
                act.activation(dst, four(banks[n % 4][:, :]), ACT.Copy).then_inc(s[ready], 1)

            def round_(i, more):
                copy_in(i, QK)
                copy_in(i, QK + 1)
                for n, (h, q) in enumerate(order):
                    act.wait_ge(s["gcrow_ps"], at(i, 8, n + 1))
                    for b in range(4):
                        act.activation(NP[:, h, 4 * q + b, 1, :], banks[4 + n % 2][:, b * P:(b + 1) * P], ACT.Exp,
                                       bias=gcnR[:, h, 4 * q + b:4 * q + b + 1]).then_inc(s["E_ready"], 1)
                copy_in(i, QK + 2)
                silu(i, QK)
                copy_in(i, QK + 3)
                silu(i, QK + 1)
                for b in range(B):
                    out_gate(i, b)
                silu(i, QK + 2)
                if more:
                    copy_in(i + 1, 0)
                silu(i, QK + 3)
                if more:
                    copy_in(i + 1, 1)
                    silu(i + 1, 0)
                    copy_in(i + 1, 2)
                    silu(i + 1, 1)
                for n, (h, q) in enumerate(quads):
                    copy_quad(i, "MT_ps", n, NP[:, h, 4 * q:4 * q + 4, 0, :], "MT_ready")
                if more:
                    copy_in(i + 1, 3)
                    silu(i + 1, 2)
                    silu(i + 1, 3)
                for n, (h, q) in enumerate(quads):
                    copy_quad(i, "W_ps", n, rr(Y, h, q), "W_ready")
                if more:
                    take_root(i + 1)
                for n, (h, q) in enumerate(quads):
                    copy_quad(i, "C_ps", n, rr(Y, h, q), "C_ready")
                    if n % 2:
                        act.wait_ge(s["C_ready"], at(i, 8, n + 1))
                        act.activation(rr(V, h, q), rr(Y, h, q), ACT.Square).then_inc(s["csqa_ready"], 1)
                act.wait_ge(s["var_ready"], at(i, 2, 2))
                act.activation(f[:, 1], f[:, 0], ACT.Sqrt).then_inc(s["rms_ready"], 1)
                for b in range(B):
                    act.wait_ge(s["yT_ps"], at(i, B, b + 1))
                    if b >= 2:
                        act.wait_ge(s["out_ps"], at(i, B, b - 1))
                    act.activation(yT[:, b % 2], four(banks[b % 2][:, :]), ACT.Copy).then_inc(s["yT_ready"], 1)

            for m in range(QK + 1):
                if m < QK:
                    copy_in(0, m, first=True)
                if m >= 1:
                    silu(0, m - 1)
            take_root(0)
            with act.Fori(0, ROUNDS - 1) as i:
                round_(i, True)
            round_(ROUNDS - 1, False)
            act.wait_ge(s["ln_step"], 3 * B + 1)
            act.activation(f[:, 1, 0, :], f[:, 0, 0, :], ACT.Ln).then_inc(s["ln_log"], 1)
            act.wait_ge(s["ln_log"], 1)
            act.activation(f[:, 1, 0, :], f[:, 1, 0, :], ACT.Exp, scale=-0.5).then_inc(s["ln_rstd"], 1)

        @block.vector
        def _(dve):
            link = Linked(dve, s["gate_step"])
            ba = banks[4][:, :].rearrange("p (b k h) -> p b k h", b=B, k=2)
            dve.wait_ge(s["weights"], 48)
            dve.wait_ge(s["gate_act"], 1)
            link(dve.tensor_tensor(sm[:, 1], ba[:, :, 1, :], spread(bias[:, 0, :], B), ALU.add))
            link(dve.scalar_tensor_tensor(sm[:, 2], sm[:, 1], -1.0, sm[:, 1], ALU.mult, ALU.max))
            dve.wait_ge(s["gate_act"], 2)
            link(dve.tensor_scalar(sm[:, 3], sm[:, 2], 1.0, None, ALU.add))
            dve.wait_ge(s["gate_act"], 4)
            link(dve.scalar_tensor_tensor(sm[:, 1], sm[:, 1], 0.0, sm[:, 2], ALU.max, ALU.add))
            link(dve.tensor_scalar(sm[:, 0], sm[:, 0], 1.0, None, ALU.add))
            link(dve.scalar_tensor_tensor(g[:, :, :], sm[:, 1], -1.0, spread(bias[:, 1, :], B), ALU.mult, ALU.mult))
            link(dve.reciprocal(beta[:, :, :], sm[:, 0]))
            dve.wait_ge(s["gc_ps"], 1)
            link(dve.tensor_scalar(flat(gcn[:, :, :]), banks[5][:, 0:B * VAL_HEADS], -1.0, None, ALU.mult))
            dve.wait_ge(s["consts"], 1)

            def tap(r, m, t):
                if t == 1:
                    dve.wait_ge(s["tap0_ready"], at(r, CHUNKS, m + 1))
                else:
                    dve.wait_ge(s["conv_step"], at(r, 2 * CHUNKS, 2 * m + t - 1))
                w = wcqk[:, m, t:t + 1] if m < QK else wcv[:, m - QK, t:t + 1]
                dve.scalar_tensor_tensor(cv[:, m % 2], pad[:, m % 2, :, t:t + S], w, cv[:, m % 2], ALU.mult, ALU.add)\
                    .then_inc(s["conv_step" if t < TAPS - 1 else "cv_ready"], 1)

            def conv(r, m):
                for t in range(1, TAPS):
                    tap(r, m, t)

            def values(i, n, q):
                dve.wait_ge(s["vt_ps"], at(i, 2 * HB, 2 * n + q + 1))
                dve.tensor_tensor(rr(V, n, q), four(banks[4 + q][:, :]), along(nrm[:, 0, n // 2, 0, 4 * q:4 * q + 4], P), ALU.mult)\
                    .then_inc(s["V_ready"], 1)

            def round_(i, more):
                for dst, src in ((gR, g), (gcnR, gcn), (betaR, beta)):
                    dve.tensor_copy(dst[:, :, :], src[:, :, bass.ds(i * HB, HB)].rearrange("p b h -> p h b"))\
                        .then_inc(s["gates_used"], 1)
                link = Linked(dve, s["norm_step"], 3 + KB, i)
                dve.wait_ge(s["root_ready"], at(i, 1, 1))
                link(dve.tensor_scalar(nrm[:, 0], root[:, :, :, :], TINY, None, ALU.max))
                link(dve.reciprocal(nrm[:, 1], nrm[:, 0]))
                link(dve.tensor_tensor(nrm[:, 2], nrm[:, 1], nrm[:, 1], ALU.mult))
                dve.wait_ge(s["gates_used"], at(i, 3, 3))
                for k in range(KB):
                    link(dve.tensor_tensor(cj[:, 2 * k:2 * k + 2, :], betaR[:, 2 * k:2 * k + 2, :], spread(nrm[:, 2, k, 0, :], 2), ALU.mult))
                link.close()
                for grp in range(4):
                    k, q = grp // 2, grp % 2
                    dve.wait_ge(s["E_ready"], at(i, ITEMS, 8 * grp + 8))
                    for u in range(2):
                        dve.wait_ge(s["GP_ps"], at(i, 8, 2 * grp + u + 1))
                        for b in range(2):
                            gp = banks[6 + u][:, b * 2 * P:(b + 1) * 2 * P].rearrange("p (a n) -> p a n", a=2)
                            for e in range(2):
                                h, bb = 2 * k + e, 4 * q + 2 * u + b
                                dve.scalar_tensor_tensor(NP[:, h, bb, :, :], spread(NP[:, h, bb, 1, :], 2), cj[:, h, bb:bb + 1], gp,
                                                         ALU.mult, ALU.mult).then_inc(s["NP_ready"], 1)
                conv(i, QK)
                conv(i, QK + 1)
                elim = Linked(dve, s["elim_step"], ELIM, i)
                elim(dve.tensor_copy(T[:, :, :], T0[:, :, :]))
                dve.wait_ge(s["gathered"], at(i, 16, 16))
                for j in range(BL - 1):
                    n, w = BL - 1 - j, j + 1
                    part = tmp[:, 0:n * w].rearrange("p (n w) -> p n w", n=n)
                    elim(dve.tensor_tensor(part, along(A[:, j, j + 1:BL], w), spread(T[:, j, 0:w], n), ALU.mult))
                    elim(dve.tensor_tensor(T[:, j + 1:BL, 0:w], T[:, j + 1:BL, 0:w], part, ALU.subtract))
                elim(dve.tensor_copy(A[:, :, :], T[:, :, :].rearrange("p i k -> p k i")))
                elim.close()
                for n in range(HB):
                    values(i, n, 0)
                    values(i, n, 1)
                    if n < 2:
                        conv(i, QK + 2 + n)
                    elif more:
                        conv(i + 1, n - 2)
                for rep in range(3):
                    for n, (h, q) in enumerate(quads):
                        dve.wait_ge(s["apply_ps"], at(i, 24, 8 * rep + n + 1))
                        dve.tensor_tensor(rr(Y, h, q), rr(V, h, q), four(banks[n % 4][:, :]), ALU.subtract).then_inc(s["y_ready"], 1)
                        if more and rep < 2 and n >= 5:
                            tap(i + 1, rep + 2, n - 4)
                for n, (h, q) in enumerate(quads):
                    dve.wait_ge(s["csqa_ready" if n % 2 else "csq_ready"], at(i, 4, n // 2 + 1))
                    dve.tensor_reduce(s2[:, h, 4 * q:4 * q + 4], rr(V, h, q), AX.X, ALU.add).then_inc(s["s2_ready"], 1)
                dve.wait_ge(s["s2_ready"], at(i, 8, 8))
                for k in range(KB):
                    dve.tensor_tensor(f[:, 0, 2 * k:2 * k + 2, :], s2[:, 2 * k:2 * k + 2, :], spread(nrm[:, 2, k, 1, :], 2), ALU.mult)\
                        .then_inc(s["f_step"], 1)
                dve.wait_ge(s["f_step"], at(i, F_STEPS, KB))
                dve.tensor_scalar(f[:, 0], f[:, 0], 1.0 / (DK * DK), RMS_EPS, ALU.mult, ALU.add).then_inc(s["var_ready"], 2)
                dve.wait_ge(s["rms_ready"], at(i, 1, 1))
                dve.reciprocal(f[:, 0], f[:, 1]).then_inc(s["f_step"], 1)
                dve.wait_ge(s["f_step"], at(i, F_STEPS, KB + 1))
                for k in range(KB):
                    dve.scalar_tensor_tensor(f[:, 2, 2 * k:2 * k + 2, :], f[:, 0, 2 * k:2 * k + 2, :], DK ** -0.5, spread(nrm[:, 1, k, 1, :], 2),
                                             ALU.mult, ALU.mult).then_inc(s["f_step"], 1)
                dve.wait_ge(s["f_step"], at(i, F_STEPS, F_STEPS))

                def add_out(b):
                    dve.wait_ge(s["out_ps"], at(i, B, b + 1))
                    dve.tensor_tensor(acc[:, b, :], acc[:, b, :], banks[2 + b % 2][:, 0:D], ALU.add).then_inc(s["acc_step"], 1)

                for b in range(B):
                    for h in range(HB):
                        dve.scalar_tensor_tensor(Y[:, h, b, :], Y[:, h, b, :], f[:, 2, h, b:b + 1], zs[:, b, h * P:(h + 1) * P],
                                                 ALU.mult, ALU.mult).then_inc(s["y_scaled"], 1)
                    if b >= 2:
                        add_out(b - 2)
                add_out(B - 2)
                add_out(B - 1)

            for m in range(QK):
                conv(0, m)
            with dve.Fori(0, ROUNDS - 1) as i:
                round_(i, True)
            round_(ROUNDS - 1, False)
            dve.wait_ge(s["acc_step"], ROUNDS * B)
            link = Linked(dve, s["ln_step"])
            for b in range(B):
                dve.bn_stats(cj[:, 0, 0:6], acc[:, b, :]).then_inc(s["ln_step"], 1)
                dve.wait_ge(s["ln_step"], 3 * b + 1)
                dve.bn_aggr(gR[:, 0, 0:2], cj[:, 0, 0:6]).then_inc(s["ln_step"], 1)
                dve.wait_ge(s["ln_step"], 3 * b + 2)
                dve.tensor_copy(f[:, 2, 0:2, b], gR[:, 0, 0:2]).then_inc(s["ln_step"], 1)
                dve.wait_ge(s["ln_step"], 3 * b + 3)
            dve.tensor_scalar(f[:, 0, 0, :], f[:, 2, 1, :], LN_EPS, None, ALU.add).then_inc(s["ln_step"], 1)
            dve.wait_ge(s["ln_rstd"], 1)
            for b in range(B):
                dve.tensor_scalar(acc[:, b, :], acc[:, b, :], f[:, 2, 0, b:b + 1], f[:, 1, 0, b:b + 1], ALU.subtract, ALU.mult)\
                    .then_inc(s["xo_ready"], 1)


def layout_layer1_delta_rule(inp):
    W = inp["L1_attn_W_qkv"]
    q, k, v = (a.reshape(-1, P, D) for a in np.split(W, [KEY_HEADS * DK, 2 * KEY_HEADS * DK]))
    cw = inp["L1_attn_conv_w"]
    cq, ck, cvv = (a.reshape(-1, P, TAPS) for a in np.split(cw, [KEY_HEADS * DK, 2 * KEY_HEADS * DK]))

    def rounds(k, q, v):
        kq = np.stack([k, q], axis=1).reshape(ROUNDS, QK, *k.shape[1:])
        return np.concatenate([kq, v.reshape(ROUNDS, HB, *v.shape[1:])], axis=1)
    wqkv = rounds(k, q, v).reshape(ROUNDS, CHUNKS, P, DC, P).transpose(0, 4, 1, 3, 2)
    wconv = rounds(ck, cq, cvv).transpose(0, 2, 1, 3)
    wz = inp["L1_attn_W_z"].reshape(ROUNDS, HB * P, DC, P).transpose(0, 3, 2, 1)
    wout = inp["L1_attn_W_out"].T.reshape(ROUNDS, HB, P, D).transpose(0, 2, 1, 3)
    wba = np.concatenate([inp["L1_attn_W_b"], inp["L1_attn_W_a"]]).T.reshape(DC, P, 2 * VAL_HEADS).transpose(1, 0, 2)
    bias = np.broadcast_to(np.stack([inp["L1_attn_dt_bias"], inp["L1_attn_A_log"]])[None], (P, 2, VAL_HEADS))
    wqk, wcqk = (np.concatenate([a, a[:1]]) for a in (wqkv.reshape(ROUNDS, P, CHUNKS, DC * P)[:, :, :QK], wconv[:, :, :QK]))
    return dict(wqk=wqk, wcqk=wcqk, wv=wqkv.reshape(ROUNDS, P, CHUNKS, DC * P)[:, :, QK:], wcv=wconv[:, :, QK:], wz=wz, wout=wout, wba=wba, bias=bias, normw=inp["L1_attn_norm_w"].reshape(P, 1))


LEVELS, QUANT_EPS = 127.0, 1e-8
MAGIC = 1.5 * 2.0 ** 23


class Quantizer:

    STEPS = 5

    def __init__(self, ph, name, per):
        self.col = ph.sb(name + "_col", [P, 2])
        self.t = ph.sb(name + "_t", [P, 2, D])
        self.step = ph.sem(name + "_step")
        self.done = ph.sem(name + "_done")
        self.per = per

    def on_vector(self, dve, i, n, src, out, step_out):
        link = Linked(dve, self.step, self.STEPS * self.per, i)
        link.n = self.STEPS * n
        link(dve.tensor_reduce(self.col[:, 0:1], src, AX.X, ALU.max, apply_absolute_value=True))
        link(dve.tensor_scalar(step_out, self.col[:, 0:1], 1.0 / LEVELS, QUANT_EPS, ALU.mult, ALU.max))
        link(dve.reciprocal(self.col[:, 1:2], step_out))
        link(dve.tensor_scalar(self.t[:, 0, :], src, self.col[:, 1:2], LEVELS, ALU.mult, ALU.min))
        link(dve.tensor_scalar(self.t[:, 1, :], self.t[:, 0, :], -LEVELS, MAGIC, ALU.max, ALU.add))
        dve.tensor_scalar(out, self.t[:, 1, :], MAGIC, None, ALU.subtract).then_inc(self.done, 1)
        dve.wait_ge(self.done, at(i, self.per, n + 1))


class Layer1Lane:

    def __init__(self, nc, ctx, sems, n, ident):
        self.n = n
        ph = Phase(nc, f"d{n}", ctx, sems)
        sb = ph.sb
        self.xt = sb("xt", [P, D])
        self.ct = sb("ct", [P, D])
        self.mask = sb("mask", [P, P])
        self.cT = sb("cT", [P, DC, P])
        self.xstep = sb("xstep", [P, 2])
        self.y8 = sb("y8", [P, 2, D])
        self.yb = sb("yb", [P, 2, D])
        self.qT = sb("qT", [P, DC, P])
        self.kT = sb("kT", [P, DC, P])
        self.kexp = sb("kexp", [P, DC, 8, P])
        self.vaug = sb("vaug", [P, H, HD + 1])
        self.pbuf = sb("pbuf", [P, 2, 4, P])
        self.ptbuf = sb("ptbuf", [P, 2, 4, P])
        self.stats = sb("stats", [P, 32])
        self.osb = sb("osb", [P, H, HD])
        self.x5 = sb("x5", [P, D])
        self.x5T = sb("x5T", [P, DC, P])
        self.col = sb("col", [P, 6])
        self.prob = sb("prob", [P, 5, H])
        self.qT2 = sb("qT2", [P, DC, P])
        self.kv = sb("kv", [P, 2, H, HD])
        self.best = sb("best", [P, 2, HD])
        self.krep = sb("krep", [P, 8, HD])
        self.krepT = sb("krepT", [P, P])
        self.vaug2 = sb("vaug2", [P, HD + 1])
        self.osb2 = sb("osb2", [P, H, HD])
        self.xo = sb("xo", [P, D])
        self.x8 = sb("x8", [P, 2, D], BF16)
        self.x8T = sb("x8T", [P, 2, DC, P], BF16)
        self.M, self.S, self.T, self.O = (ph.bank(k) for k in "MSTO")
        self.Mb = self.M[:, :].bitcast(BF16)
        self.ln1, self.ln2 = LayerNorm(ph, "ln1"), LayerNorm(ph, "ln2")
        self.xquant = Quantizer(ph, "xquant", 2)
        banks = (self.S, self.T, self.O)
        self.cross_att = Attention(ph, "cross", HD, banks, self.pbuf, self.ptbuf, self.stats, self.osb, ident)
        self.self_att = Attention(ph, "self", HD, banks, self.pbuf, self.ptbuf, self.stats, self.osb2, ident)
        self.x_loaded, self.ctx_loaded, self.mask_loaded, self.stored = (
            ph.sem(k) for k in "x_loaded ctx_loaded mask_loaded stored".split())
        self.xo_free, self.cT_ps, self.cT_ready, self.kv_ps = (
            ph.sem(k) for k in "xo_free cT_ps cT_ready kv_ps".split())
        self.kT_ready, self.v_ready, self.kexp_ready, self.x8T_ps = (
            ph.sem(k) for k in "kT_ready v_ready kexp_ready x8T_ps".split())
        self.x8T_ready, self.y8_ps, self.y8_step, self.yb_ready = (
            ph.sem(k) for k in "x8T_ready y8_ps y8_step yb_ready".split())
        self.qT_ps, self.qT_ready, self.x5T_ps, self.x5T_ready = (
            ph.sem(k) for k in "qT_ps qT_ready x5T_ps x5T_ready".split())
        self.logits_ps, self.top_step, self.exp_ready, self.qkv_ps = (
            ph.sem(k) for k in "logits_ps top_step exp_ready qkv_ps".split())
        self.qT2_ready, self.best_step, self.krep_ready, self.vaug2_ready = (
            ph.sem(k) for k in "qT2_ready best_step krep_ready vaug2_ready".split())
        self.krepT_ps, self.krepT_ready, self.kexp2_ready = (
            ph.sem(k) for k in "krepT_ps krepT_ready kexp2_ready".split())


def layer1_attention(nc, sems, d, x_src, x_dst):
    ctx = ExitStack()
    with ctx:
        ph = Phase(nc, "d", ctx, sems)
        sb, sem = ph.sb, ph.sem
        shapes = dict(wq8=[P, DC, D], wo8=[P, DC, D], wk=[P, DC, D], wv=[P, DC, D], bk=[P, DC], bv=[1, D],
                      bqo=[P, 2, D], wtop=[P, DC, H], wqkv=[P, DC, 3 * D])
        w = {k: sb(k, s) for k, s in shapes.items()}
        ident = sb("ident", [P, P])
        identb = sb("identb", [P, P], BF16)
        causal = sb("causal", [P, P])
        causalb = sb("causalb", [P, P], BF16)
        own_block = sb("own_block", [P, 8])
        head_id = sb("head_id", [P, 2, H])
        ones = sb("ones", [1, P])
        w8 = sb("w8", [P, 2, DC, D], BF16)
        w8T = sb("w8T", [P, 2, DC, D], BF16)
        wstep = sb("wstep", [P, 2, DC])
        wstep_row = sb("wstep_row", [P, 2, D])
        wquant = Quantizer(ph, "wquant", 2 * DC)
        s = {n: sem(n) for n in "weights pool_step consts w8T_ps w8T_ready wstep_ps wstep_ready".split()}

        lanes = [Layer1Lane(nc, ctx, sems, n, ident[:, :]) for n in range(LANES)]
        TOP = 10
        half = lambda ap: ap.rearrange("p (c n) -> p c n", c=DC)
        block = ctx.enter_context(nc.Block())

        @block.sync
        def _(sp):
            for k in shapes:
                sp.dma_start(w[k][:], d[k]).then_inc(s["weights"], 16)
            for L in lanes:
                sp.dma_start(L.ct[:, :], batch(d["ctx"], L.n)).then_inc(L.ctx_loaded, 16)
                sp.dma_start(L.xt[:, :], batch(x_src, L.n)).then_inc(L.x_loaded, 16)
                sp.dma_start(L.mask[:, :], batch(d["mask"], L.n)).then_inc(L.mask_loaded, 16)
                sp.sem_inc(L.xo_free, 1)
            with sp.Fori(0, B // LANES - 1) as i:
                for L in lanes:
                    sp.wait_ge(L.cT_ps, i + 1)
                    sp.dma_start(L.ct[:, :], batch(d["ctx"], (i + 1) * LANES + L.n)).then_inc(L.ctx_loaded, 16)
                for L in lanes:
                    sp.wait_ge(L.cross_att.scores_ready, at(i, QUADS, QUADS))
                    sp.dma_start(L.mask[:, :], batch(d["mask"], (i + 1) * LANES + L.n)).then_inc(L.mask_loaded, 16)
                for L in lanes:
                    sp.wait_ge(L.ln1.step, at(i, L.ln1.DVE_STEPS, 1))
                    sp.dma_start(L.xt[:, :], batch(x_src, (i + 1) * LANES + L.n)).then_inc(L.x_loaded, 16)
                for L in lanes:
                    store_batch(sp, i, i * LANES + L.n, L.ln2.done, L.xo[:, :], x_dst, L.stored, L.xo_free)
            for L in lanes:
                store_batch(sp, B // LANES - 1, B - LANES + L.n, L.ln2.done, L.xo[:, :], x_dst, L.stored, L.xo_free)

        @block.gpsimd
        def _(pool):
            link = Linked(pool, s["pool_step"])
            fill_identity(pool, link, ident[:, :])
            link(pool.tensor_copy(identb[:, :], ident[:, :]))
            link(pool.memset(causal[:, :], 0.0))
            link(pool.affine_select(out=causal[:, :], in_=causal[:, :], compare_op=ALU.is_ge, fill=MASKED,
                                    base=0, pattern=[[-1, P]], channel_multiplier=1))
            link(pool.tensor_copy(causalb[:, :], causal[:, :]))
            link(pool.memset(own_block[:, :], 1.0))
            link(pool.affine_select(out=own_block[:, :], in_=own_block[:, :], compare_op=ALU.is_ge, fill=0.0,
                                    base=0, pattern=[[-HD, 8]], channel_multiplier=1))
            link(pool.affine_select(out=own_block[:, :], in_=own_block[:, :], compare_op=ALU.is_ge, fill=0.0,
                                    base=HD - 1, pattern=[[HD, 8]], channel_multiplier=-1))
            link(pool.iota(head_id[:, :, :], pattern=[[H, 2], [1, H]], base=0, channel_multiplier=0,
                           allow_small_or_imprecise_dtypes=True))
            link(pool.memset(ones[:, :], 1.0))
            for L in lanes:
                link(pool.memset(L.vaug2[:, :], 1.0))
                link(pool.memset(L.vaug[:, :, :], 1.0))
            pool.sem_inc(s["consts"], 1)
            with pool.Fori(0, B // LANES) as i:
                for c in range(DC):
                    for L in lanes:
                        if c == 0:
                            pool.wait_ge(L.kT_ready, at(i, DC, DC))
                        pool.tensor_tensor(L.kexp[:, c], spread(L.kT[:, c, :], 8), along(own_block[:, :], P), ALU.mult)\
                            .then_inc(L.kexp_ready, 1)
                for L in lanes:
                    pool.wait_ge(L.krepT_ready, i + 1)
                    pool.tensor_tensor(L.kexp[:, 0], spread(L.krepT[:, :], 8), along(own_block[:, :], P), ALU.mult)\
                        .then_inc(L.kexp2_ready, 1)

        @block.tensor
        def _(pe):
            pe.wait_ge(s["weights"], 16 * len(shapes))
            pe.wait_ge(s["consts"], 1)
            for k in range(2):
                for c in range(DC):
                    pe.wait_ge(wquant.done, 2 * k + c + 1)
                    for m in range(DC):
                        last = pe.transpose(lanes[k].Mb[:, m * D + c * P:m * D + (c + 1) * P],
                                            w8[:, k, c, m * P:(m + 1) * P], identb[:, :])
                last.then_inc(s["w8T_ps"], 1)
            for k in range(2):
                for c in range(DC):
                    last = pe.matmul(lanes[0].S[:, (2 * k + c) * P:(2 * k + c + 1) * P], wstep[:, k, c:c + 1].broadcast_to([P, P]), ident[:, :],
                                     start=True, stop=True)
            last.then_inc(s["wstep_ps"], 1)
            pe.wait_ge(s["w8T_ready"], 2)
            pe.wait_ge(s["wstep_ready"], 1)

            def lane_program(i, L):
                pe.wait_ge(L.ctx_loaded, at(i, 16, 16))
                for c in range(DC):
                    last = pe.transpose(L.M[:, c * P:(c + 1) * P], L.ct[:, c * P:(c + 1) * P], ident[:, :])
                last.then_inc(L.cT_ps, 1)
                yield
                pe.wait_ge(L.cT_ready, i + 1)
                for m in range(DC):
                    for c in range(DC):
                        pe.matmul(L.S[:, m * P:(m + 1) * P], w["wk"][:, c, m * P:(m + 1) * P], L.cT[:, c, :], start=c == 0, stop=c == DC - 1)
                pe.matmul(L.T[:, 0:D], ones[:, :], w["bv"][:, :], start=True, stop=False)
                for c in range(DC):
                    last = pe.matmul(L.T[:, 0:D], L.cT[:, c, :], w["wv"][:, c, :], start=False, stop=c == DC - 1)
                last.then_inc(L.kv_ps, 1)

                def project8(n, out):
                    yield
                    pe.wait_ge(L.xquant.done, at(i, 2, n + 1))
                    for c in range(DC):
                        last = pe.transpose(L.Mb[:, c * P:(c + 1) * P], L.x8[:, n, c * P:(c + 1) * P], identb[:, :])
                    last.then_inc(L.x8T_ps, 1)
                    yield
                    pe.wait_ge(L.x8T_ready, at(i, 2, n + 1))
                    for c in range(DC):
                        last = pe.matmul(out, L.x8T[:, n, c, :], w8T[:, n, c, :], start=c == 0, stop=c == DC - 1)
                    last.then_inc(L.y8_ps, 1)

                yield from project8(0, L.M[:, D:2 * D])
                yield
                pe.wait_ge(L.yb_ready, at(i, 2, 1))
                for c in range(DC):
                    last = pe.transpose(L.M[:, c * P:(c + 1) * P], L.yb[:, 0, c * P:(c + 1) * P], ident[:, :])
                last.then_inc(L.qT_ps, 1)
                yield
                pe.wait_ge(L.qT_ready, i + 1)
                pe.wait_ge(L.v_ready, i + 1)
                pe.wait_ge(L.mask_loaded, at(i, 16, 16))

                def cross_scores(n, bank):
                    if n % 2 == 0:
                        pe.wait_ge(L.kexp_ready, at(i, DC, n // 2 + 1))
                    pe.matmul(four(bank[:, :]), ident[:, :], spread(L.mask[:, :], 4), start=True, stop=False)
                    return pe.matmul(four(bank[:, :]), L.qT[:, n // 2, :], L.kexp[:, n // 2, 4 * (n % 2):4 * (n % 2) + 4, :],
                                     start=False, stop=True)

                yield from L.cross_att.on_tensor(pe, i, cross_scores, lambda n, h: L.vaug[:, 4 * n + h, :])
                yield from project8(1, L.M[:, D:2 * D])
                yield
                yield
                pe.wait_ge(L.ln1.done, i + 1)
                for c in range(DC):
                    last = pe.transpose(L.M[:, c * P:(c + 1) * P], L.x5[:, c * P:(c + 1) * P], ident[:, :])
                last.then_inc(L.x5T_ps, 1)
                yield
                pe.wait_ge(L.x5T_ready, i + 1)
                for c in range(DC):
                    last = pe.matmul(L.M[:, D:D + H], L.x5T[:, c, :], w["wtop"][:, c, :], start=c == 0, stop=c == DC - 1)
                last.then_inc(L.logits_ps, 1)
                for c in range(DC):
                    last = pe.matmul(L.O[:, :], L.x5T[:, c, :], w["wqkv"][:, c, D:3 * D], start=c == 0, stop=c == DC - 1)
                for m in range(DC):
                    for c in range(DC):
                        last = pe.matmul(L.T[:, m * P:(m + 1) * P], w["wqkv"][:, c, m * P:(m + 1) * P], L.x5T[:, c, :],
                                         start=c == 0, stop=c == DC - 1)
                last.then_inc(L.qkv_ps, 1)
                yield
                pe.wait_ge(L.krep_ready, i + 1)
                pe.transpose(L.M[:, 0:P], L.krep[:, :, :].rearrange("p r d -> p (r d)"), ident[:, :]).then_inc(L.krepT_ps, 1)
                yield
                pe.wait_ge(L.vaug2_ready, i + 1)
                pe.wait_ge(L.qT2_ready, i + 1)

                def self_scores(n, bank):
                    if n == 0:
                        pe.wait_ge(L.kexp2_ready, i + 1)
                    pe.matmul(four(bank[:, :]), identb[:, :], spread(causalb[:, :], 4), start=True, stop=False)
                    return pe.matmul(four(bank[:, :]), L.qT2[:, n // 2, :], L.kexp[:, 0, 4 * (n % 2):4 * (n % 2) + 4, :],
                                     start=False, stop=True)

                yield from L.self_att.on_tensor(pe, i, self_scores, lambda n, h: L.vaug2[:, :])

            with pe.Fori(0, B // LANES) as i:
                in_turns([lane_program(i, L) for L in lanes])

        @block.scalar
        def _(act):
            for k, bank in enumerate((lanes[0].Mb, lanes[1].Mb)):
                act.wait_ge(s["w8T_ps"], k + 1)
                act.activation(w8T[:, k], half(bank[:, 0:2 * D]), ACT.Copy).then_inc(s["w8T_ready"], 1)
            act.wait_ge(s["wstep_ps"], 1)
            act.activation(wstep_row[:, :, :], lanes[0].S[:, :].rearrange("p (k n) -> p k n", k=2), ACT.Copy).then_inc(s["wstep_ready"], 1)

            def lane_program(i, L):
                act.wait_ge(L.cT_ps, i + 1)
                act.activation(L.cT[:, :, :], half(L.M[:, 0:D]), ACT.Copy).then_inc(L.cT_ready, 1)
                yield
                act.wait_ge(L.kv_ps, i + 1)
                act.activation(L.vaug[:, :, 0:HD], L.T[:, 0:D].rearrange("p (h d) -> p h d", h=H), ACT.Copy).then_inc(L.v_ready, 1)

                def copy8(n):
                    act.wait_ge(L.x8T_ps, at(i, 2, n + 1))
                    act.activation(L.x8T[:, n], half(L.Mb[:, 0:D]), ACT.Copy).then_inc(L.x8T_ready, 1)

                yield
                copy8(0)
                yield
                act.wait_ge(L.qT_ps, i + 1)
                act.activation(L.qT[:, :, :], half(L.M[:, 0:D]), ACT.Copy, scale=0.25).then_inc(L.qT_ready, 1)
                yield
                yield from L.cross_att.on_scalar(act, i)
                yield
                copy8(1)
                yield
                yield from L.ln1.on_scalar(act, i)
                yield
                act.wait_ge(L.x5T_ps, i + 1)
                act.activation(L.x5T[:, :, :], half(L.M[:, 0:D]), ACT.Copy).then_inc(L.x5T_ready, 1)
                yield
                act.wait_ge(L.top_step, at(i, TOP, 2))
                act.activation(L.prob[:, 0, :], L.prob[:, 0, :], ACT.Exp).then_inc(L.exp_ready, 1)
                yield
                act.wait_ge(L.qkv_ps, i + 1)
                act.activation(L.qT2[:, :, :], half(L.T[:, 0:D]), ACT.Copy, scale=0.25).then_inc(L.qT2_ready, 1)
                yield
                act.wait_ge(L.krepT_ps, i + 1)
                act.activation(L.krepT[:, :], L.M[:, 0:P], ACT.Copy).then_inc(L.krepT_ready, 1)
                yield
                yield from L.self_att.on_scalar(act, i)
                yield
                yield from L.ln2.on_scalar(act, i)

            with act.Fori(0, B // LANES) as i:
                in_turns([lane_program(i, L) for L in lanes])

        @block.vector
        def _(dve):
            dve.wait_ge(s["weights"], 16 * len(shapes))
            dve.wait_ge(s["consts"], 1)
            for k, name in enumerate(("wq8", "wo8")):
                for c in range(DC):
                    wquant.on_vector(dve, 0, 2 * k + c, w[name][:, c, :], w8[:, k, c, :], wstep[:, k, c:c + 1])
            dve.wait_ge(s["wstep_ready"], 1)

            def lane_program(i, L):
                def scale8(n):
                    dve.tensor_scalar(L.y8[:, 0, :], wstep_row[:, n, :], L.xstep[:, n:n + 1], None, ALU.mult).then_inc(L.y8_step, 1)
                    dve.wait_ge(L.y8_step, at(i, 4, 2 * n + 1))
                    dve.wait_ge(L.y8_ps, at(i, 2, n + 1))
                    dve.tensor_tensor(L.y8[:, 1, :], L.y8[:, 0, :], L.M[:, D:2 * D], ALU.mult).then_inc(L.y8_step, 1)
                    dve.wait_ge(L.y8_step, at(i, 4, 2 * n + 2))
                    dve.tensor_tensor(L.yb[:, n, :], L.y8[:, 1, :], w["bqo"][:, n, :], ALU.add).then_inc(L.yb_ready, 1)

                dve.wait_ge(L.x_loaded, at(i, 16, 16))
                L.xquant.on_vector(dve, i, 0, L.xt[:, :], L.x8[:, 0, :], L.xstep[:, 0:1])
                yield
                dve.wait_ge(L.kv_ps, i + 1)
                for c in range(DC):
                    dve.tensor_scalar(L.kT[:, c, :], L.S[:, c * P:(c + 1) * P], w["bk"][:, c:c + 1], None, ALU.add).then_inc(L.kT_ready, 1)
                yield
                scale8(0)
                yield
                yield from L.cross_att.on_vector(dve, i)
                dve.wait_ge(L.cross_att.o_done, at(i, QUADS, QUADS))
                L.xquant.on_vector(dve, i, 1, L.osb[:, :, :].rearrange("p h d -> p (h d)"), L.x8[:, 1, :], L.xstep[:, 1:2])
                yield
                scale8(1)
                yield
                dve.wait_ge(L.yb_ready, at(i, 2, 2))
                yield from L.ln1.on_vector(dve, i, L.x5[:, :], L.xt[:, :], L.yb[:, 1, :])
                link = Linked(dve, L.top_step, TOP, i)
                yield
                dve.wait_ge(L.logits_ps, i + 1)
                logits = L.M[:, D:D + H]
                link(dve.tensor_reduce(L.col[:, 0:1], logits, AX.X, ALU.max))
                link(dve.tensor_scalar(L.prob[:, 0, :], logits, L.col[:, 0:1], None, ALU.subtract))
                yield
                dve.wait_ge(L.exp_ready, i + 1)
                link(dve.tensor_reduce(L.col[:, 1:2], L.prob[:, 0, :], AX.X, ALU.add))
                link(dve.reciprocal(L.col[:, 2:3], L.col[:, 1:2]))
                link(dve.tensor_scalar(L.prob[:, 1, :], L.prob[:, 0, :], L.col[:, 2:3], None, ALU.mult))
                link(dve.tensor_reduce(L.col[:, 3:4], L.prob[:, 1, :], AX.X, ALU.max))
                link(dve.tensor_scalar(L.prob[:, 2, :], L.prob[:, 1, :], L.col[:, 3:4], -float(H), ALU.is_equal, ALU.mult))
                link(dve.tensor_tensor(L.prob[:, 3, :], L.prob[:, 2, :], head_id[:, 1, :], ALU.add))
                link(dve.tensor_reduce(L.col[:, 4:5], L.prob[:, 3, :], AX.X, ALU.min))
                link(dve.tensor_scalar(L.prob[:, 4, :], head_id[:, 0, :], L.col[:, 4:5], None, ALU.is_equal))
                link.close()
                yield
                dve.wait_ge(L.qkv_ps, i + 1)
                kvp = L.O[:, :].rearrange("p (a h d) -> p a h d", a=2, h=H)
                for a in range(2):
                    dve.tensor_tensor(L.kv[:, a], kvp[:, a], along(L.prob[:, 4, :], HD), ALU.mult).then_inc(L.best_step, 1)
                for a in range(2):
                    dve.wait_ge(L.best_step, at(i, 4, a + 1))
                    dve.tensor_reduce(L.best[:, a, :], L.kv[:, a].rearrange("p h d -> p d h"), AX.X, ALU.add).then_inc(L.best_step, 1)
                dve.wait_ge(L.best_step, at(i, 4, 4))
                dve.tensor_copy(L.krep[:, :, :], spread(L.best[:, 0, :], 8)).then_inc(L.krep_ready, 1)
                dve.tensor_scalar(L.vaug2[:, 0:HD], L.best[:, 1, :], L.col[:, 3:4], None, ALU.mult).then_inc(L.vaug2_ready, 1)
                yield
                yield from L.self_att.on_vector(dve, i)
                dve.wait_ge(L.self_att.o_done, at(i, QUADS, QUADS))
                dve.wait_ge(L.xo_free, i + 1)
                yield from L.ln2.on_vector(dve, i, L.xo[:, :], L.x5[:, :], L.osb2[:, :, :].rearrange("p h d -> p (h d)"))

            with dve.Fori(0, B // LANES) as i:
                in_turns([lane_program(i, L) for L in lanes])


def layout_layer1_attention(inp):
    by_chunk = lambda a: a.reshape(DC, P, -1).transpose(1, 0, 2)
    bqo = np.broadcast_to(np.stack([inp["L1_xattn_bq"], inp["L1_xattn_bo"]])[None], (P, 2, D))
    return dict(ctx=inp["ctx_2048"], mask=inp["mask_BxSxS2_ff0"], wq8=by_chunk(inp["L1_xattn_wq"]), wo8=by_chunk(inp["L1_xattn_wo"]),
                wk=by_chunk(inp["L1_xattn_wk"].T), wv=by_chunk(inp["L1_xattn_wv"].T), bk=inp["L1_xattn_bk"].reshape(DC, P).T,
                bv=inp["L1_xattn_bv"].reshape(1, D), bqo=bqo, wtop=by_chunk(inp["L1_ffn_W_gate"].T),
                wqkv=by_chunk(inp["L1_ffn_W_qkv"].T))


PHASES = (("a", layout_layer0_attention, layer0_attention), ("b", layout_layer0_experts, layer0_experts),
          ("c", layout_layer1_delta_rule, layer1_delta_rule), ("d", layout_layer1_attention, layer1_attention))


def decoder(nc, x, weights, out):
    src = x
    for n, (tag, _, build) in enumerate(PHASES):
        last = n == len(PHASES) - 1
        dst = out if last else nc.dram_tensor(f"x_after_{tag}", (B, S, D), F32, kind="Internal").ap()
        sems = []
        build(nc, sems, weights[tag], src, dst)
        if not last:
            nc.all_engine_barrier()
            nc.clear_and_free_semaphores(sems)
            nc.all_engine_barrier()
        src = dst


def kernel(**inputs):
    import concourse.bacc as bacc
    from concourse.bass_utils import run_bass_kernel_spmd

    inputs = {k: np.asarray(v) for k, v in inputs.items()}
    nc = bacc.Bacc("TRN2", target_bir_lowering=False, num_devices=1)
    arrays = {"x": np.ascontiguousarray(inputs["x"])}
    handles = {"x": nc.dram_tensor("x", arrays["x"].shape, F32, kind="ExternalInput").ap()}
    weights = {}
    for tag, layout, _ in PHASES:
        weights[tag] = {}
        for name, a in layout(inputs).items():
            full = f"{tag}_in_{name}"
            arrays[full] = np.ascontiguousarray(a)
            weights[tag][name] = nc.dram_tensor(full, a.shape, mybir.dt.from_np(a.dtype), kind="ExternalInput").ap()
    out = nc.dram_tensor("out", (B, S, D), F32, kind="ExternalOutput").ap()
    decoder(nc, handles["x"], weights, out)
    return run_bass_kernel_spmd(nc, [arrays], core_ids=[0]).results[0]["out"]
```

```python
from contextlib import ExitStack

import numpy as np

import concourse.bass as bass
from concourse import mybir

F32 = mybir.dt.float32
BF16 = mybir.dt.bfloat16
I32 = mybir.dt.int32
ALU = mybir.AluOpType
ACT = mybir.ActivationFunctionType
AX = mybir.AxisListType

B, S, D = 8, 128, 256
P = 128
DC = D // P
H = 16
QUADS = H // 4
HD = D // H
MASKED = -1e30
LN_EPS = 1e-5


def at(i, per, n):
    return i * per + n


class Linked:

    def __init__(self, eng, sem, per=0, i=0):
        self.eng, self.sem, self.per, self.i, self.n = eng, sem, per, i, 0

    def __call__(self, *together):
        for ins in together:
            ins.then_inc(self.sem, 1)
            self.n += 1
        self.eng.wait_ge(self.sem, at(self.i, self.per, self.n))

    def close(self):
        assert self.n == self.per, self.n


LANES = 2


class Phase:

    def __init__(self, nc, tag, ctx, sems):
        self.nc, self.tag, self.ctx, self.sems = nc, tag, ctx, sems

    def sb(self, name, shape, dt=F32):
        return self.ctx.enter_context(self.nc.sbuf_tensor(f"{self.tag}_{name}", shape, dt))

    def bank(self, name, dt=F32):
        return self.ctx.enter_context(self.nc.psum_tensor(f"{self.tag}_{name}", [P, 2048 // mybir.dt.size(dt)], dt))

    def sem(self, name):
        self.sems.append(self.nc.alloc_semaphore(name=f"{self.tag}_{name}"))
        return self.sems[-1]


def four(ap):
    return ap.rearrange("p (h n) -> p h n", h=4)


def spread(ap, n):
    return ap.unsqueeze(1).broadcast_to([ap.shape[0], n, ap.shape[1]])


def along(ap, n):
    return ap.unsqueeze(2).broadcast_to([ap.shape[0], ap.shape[1], n])


def batch(t, b):
    return t[bass.ds(b, 1)].rearrange("a p c -> p (a c)")


def store_batch(sp, i, b, ready, out, dst, stored, free):
    sp.wait_ge(ready, at(i, 1, 1))
    sp.dma_start(batch(dst, b), out).then_inc(stored, 16)
    sp.wait_ge(stored, at(i, 16, 16))
    sp.sem_inc(free, 1)


def in_turns(programs):
    done = object()
    running = list(programs)
    while running:
        running = [p for p in running if next(p, done) is not done]


def fill_identity(pool, link, tile):
    link(pool.memset(tile, 0.0))
    link(pool.affine_select(out=tile, in_=tile, compare_op=ALU.not_equal, fill=1.0, base=0,
                            pattern=[[-1, P]], channel_multiplier=1))


class Attention:

    def __init__(self, ph, name, width, banks, pbuf, ptbuf, stats, out, ident):
        self.width, self.out, self.ident = width, out, ident
        self.S, self.PT, self.O = banks
        self.p, self.pt, self.stats = pbuf, ptbuf, stats
        self.scores_ready = ph.sem(name + "_scores_ready")
        self.max_ready = ph.sem(name + "_max_ready")
        self.shifted = ph.sem(name + "_shifted")
        self.exp_ready = ph.sem(name + "_exp_ready")
        self.pt_ready = ph.sem(name + "_pt_ready")
        self.pt_copied = ph.sem(name + "_pt_copied")
        self.o_ready = ph.sem(name + "_o_ready")
        self.recip_ready = ph.sem(name + "_recip_ready")
        self.o_done = ph.sem(name + "_o_done")

    def on_tensor(self, pe, i, scores, values):
        w = self.width + 1
        for s in range(QUADS + 2):
            if s < QUADS:
                if s >= 1:
                    pe.wait_ge(self.shifted, at(i, QUADS, s))
                scores(s, self.S).then_inc(self.scores_ready, 1)
            if 1 <= s <= QUADS:
                n = s - 1
                pe.wait_ge(self.exp_ready, at(i, QUADS, n + 1))
                if n >= 1:
                    pe.wait_ge(self.pt_copied, at(i, QUADS, n))
                for h in range(4):
                    last = pe.transpose(self.PT[:, h * P:(h + 1) * P], self.p[:, n % 2, h, :], self.ident)
                last.then_inc(self.pt_ready, 1)
            if s >= 2:
                n = s - 2
                pe.wait_ge(self.pt_copied, at(i, QUADS, n + 1))
                if n >= 1:
                    pe.wait_ge(self.o_done, at(i, QUADS, n))
                for h in range(4):
                    last = pe.matmul(self.O[:, h * w:(h + 1) * w], self.pt[:, n % 2, h, :],
                                     values(n, h), start=True, stop=True)
                last.then_inc(self.o_ready, 1)
            yield

    def on_scalar(self, act, i):
        for s in range(QUADS + 1):
            if s >= 1:
                n = s - 1
                act.wait_ge(self.pt_ready, at(i, QUADS, n + 1))
                if n >= 2:
                    act.wait_ge(self.o_ready, at(i, QUADS, n - 1))
                act.activation(self.pt[:, n % 2], four(self.PT[:, :]), ACT.Copy).then_inc(self.pt_copied, 1)
            if s < QUADS:
                act.wait_ge(self.shifted, at(i, QUADS, s + 1))
                act.activation(self.p[:, s % 2], self.p[:, s % 2], ACT.Exp).then_inc(self.exp_ready, 1)
            yield

    def on_vector(self, dve, i):
        w = self.width + 1
        for s in range(QUADS + 2):
            if s < QUADS:
                dve.wait_ge(self.scores_ready, at(i, QUADS, s + 1))
                dve.tensor_reduce(self.stats[:, 4 * s:4 * s + 4], four(self.S[:, :]), AX.X, ALU.max)\
                   .then_inc(self.max_ready, 1)
                dve.wait_ge(self.max_ready, at(i, QUADS, s + 1))
                if s >= 2:
                    dve.wait_ge(self.pt_ready, at(i, QUADS, s - 1))
                dve.tensor_tensor(self.p[:, s % 2], four(self.S[:, :]), along(self.stats[:, 4 * s:4 * s + 4], P),
                                  ALU.subtract).then_inc(self.shifted, 1)
            if s >= 2:
                n = s - 2
                dve.wait_ge(self.o_ready, at(i, QUADS, n + 1))
                o = self.O[:, 0:4 * w].rearrange("p (h w) -> p h w", h=4)
                dve.reciprocal(self.stats[:, 16 + 4 * n:20 + 4 * n].unsqueeze(2), o[:, :, self.width:w]).then_inc(self.recip_ready, 1)
                dve.wait_ge(self.recip_ready, at(i, QUADS, n + 1))
                dve.tensor_tensor(self.out[:, 4 * n:4 * n + 4, :], o[:, :, 0:self.width],
                                  along(self.stats[:, 16 + 4 * n:20 + 4 * n], self.width), ALU.mult).then_inc(self.o_done, 1)
            yield


class LayerNorm:

    DVE_STEPS = 9

    def __init__(self, ph, name):
        self.r = ph.sb(name + "_sum", [P, D])
        self.st = ph.sb(name + "_stats", [P, 6])
        self.c = ph.sb(name + "_cols", [P, 8])
        self.rstd = ph.sb(name + "_rstd", [P, 3])
        self.step = ph.sem(name + "_step")
        self.root_ready = ph.sem(name + "_root_ready")
        self.rstd_ready = ph.sem(name + "_rstd_ready")
        self.done = ph.sem(name + "_done")

    def on_vector(self, dve, i, out, x, y):
        link = Linked(dve, self.step, self.DVE_STEPS, i)
        col = lambda n: self.c[:, n:n + 1]
        link(dve.tensor_tensor(self.r[:, :], x, y, ALU.add))
        link(dve.bn_stats(self.st[:, :], self.r[:, :]))
        link(dve.tensor_tensor(col(0), self.st[:, 1:2], self.st[:, 4:5], ALU.subtract),
             dve.tensor_tensor(col(1), self.st[:, 1:2], self.st[:, 4:5], ALU.add),
             dve.tensor_tensor(col(2), self.st[:, 2:3], self.st[:, 5:6], ALU.add))
        link(dve.scalar_tensor_tensor(col(3), col(0), 0.25, col(0), ALU.mult, ALU.mult),
             dve.tensor_scalar(col(4), col(2), 1.0 / D, LN_EPS, ALU.mult, ALU.add),
             dve.tensor_scalar(col(5), col(1), 0.5, None, ALU.mult))
        link(dve.tensor_tensor(self.rstd[:, 0:1], col(3), col(4), ALU.add))
        link.close()
        yield
        dve.wait_ge(self.root_ready, at(i, 1, 1))
        dve.reciprocal(self.rstd[:, 2:3], self.rstd[:, 1:2]).then_inc(self.rstd_ready, 1)
        dve.wait_ge(self.rstd_ready, at(i, 1, 1))
        dve.tensor_scalar(out, self.r[:, :], col(5), self.rstd[:, 2:3], ALU.subtract, ALU.mult).then_inc(self.done, 1)

    def on_scalar(self, act, i):
        act.wait_ge(self.step, at(i, self.DVE_STEPS, self.DVE_STEPS))
        act.activation(self.rstd[:, 1:2], self.rstd[:, 0:1], ACT.Sqrt).then_inc(self.root_ready, 1)


KV = 4
LAT, QLAT, ROPE, XHD = 64, 96, 64, 128
LOOKBACK = 8
PAIRS = H // 2


class Layer0Lane:

    def __init__(self, nc, ctx, sems, n, ident):
        self.n = n
        ph = Phase(nc, f"a{n}", ctx, sems)
        sb = ph.sb
        self.xt = sb("xt", [P, D])
        self.ct = sb("ct", [P, D])
        self.xcT = sb("xcT", [P, 4, P])
        self.t1 = sb("t1", [P, 4, P])
        self.t2 = sb("t2", [P, 4, P])
        self.qk = sb("qk", [P, 4, P])
        self.kexp = sb("kexp", [P, DC, 8, P])
        self.vaug = sb("vaug", [P, KV, HD + 1])
        self.kvT = sb("kvT", [P, P])
        self.kvaug = sb("kvaug", [P, LAT + 1])
        self.seg = sb("seg", [P, 1])
        self.near = sb("near", [P, 2, P])
        self.key = sb("key", [P, 2, P])
        self.Q = sb("Q", [P, PAIRS, 2, P])
        self.pbuf = sb("pbuf", [P, 2, 4, P])
        self.ptbuf = sb("ptbuf", [P, 2, 4, P])
        self.stats = sb("stats", [P, 32])
        self.osb = sb("osb", [P, H, HD])
        self.oT = sb("oT", [P, DC, P])
        self.x1 = sb("x1", [P, D])
        self.x1T = sb("x1T", [P, DC, P])
        self.qcT = sb("qcT", [QLAT, P])
        self.lat = sb("lat", [P, H, LAT])
        self.latT = sb("latT", [P, PAIRS, P])
        self.x2 = sb("x2", [P, D])
        self.segb = sb("segb", [P, P], BF16)
        self.M, self.S, self.T, self.O = (ph.bank(k) for k in "MSTO")
        self.ln1, self.ln2 = LayerNorm(ph, "ln1"), LayerNorm(ph, "ln2")
        banks = (self.S, self.T, self.O)
        self.self_att = Attention(ph, "self", HD, banks, self.pbuf, self.ptbuf, self.stats, self.osb, ident)
        self.cross_att = Attention(ph, "cross", LAT, banks, self.pbuf, self.ptbuf, self.stats, self.lat, ident)
        self.x_loaded, self.ctx_loaded, self.x2_stored, self.x2_free = (
            ph.sem(k) for k in "x_loaded ctx_loaded x2_stored x2_free".split())
        self.xcT_ps, self.xcT_ready, self.v_ps, self.v_ready = (
            ph.sem(k) for k in "xcT_ps xcT_ready v_ps v_ready".split())
        self.qk_ps, self.rope_step, self.qk_ready, self.kexp_ready = (
            ph.sem(k) for k in "qk_ps rope_step qk_ready kexp_ready".split())
        self.kr_ps, self.kr_ready, self.seg_step, self.oT_ps = (
            ph.sem(k) for k in "kr_ps kr_ready seg_step oT_ps".split())
        self.oT_ready, self.y1_ps, self.x1T_ps, self.x1T_ready = (
            ph.sem(k) for k in "oT_ready y1_ps x1T_ps x1T_ready".split())
        self.qc_ps, self.qc_ready, self.Q_ps, self.Qa_ready = (
            ph.sem(k) for k in "qc_ps qc_ready Q_ps Qa_ready".split())
        self.Qr_ready, self.latT_ps, self.latT_ready, self.y2_ps = (
            ph.sem(k) for k in "Qr_ready latT_ps latT_ready y2_ps".split())


def layer0_attention(nc, sems, d, x_src, x_dst):
    ctx = ExitStack()
    with ctx:
        ph = Phase(nc, "a", ctx, sems)
        sb, sem = ph.sb, ph.sem
        shapes = dict(wqk=[P, 2, DC, 4, P], wv=[P, DC, KV * HD], wo=[P, DC, D], bo=[1, D], rope=[P, 2, P],
                      wkvc2=[P, DC, 2 * LAT], wdq=[P, DC, QLAT], wuq=[P, H, QLAT], wuk=[P, H, LAT],
                      wqr=[QLAT, 2, PAIRS, P], wkr2=[LAT, 2, 2 * ROPE], wuv=[P, H, LAT], wxo=[P, H, D],
                      xrope=[P, 4, P], itok=[P, B])
        w = {k: sb(k, s, I32 if k == "itok" else F32) for k, s in shapes.items()}
        ident = sb("ident", [P, P])
        identb = sb("identb", [P, P], BF16)
        causal = sb("causal", [P, P])
        causalb = sb("causalb", [P, P], BF16)
        own_block = sb("own_block", [P, 8])
        key_id = sb("key_id", [P, 2, P])
        ones = sb("ones", [1, P])
        wabs = sb("wabs", [QLAT, PAIRS, P])
        wuvo = sb("wuvo", [P, PAIRS, D])
        factors = ("wuq", "wuk", "wuv", "wxo")
        factors_loaded, weights = sem("factors_loaded"), sem("weights")
        pool_step, consts = sem("pool_step"), sem("consts")
        products_ready, products_copied = sem("products_ready"), sem("products_copied")

        lanes = [Layer0Lane(nc, ctx, sems, n, ident[:, :]) for n in range(LANES)]
        xscale = float(np.float32(1.0) / np.sqrt(np.float32(XHD + ROPE)))
        block = ctx.enter_context(nc.Block())

        @block.sync
        def _(sp):
            for k in factors:
                sp.dma_start(w[k][:], d[k]).then_inc(factors_loaded, 16)
            for k in shapes:
                if k not in factors:
                    sp.dma_start(w[k][:], d[k]).then_inc(weights, 16)
            for L in lanes:
                sp.dma_start(L.xt[:, :], batch(x_src, L.n)).then_inc(L.x_loaded, 16)
                sp.dma_start(L.ct[:, :], batch(d["ctx"], L.n)).then_inc(L.ctx_loaded, 16)
                sp.sem_inc(L.x2_free, 1)
            with sp.Fori(0, B // LANES - 1) as i:
                for L in lanes:
                    sp.wait_ge(L.xcT_ps, i + 1)
                    sp.dma_start(L.ct[:, :], batch(d["ctx"], (i + 1) * LANES + L.n)).then_inc(L.ctx_loaded, 16)
                for L in lanes:
                    sp.wait_ge(L.ln1.step, at(i, L.ln1.DVE_STEPS, 1))
                    sp.dma_start(L.xt[:, :], batch(x_src, (i + 1) * LANES + L.n)).then_inc(L.x_loaded, 16)
                for L in lanes:
                    store_batch(sp, i, i * LANES + L.n, L.ln2.done, L.x2[:, :], x_dst, L.x2_stored, L.x2_free)
            for L in lanes:
                store_batch(sp, B // LANES - 1, B - LANES + L.n, L.ln2.done, L.x2[:, :], x_dst, L.x2_stored, L.x2_free)

        @block.gpsimd
        def _(pool):
            link = Linked(pool, pool_step)
            fill_identity(pool, link, ident[:, :])
            link(pool.tensor_copy(identb[:, :], ident[:, :]))
            link(pool.memset(causal[:, :], 0.0))
            link(pool.affine_select(out=causal[:, :], in_=causal[:, :], compare_op=ALU.is_ge, fill=MASKED,
                                    base=0, pattern=[[-1, P]], channel_multiplier=1))
            link(pool.tensor_copy(causalb[:, :], causal[:, :]))
            link(pool.memset(own_block[:, :], 1.0))
            link(pool.affine_select(out=own_block[:, :], in_=own_block[:, :], compare_op=ALU.is_ge, fill=0.0,
                                    base=0, pattern=[[-HD, 8]], channel_multiplier=1))
            link(pool.affine_select(out=own_block[:, :], in_=own_block[:, :], compare_op=ALU.is_ge, fill=0.0,
                                    base=HD - 1, pattern=[[HD, 8]], channel_multiplier=-1))
            link(pool.iota(key_id[:, :, :], pattern=[[LOOKBACK, 2], [1, P]], base=0, channel_multiplier=0,
                           allow_small_or_imprecise_dtypes=True))
            link(pool.memset(ones[:, :], 1.0))
            for L in lanes:
                link(pool.memset(L.vaug[:, :, :], 1.0))
                link(pool.memset(L.kvaug[:, :], 1.0))
            pool.sem_inc(consts, 1)
            with pool.Fori(0, B // LANES) as i:
                for c in range(DC):
                    for L in lanes:
                        if c == 0:
                            pool.wait_ge(L.qk_ready, i + 1)
                        pool.tensor_tensor(L.kexp[:, c], spread(L.qk[:, 2 + c, :], 8), along(own_block[:, :], P), ALU.mult)\
                            .then_inc(L.kexp_ready, 1)

        @block.tensor
        def _(pe):
            pe.wait_ge(factors_loaded, 16 * len(factors))
            for h in range(H):
                bank, at0 = (lanes[0].M, lanes[1].M)[h // 8], (h % 8) * LAT
                pe.matmul(bank[0:QLAT, at0:at0 + LAT], w["wuq"][:, h, :], w["wuk"][:, h, :], start=True, stop=True)
            for h in range(H):
                bank, row, col = (lanes[0].S, lanes[1].S, lanes[0].T, lanes[1].T)[h // 4], LAT * (h % 2), (h // 2 % 2) * D
                last = pe.matmul(bank[row:row + LAT, col:col + D], w["wuv"][:, h, :], w["wxo"][:, h, :],
                                 start=True, stop=True)
            last.then_inc(products_ready, 1)
            pe.wait_ge(weights, 16 * (len(shapes) - len(factors)))
            pe.wait_ge(consts, 1)
            pe.wait_ge(products_copied, 6)

            def start_batch(i, L):
                pe.wait_ge(L.x_loaded, at(i, 16, 16))
                pe.wait_ge(L.ctx_loaded, at(i, 16, 16))
                for c in range(DC):
                    pe.transpose(L.M[:, c * P:(c + 1) * P], L.xt[:, c * P:(c + 1) * P], ident[:, :])
                for c in range(DC):
                    last = pe.transpose(L.M[:, (2 + c) * P:(3 + c) * P], L.ct[:, c * P:(c + 1) * P], ident[:, :])
                last.then_inc(L.xcT_ps, 1)
                yield
                pe.wait_ge(L.xcT_ready, i + 1)
                for c in range(DC):
                    pe.matmul(L.O[:, 0:KV * HD], L.xcT[:, c, :], w["wv"][:, c, :], start=c == 0, stop=c == DC - 1)
                for c in range(DC):
                    pe.matmul(L.O[:, 64:192], w["wkvc2"][:, c, :], L.xcT[:, 2 + c, :], start=c == 0, stop=c == DC - 1)
                for c in range(DC):
                    last = pe.matmul(L.O[:, 192:256], L.xcT[:, 2 + c, :], w["wkvc2"][:, c, 0:LAT],
                                     start=c == 0, stop=c == DC - 1)
                last.then_inc(L.v_ps, 1)
                for r, bank in enumerate((L.M, L.S)):
                    for n in range(4):
                        for c in range(DC):
                            last = pe.matmul(bank[:, n * P:(n + 1) * P], w["wqk"][:, r, c, n, :], L.xcT[:, c, :],
                                             start=c == 0, stop=c == DC - 1)
                last.then_inc(L.qk_ps, 1)
                yield
                pe.wait_ge(L.v_ready, at(i, 5, 5))
                for r in range(2):
                    last = pe.matmul(L.O[:, r * P:(r + 1) * P], w["wkr2"][:, r, :], L.kvT[0:LAT, :], start=True, stop=True)
                last.then_inc(L.kr_ps, 1)
                yield

            def lane_program(i, L, more):
                pe.wait_ge(L.kr_ready, at(i, 2, 2))
                mask4 = spread(causalb[:, :], 4)

                def self_scores(n, bank):
                    if n % 2 == 0:
                        pe.wait_ge(L.kexp_ready, at(i, 2, n // 2 + 1))
                    pe.matmul(four(bank[:, :]), identb[:, :], mask4, start=True, stop=False)
                    return pe.matmul(four(bank[:, :]), L.qk[:, n // 2, :], L.kexp[:, n // 2, 4 * (n % 2):4 * (n % 2) + 4, :],
                                     start=False, stop=True)

                yield from L.self_att.on_tensor(pe, i, self_scores, lambda n, h: L.vaug[:, n, :])
                pe.wait_ge(L.self_att.o_done, at(i, QUADS, QUADS))
                for c in range(DC):
                    last = pe.transpose(L.M[:, c * P:(c + 1) * P], L.osb[:, 8 * c:8 * c + 8, :].rearrange("p h d -> p (h d)"),
                                        ident[:, :])
                last.then_inc(L.oT_ps, 1)
                yield
                pe.wait_ge(L.oT_ready, i + 1)
                pe.matmul(L.M[:, D:2 * D], ones[:, :], w["bo"][:, :], start=True, stop=False)
                for c in range(DC):
                    last = pe.matmul(L.M[:, D:2 * D], L.oT[:, c, :], w["wo"][:, c, :], start=False, stop=c == DC - 1)
                last.then_inc(L.y1_ps, 1)
                yield
                yield
                pe.wait_ge(L.ln1.done, i + 1)
                for c in range(DC):
                    last = pe.transpose(L.M[:, c * P:(c + 1) * P], L.x1[:, c * P:(c + 1) * P], ident[:, :])
                last.then_inc(L.x1T_ps, 1)
                yield
                pe.wait_ge(L.x1T_ready, i + 1)
                for c in range(DC):
                    last = pe.matmul(L.M[0:QLAT, 2 * P:3 * P], w["wdq"][:, c, :], L.x1T[:, c, :], start=c == 0, stop=c == DC - 1)
                last.then_inc(L.qc_ps, 1)
                yield
                pe.wait_ge(L.qc_ready, i + 1)
                for half in range(2):
                    if half:
                        pe.wait_ge(L.Qa_ready, at(i, 4, 2))
                        pe.wait_ge(L.Qr_ready, at(i, 4, 2))
                    for bank, wt in zip((L.M, L.S, L.T), (wabs[:, :, :], w["wqr"][:, 0], w["wqr"][:, 1])):
                        for n in range(4):
                            last = pe.matmul(bank[:, n * P:(n + 1) * P], wt[:, 4 * half + n, :], L.qcT[:, :],
                                             start=True, stop=True)
                    last.then_inc(L.Q_ps, 1)
                    yield
                pe.wait_ge(L.seg_step, at(i, 4, 4))
                seg4 = spread(L.segb[:, :], 4)

                def cross_scores(n, bank):
                    if n % 2 == 0:
                        pe.wait_ge(L.Qa_ready, at(i, 4, 4))
                        pe.wait_ge(L.Qr_ready, at(i, 4, 4))
                    pe.matmul(four(bank[:, :]), identb[:, :], seg4, start=True, stop=False)
                    for h in range(4):
                        last = pe.matmul(bank[:, h * P:(h + 1) * P], L.Q[:, (4 * n + h) // 2, h % 2, :], L.key[:, h % 2, :],
                                         start=False, stop=h == 3)
                    return last

                yield from L.cross_att.on_tensor(pe, i, cross_scores, lambda n, h: L.kvaug[:, :])
                pe.wait_ge(L.cross_att.o_done, at(i, QUADS, QUADS))
                for half, bank in enumerate((L.M, L.S)):
                    for n in range(4):
                        pair = 4 * half + n
                        last = pe.transpose(bank[:, n * P:(n + 1) * P],
                                            L.lat[:, 2 * pair:2 * pair + 2, :].rearrange("p h d -> p (h d)"), ident[:, :])
                    last.then_inc(L.latT_ps, 1)
                yield
                for pair in range(PAIRS):
                    if pair % 4 == 0:
                        pe.wait_ge(L.latT_ready, at(i, 2, pair // 4 + 1))
                    last = pe.matmul(L.T[:, 0:D], L.latT[:, pair, :], wuvo[:, pair, :], start=pair == 0, stop=pair == PAIRS - 1)
                last.then_inc(L.y2_ps, 1)
                yield
                if more:
                    yield from start_batch(i + 1, L)

            in_turns([start_batch(0, L) for L in lanes])
            with pe.Fori(0, B // LANES - 1) as i:
                in_turns([lane_program(i, L, True) for L in lanes])
            in_turns([lane_program(B // LANES - 1, L, False) for L in lanes])

        @block.scalar
        def _(act):
            act.wait_ge(products_ready, 1)
            for k, bank in enumerate((lanes[0].M, lanes[1].M)):
                act.activation(wabs[:, 4 * k:4 * k + 4, :], four(bank[0:QLAT, :]), ACT.Copy).then_inc(products_copied, 1)
            for k, bank in enumerate((lanes[0].S, lanes[1].S, lanes[0].T, lanes[1].T)):
                act.activation(wuvo[:, 2 * k:2 * k + 2, :], bank[:, :].rearrange("p (a n) -> p a n", a=2), ACT.Copy)\
                   .then_inc(products_copied, 1)

            def start_batch(i, L):
                act.wait_ge(L.xcT_ps, i + 1)
                act.activation(L.xcT[:, :, :], four(L.M[:, :]), ACT.Copy).then_inc(L.xcT_ready, 1)
                yield
                act.wait_ge(L.v_ps, i + 1)
                act.activation(L.vaug[:, :, 0:HD], L.O[:, 0:64].rearrange("p (g d) -> p g d", g=KV), ACT.Copy).then_inc(L.v_ready, 1)
                act.activation(L.kvT[:, :], L.O[:, 64:192], ACT.Copy).then_inc(L.v_ready, 1)
                for parity in range(2):
                    rows = slice(LAT * parity, LAT * parity + LAT)
                    act.activation(L.key[rows, parity, :], L.O[rows, 64:192], ACT.Copy).then_inc(L.v_ready, 1)
                act.activation(L.kvaug[:, 0:LAT], L.O[:, 192:256], ACT.Copy).then_inc(L.v_ready, 1)
                yield

            def lane_program(i, L, more):
                yield from L.self_att.on_scalar(act, i)
                act.wait_ge(L.oT_ps, i + 1)
                act.activation(L.oT[:, :, :], L.M[:, 0:D].rearrange("p (c n) -> p c n", c=DC), ACT.Copy).then_inc(L.oT_ready, 1)
                yield
                L.ln1.on_scalar(act, i)
                yield
                act.wait_ge(L.x1T_ps, i + 1)
                act.activation(L.x1T[:, :, :], L.M[:, 0:D].rearrange("p (c n) -> p c n", c=DC), ACT.Copy).then_inc(L.x1T_ready, 1)
                yield
                act.wait_ge(L.qc_ps, i + 1)
                act.activation(L.qcT[:, :], L.M[0:QLAT, 2 * P:3 * P], ACT.Copy).then_inc(L.qc_ready, 1)
                yield
                for half in range(2):
                    act.wait_ge(L.Q_ps, at(i, 2, half + 1))
                    for parity in range(2):
                        rows = slice(LAT * parity, LAT * parity + LAT)
                        act.activation(L.Q[rows, 4 * half:4 * half + 4, parity, :], four(L.M[rows, :]), ACT.Copy,
                                       scale=xscale).then_inc(L.Qa_ready, 1)
                    yield
                yield
                yield from L.cross_att.on_scalar(act, i)
                for half, bank in enumerate((L.M, L.S)):
                    act.wait_ge(L.latT_ps, at(i, 2, half + 1))
                    act.activation(L.latT[:, 4 * half:4 * half + 4, :], four(bank[:, :]), ACT.Copy).then_inc(L.latT_ready, 1)
                yield
                if not more:
                    L.ln2.on_scalar(act, i)
                    return
                next_start = start_batch(i + 1, L)
                next(next_start)
                yield
                L.ln2.on_scalar(act, i)
                yield from next_start

            in_turns([start_batch(0, L) for L in lanes])
            with act.Fori(0, B // LANES - 1) as i:
                in_turns([lane_program(i, L, True) for L in lanes])
            in_turns([lane_program(B // LANES - 1, L, False) for L in lanes])

        @block.vector
        def _(dve):
            dve.wait_ge(weights, 16 * (len(shapes) - len(factors)))
            dve.wait_ge(consts, 1)

            ALL = slice(0, P)
            OTHER = (slice(LAT, P), slice(0, LAT))

            def rotate(L, link, done, out, plain, swapped, cos, sin, n):
                link(dve.tensor_tensor(L.t1[:, 0:n, :], plain, spread(cos, n), ALU.mult))
                link(dve.tensor_tensor(L.t2[:, 0:n, :], swapped, spread(sin, n), ALU.mult))
                for rows, part in out:
                    dve.tensor_tensor(part, L.t1[rows, 0:n, :], L.t2[rows, 0:n, :], ALU.add).then_inc(done, 1)


            def start_batch(i, L):
                link = Linked(dve, L.seg_step, 4, i)
                link(dve.tensor_copy(L.seg[:, :], w["itok"][:, bass.ds(i * LANES + L.n, 1)]))
                link(dve.tensor_scalar(L.near[:, 0, :], key_id[:, 0, :], L.seg[:, :], MASKED, ALU.is_gt, ALU.mult))
                link(dve.tensor_scalar(L.near[:, 1, :], key_id[:, 1, :], L.seg[:, :], MASKED, ALU.is_lt, ALU.mult))
                link(dve.tensor_tensor(L.segb[:, :], L.near[:, 0, :], L.near[:, 1, :], ALU.add))
                link.close()
                link = Linked(dve, L.rope_step, 8, i)
                dve.wait_ge(L.qk_ps, i + 1)
                rotate(L, link, L.qk_ready, [(ALL, L.qk[:, :, :])], four(L.M[:, :]), four(L.S[:, :]), w["rope"][:, 0, :], w["rope"][:, 1, :], 4)
                yield
                dve.wait_ge(L.kr_ps, i + 1)
                dve.wait_ge(L.qk_ready, i + 1)
                rotate(L, link, L.kr_ready, [(r, L.key[r, q, :].unsqueeze(1)) for q, r in enumerate(OTHER)], L.O[:, 0:P].unsqueeze(1), L.O[:, P:2 * P].unsqueeze(1),
                       w["xrope"][:, 0, :], w["xrope"][:, 1, :], 1)
                yield

            def lane_program(i, L, more):
                link = Linked(dve, L.rope_step, 8, i)
                link.n = 4
                yield from L.self_att.on_vector(dve, i)
                dve.wait_ge(L.y1_ps, i + 1)
                yield from L.ln1.on_vector(dve, i, L.x1[:, :], L.xt[:, :], L.M[:, D:2 * D])
                yield
                dve.wait_ge(L.kr_ready, at(i, 2, 2))
                for half in range(2):
                    dve.wait_ge(L.Q_ps, at(i, 2, half + 1))
                    if half:
                        dve.wait_ge(L.Qr_ready, at(i, 4, 2))
                    rotate(L, link, L.Qr_ready, [(r, L.Q[r, 4 * half:4 * half + 4, q, :]) for q, r in enumerate(OTHER)], four(L.S[:, :]), four(L.T[:, :]),
                           w["xrope"][:, 2, :], w["xrope"][:, 3, :], 4)
                    yield
                link.close()
                yield
                yield from L.cross_att.on_vector(dve, i)
                dve.wait_ge(L.y2_ps, i + 1)
                dve.wait_ge(L.x2_free, i + 1)
                yield from L.ln2.on_vector(dve, i, L.x2[:, :], L.x1[:, :], L.T[:, 0:D])
                if more:
                    yield from start_batch(i + 1, L)

            in_turns([start_batch(0, L) for L in lanes])
            with dve.Fori(0, B // LANES - 1) as i:
                in_turns([lane_program(i, L, True) for L in lanes])
            in_turns([lane_program(B // LANES - 1, L, False) for L in lanes])


def layout_layer0_attention(inp):
    f = np.float32
    by_chunk = lambda a: np.ascontiguousarray(a.reshape(DC, P, -1).transpose(1, 0, 2))
    half = HD // 2
    Wq = inp["L0_attn_Wq"].reshape(D, DC, P)
    Wk = inp["L0_attn_Wk"].reshape(D, DC, 2, HD).repeat(4, axis=2).reshape(D, DC, P)
    plain = np.concatenate([Wq, Wk], axis=1)
    swap = plain.reshape(D, 4, 8, 2, half)[:, :, :, ::-1].reshape(D, 4, P)
    wqk = np.stack([plain, swap]).reshape(2, DC, P, 4, P).transpose(2, 0, 1, 3, 4)
    inv = (1.0 / f(10000.0) ** (np.arange(0, HD, 2, dtype=f) / f(HD))).astype(f)
    ang = np.outer(np.arange(S, dtype=f), inv).astype(f)
    row = np.arange(P)
    sign = np.where(row % HD < half, -1, 1).astype(f)[:, None]
    root = f(0.5)
    rope = np.stack([root * np.cos(ang).T[row % half], root * sign * np.sin(ang).T[row % half]], axis=1)
    xh = ROPE // 2
    xinv = (1.0 / f(10000.0) ** (np.arange(xh, dtype=f) / f(xh))).astype(f)
    xang = (np.arange(S, dtype=f)[:, None] * xinv).astype(f)
    xsign = np.where(row % ROPE < xh, -1, 1).astype(f)[:, None]
    xc, xs = np.cos(xang).T[row % xh], xsign * np.sin(xang).T[row % xh]
    scale = f(1.0) / np.sqrt(f(XHD + ROPE))
    xrope = np.stack([xc, xs, xc * scale, xs * scale], axis=1)
    Wkvc = inp["L0_xattn_W_kvc"]
    Wqr = inp["L0_xattn_W_qr"].reshape(QLAT, PAIRS, 2, ROPE)[:, :, ::-1]
    Wqr_s = Wqr.reshape(QLAT, PAIRS, 2, 2, xh)[:, :, :, ::-1]
    Wkr = inp["L0_xattn_W_kr"]
    Wkr_s = Wkr.reshape(LAT, 2, xh)[:, ::-1].reshape(LAT, ROPE)
    head_d = lambda a, n: a.reshape(n, H, XHD).transpose(2, 1, 0)
    out = dict(
        ctx=inp["ctx_2048"], wqk=wqk, wv=by_chunk(inp["L0_attn_Wv"]), wo=by_chunk(inp["L0_attn_Wo"]),
        bo=inp["L0_attn_bo"].reshape(1, D), rope=rope, wkvc2=by_chunk(np.concatenate([Wkvc, Wkvc], axis=1)),
        wdq=by_chunk(inp["L0_xattn_W_dq"]), wuq=head_d(inp["L0_xattn_W_uq"], QLAT), wuk=head_d(inp["L0_xattn_W_uk"], LAT),
        wqr=np.stack([Wqr.reshape(QLAT, PAIRS, P), Wqr_s.reshape(QLAT, PAIRS, P)], axis=1),
        wkr2=np.stack([np.concatenate([a, a], axis=1) for a in (Wkr, Wkr_s)], axis=1),
        wuv=head_d(inp["L0_xattn_W_uv"], LAT), wxo=inp["L0_xattn_W_o"].reshape(H, XHD, D).transpose(1, 0, 2),
        xrope=xrope, itok=inp["itok_BxS_0_1023"].T)
    return out


EXPERTS, TOP, INNER = 16, 4, 176
ROUTED = EXPERTS * INNER // P
ECH = ROUTED + -(-2 * INNER // P)
GROUPS = (1, 4, 5, 5, 5, 5)
HALF = B // 2
TOKENS = HALF * S
PARTS = 3


def layer0_experts(nc, sems, d, x_src, x_dst):
    ctx = ExitStack()
    with ctx:
        ph = Phase(nc, "b", ctx, sems)
        sb, sem = ph.sb, ph.sem
        wgate = sb("wgate", [P, DC, EXPERTS])
        wup = sb("wup", [P, ECH, 2, DC, P])
        wdown = sb("wdown", [P, ECH, D])
        ident = sb("ident", [P, P])
        identb = sb("identb", [P, P], BF16)
        before = sb("before", [P, EXPERTS, EXPERTS])
        owner = sb("owner", [P, ROUTED * P], BF16)
        xt = sb("xt", [P, B, D])
        xT = sb("xT", [P, 2, DC, TOKENS])
        logits = sb("logits", [P, B, EXPERTS])
        col = sb("col", [P, 3, HALF])
        prob = sb("prob", [P, 2, HALF, EXPERTS])
        cmp_ = sb("cmp", [P, 2, HALF, EXPERTS, EXPERTS])
        rank = sb("rank", [P, HALF, EXPERTS])
        route = sb("route", [P, 2, HALF, EXPERTS])
        parts = sb("parts", [P, HALF, P // EXPERTS, EXPERTS], BF16)
        partsT = sb("partsT", [P, TOKENS], BF16)
        zeros = sb("zeros", [P, TOKENS], BF16)
        sg = sb("sg", [P, 2, TOKENS])
        prod = sb("prod", [P, 2, TOKENS])
        inner = sb("inner", [P, 2, TOKENS])
        res = sb("res", [P, HALF, D])
        st = sb("st", [P, HALF, 6])
        c = sb("cols", [P, 8, HALF])
        xo = sb("xo", [P, HALF, D])
        G0, G1, U0, U1, R0, R1, Y0, Y1 = (ph.bank(n) for n in ("G0", "G1", "U0", "U1", "R0", "R1", "Y0", "Y1"))
        G, U, R, Y = (G0, G1), (U0, U1), (R0, R1), (Y0, Y1)
        names = """weights pool_step owner_copied consts x_loaded stored xo_free xT_ps xT_ready logits_ps logits_ready
            route_step exp_ready partsT_ps partsT_ready gate_ps up_ps silu_ready prod_ready R_ps inner_ready down_ps
            y_free ln_step rms_ready xo_ready""".split()
        s = {n: sem(n) for n in names}
        group_loaded = [sem(f"group{n}_loaded") for n in range(len(GROUPS))]
        first = [sum(GROUPS[:n]) for n in range(len(GROUPS) + 1)]
        ROUTE, LN = 16, 12
        block = ctx.enter_context(nc.Block())

        @block.sync
        def _(sp):
            sp.dma_start(xt[:, :, :], x_src.rearrange("b p c -> p b c")).then_inc(s["x_loaded"], 16)
            sp.dma_start(wgate[:], d["wgate"]).then_inc(s["weights"], 16)
            for n, loaded in enumerate(group_loaded):
                chunks = slice(first[n], first[n + 1])
                sp.dma_start(wup[:, chunks], d["wup"][:, chunks]).then_inc(loaded, 16)
                sp.dma_start(wdown[:, chunks], d["wdown"][:, chunks]).then_inc(loaded, 16)
                if n == 0:
                    sp.wait_ge(s["pool_step"], 6)
                    for k in range(1, PARTS):
                        sp.dma_start(owner[k * EXPERTS:(k + 1) * EXPERTS, :], owner[0:EXPERTS, :]).then_inc(s["owner_copied"], 16)
            sp.sem_inc(s["xo_free"], 1)
            with sp.Fori(0, 2) as i:
                sp.wait_ge(s["xo_ready"], at(i, HALF, HALF))
                sp.dma_start(x_dst[bass.ds(i * HALF, HALF)].rearrange("b p c -> p b c"), xo[:, :, :]).then_inc(s["stored"], 16)
                sp.wait_ge(s["stored"], at(i, 16, 16))
                sp.sem_inc(s["xo_free"], 1)

        @block.gpsimd
        def _(pool):
            link = Linked(pool, s["pool_step"])
            fill_identity(pool, link, ident[:, :])
            link(pool.tensor_copy(identb[:, :], ident[:, :]))
            link(pool.memset(owner[:, :], 1.0))
            link(pool.affine_select(out=owner[:, :], in_=owner[:, :], compare_op=ALU.is_ge, fill=0.0, base=0,
                                    pattern=[[1, ROUTED * P]], channel_multiplier=-INNER))
            link(pool.affine_select(out=owner[:, :], in_=owner[:, :], compare_op=ALU.is_ge, fill=0.0, base=INNER - 1,
                                    pattern=[[-1, ROUTED * P]], channel_multiplier=INNER))
            link(pool.memset(zeros[:, :], 0.0))
            link(pool.memset(parts[:, :, :, :], 0.0))
            link(pool.memset(before[:, :, :], 1.0))
            link(pool.affine_select(out=before[:, :, :], in_=before[:, :, :], compare_op=ALU.is_ge, fill=0.0, base=-1,
                                    pattern=[[1, EXPERTS], [-1, EXPERTS]], channel_multiplier=0))
            pool.sem_inc(s["consts"], 1)

        @block.tensor
        def _(pe):
            pe.wait_ge(s["pool_step"], 2)
            pe.wait_ge(s["x_loaded"], 16)
            for h in range(2):
                for m in range(DC):
                    bank = (G, U)[h][m]
                    for b in range(HALF):
                        last = pe.transpose(bank[:, b * P:(b + 1) * P], xt[:, h * HALF + b, m * P:(m + 1) * P], ident[:, :])
                    last.then_inc(s["xT_ps"], 1)
            pe.wait_ge(s["weights"], 16)
            pe.wait_ge(s["xT_ready"], 2 * DC)
            for b in range(B):
                for m in range(DC):
                    last = pe.matmul(R0[:, b * EXPERTS:(b + 1) * EXPERTS], xT[:, b // HALF, m, b % HALF * P:(b % HALF + 1) * P],
                                     wgate[:, m, :], start=m == 0, stop=m == DC - 1)
            last.then_inc(s["logits_ps"], 1)
            pe.wait_ge(s["consts"], 1)
            pe.wait_ge(s["owner_copied"], 16 * (PARTS - 1))
            with pe.Fori(0, 2) as i:
                for t in range(ECH + 2):
                    if t < ECH:
                        if t in first:
                            pe.wait_ge(group_loaded[first.index(t)], 32)
                        if t >= 2:
                            pe.wait_ge(s["silu_ready"], at(i, ECH, t - 1))
                            if t - 2 < ROUTED:
                                pe.wait_ge(s["prod_ready"], at(i, ROUTED, t - 1))
                            else:
                                pe.wait_ge(s["inner_ready"], at(i, ECH, t - 1))
                        for k, (bank, done) in enumerate(((G[t % 2], "gate_ps"), (U[t % 2], "up_ps"))):
                            for m in range(DC):
                                last = pe.matmul(bank[:, :], wup[:, t, k, m, :], xT[:, bass.ds(i, 1), m, :].rearrange("p a n -> p (a n)"),
                                                 start=m == 0, stop=m == DC - 1)
                            last.then_inc(s[done], 1)
                    if t == 1:
                        pe.wait_ge(s["route_step"], at(i, ROUTE, ROUTE))
                        for b in range(HALF):
                            last = pe.transpose(R1[:, :].bitcast(BF16)[:, b * P:(b + 1) * P],
                                                parts[:, b].rearrange("p k e -> p (k e)"), identb[:, :])
                        last.then_inc(s["partsT_ps"], 1)
                        pe.wait_ge(s["partsT_ready"], i + 1)
                    if 1 <= t <= ROUTED:
                        n = t - 1
                        if n >= 2:
                            pe.wait_ge(s["inner_ready"], at(i, ECH, n - 1))
                        pe.matmul(R[n % 2][:, :], owner[:, n * P:(n + 1) * P], partsT[:, :], start=True, stop=True)\
                            .then_inc(s["R_ps"], 1)
                    if t >= 2:
                        n = t - 2
                        pe.wait_ge(s["inner_ready"], at(i, ECH, n + 1))
                        if n == 0:
                            pe.wait_ge(s["y_free"], at(i, 2, 2))
                            for bank in Y:
                                pe.matmul(bank[:, :], identb[:, :], zeros[:, :], start=True, stop=False)
                        for b in range(HALF):
                            last = pe.matmul(Y[b // 2][:, b % 2 * D:(b % 2 + 1) * D], inner[:, n % 2, b * P:(b + 1) * P], wdown[:, n, :],
                                             start=False, stop=n == ECH - 1 and b % 2 == 1)
                        last.then_inc(s["down_ps"], 1)

        @block.scalar
        def _(act):
            for h in range(2):
                for m in range(DC):
                    act.wait_ge(s["xT_ps"], DC * h + m + 1)
                    act.activation(xT[:, h, m, :], (G, U)[h][m][:, :], ACT.Copy).then_inc(s["xT_ready"], 1)
            act.wait_ge(s["logits_ps"], 1)
            act.activation(logits[:, :, :], R0[:, 0:B * EXPERTS].rearrange("p (b e) -> p b e", b=B), ACT.Copy)\
                .then_inc(s["logits_ready"], 1)
            with act.Fori(0, 2) as i:
                act.wait_ge(s["route_step"], at(i, ROUTE, 2))
                act.activation(prob[:, 0], prob[:, 0], ACT.Exp).then_inc(s["exp_ready"], 1)
                for t in range(ECH):
                    act.wait_ge(s["gate_ps"], at(i, ECH, t + 1))
                    if t >= 2:
                        if t - 2 < ROUTED:
                            act.wait_ge(s["prod_ready"], at(i, ROUTED, t - 1))
                        else:
                            act.wait_ge(s["inner_ready"], at(i, ECH, t - 1))
                    act.activation(sg[:, t % 2, :], G[t % 2][:, :], ACT.Silu).then_inc(s["silu_ready"], 1)
                    if t == 1:
                        act.wait_ge(s["partsT_ps"], i + 1)
                        act.activation(partsT[:, :], R1[:, :].bitcast(BF16)[:, 0:TOKENS], ACT.Copy)\
                            .then_inc(s["partsT_ready"], 1)
                act.wait_ge(s["ln_step"], at(i, LN, LN - 1))
                act.activation(c[:, 6, :], c[:, 6, :], ACT.Sqrt).then_inc(s["rms_ready"], 1)

        @block.vector
        def _(dve):
            dve.wait_ge(s["consts"], 1)
            dve.wait_ge(s["logits_ready"], 1)
            dve.sem_inc(s["y_free"], 2)
            with dve.Fori(0, 2) as i:
                link = Linked(dve, s["route_step"], ROUTE, i)
                mine = logits[:, bass.ds(i * HALF, HALF), :]
                link(dve.tensor_reduce(col[:, 0, :], mine, AX.X, ALU.max))
                link(dve.tensor_tensor(prob[:, 0], mine, along(col[:, 0, :], EXPERTS), ALU.subtract))
                dve.wait_ge(s["exp_ready"], i + 1)
                link(dve.tensor_reduce(col[:, 1, :], prob[:, 0], AX.X, ALU.add))
                link(dve.reciprocal(col[:, 2, :], col[:, 1, :]))
                link(dve.tensor_tensor(prob[:, 1], prob[:, 0], along(col[:, 2, :], EXPERTS), ALU.mult))
                every = [P, HALF, EXPERTS, EXPERTS]
                pj, pi = prob[:, 1].unsqueeze(2).broadcast_to(every), prob[:, 1].unsqueeze(3).broadcast_to(every)
                link(dve.tensor_tensor(cmp_[:, 0], pj, pi, ALU.is_gt),
                     dve.tensor_tensor(cmp_[:, 1], pj, pi, ALU.is_equal))
                link(dve.tensor_tensor(cmp_[:, 1], cmp_[:, 1], before[:, :, :].unsqueeze(1).broadcast_to(every), ALU.mult))
                link(dve.tensor_tensor(cmp_[:, 0], cmp_[:, 0], cmp_[:, 1], ALU.add))
                link(dve.tensor_reduce(rank[:, :, :], cmp_[:, 0], AX.X, ALU.add))
                link(dve.scalar_tensor_tensor(route[:, 0], rank[:, :, :], TOP - 0.5, prob[:, 1], ALU.is_lt, ALU.mult))
                link(dve.tensor_copy(parts[:, :, 0, :], route[:, 0]))
                link(dve.tensor_tensor(route[:, 1], route[:, 0], parts[:, :, 0, :], ALU.subtract))
                link(dve.tensor_copy(parts[:, :, 1, :], route[:, 1]))
                link(dve.tensor_tensor(route[:, 0], route[:, 1], parts[:, :, 1, :], ALU.subtract))
                dve.tensor_copy(parts[:, :, 2, :], route[:, 0]).then_inc(s["route_step"], 1)
                for n in range(ECH):
                    dve.wait_ge(s["silu_ready"], at(i, ECH, n + 1))
                    dve.wait_ge(s["up_ps"], at(i, ECH, n + 1))
                    if n >= 2:
                        dve.wait_ge(s["down_ps"], at(i, ECH, n - 1))
                    if n < ROUTED:
                        dve.tensor_tensor(prod[:, n % 2, :], sg[:, n % 2, :], U[n % 2][:, :], ALU.mult).then_inc(s["prod_ready"], 1)
                        dve.wait_ge(s["prod_ready"], at(i, ROUTED, n + 1))
                        dve.wait_ge(s["R_ps"], at(i, ROUTED, n + 1))
                        dve.tensor_tensor(inner[:, n % 2, :], prod[:, n % 2, :], R[n % 2][:, :], ALU.mult).then_inc(s["inner_ready"], 1)
                    else:
                        dve.tensor_tensor(inner[:, n % 2, :], sg[:, n % 2, :], U[n % 2][:, :], ALU.mult).then_inc(s["inner_ready"], 1)
                link = Linked(dve, s["ln_step"], LN, i)
                dve.wait_ge(s["down_ps"], at(i, ECH, ECH))
                for k in range(2):
                    dve.tensor_tensor(res[:, 2 * k:2 * k + 2, :], xt[:, bass.ds(i * HALF + 2 * k, 2), :],
                                      Y[k][:, :].rearrange("p (b n) -> p b n", b=2), ALU.add).then_inc(s["y_free"], 1)
                dve.wait_ge(s["y_free"], at(i, 2, 4))
                link(*(dve.bn_stats(st[:, b, :], res[:, b, :]) for b in range(HALF)))
                link(dve.tensor_tensor(c[:, 0, :], st[:, :, 1], st[:, :, 4], ALU.subtract),
                     dve.tensor_tensor(c[:, 1, :], st[:, :, 1], st[:, :, 4], ALU.add),
                     dve.tensor_tensor(c[:, 2, :], st[:, :, 2], st[:, :, 5], ALU.add))
                link(dve.scalar_tensor_tensor(c[:, 3, :], c[:, 0, :], 0.25, c[:, 0, :], ALU.mult, ALU.mult),
                     dve.tensor_scalar(c[:, 4, :], c[:, 2, :], 1.0 / D, LN_EPS, ALU.mult, ALU.add),
                     dve.tensor_scalar(c[:, 5, :], c[:, 1, :], 0.5, None, ALU.mult))
                link(dve.tensor_tensor(c[:, 6, :], c[:, 3, :], c[:, 4, :], ALU.add))
                dve.wait_ge(s["rms_ready"], i + 1)
                link(dve.reciprocal(c[:, 7, :], c[:, 6, :]))
                link.close()
                dve.wait_ge(s["xo_free"], i + 1)
                for b in range(HALF):
                    dve.tensor_scalar(xo[:, b, :], res[:, b, :], c[:, 5, b:b + 1], c[:, 7, b:b + 1], ALU.subtract, ALU.mult)\
                        .then_inc(s["xo_ready"], 1)


def layout_layer0_experts(inp):
    def columns(routed, shared):
        a = np.concatenate([*inp[routed], inp[shared], np.zeros((D, ECH * P - (EXPERTS + 2) * INNER), np.float32)], axis=1)
        return a.reshape(DC, P, ECH, P)
    wup = np.stack([columns("L0_ffn_wg", "L0_ffn_sg"), columns("L0_ffn_wu", "L0_ffn_su")]).transpose(2, 3, 0, 1, 4)
    down = np.concatenate([inp["L0_ffn_wd"].reshape(EXPERTS * INNER, D), inp["L0_ffn_sd"],
                           np.zeros((ECH * P - (EXPERTS + 2) * INNER, D), np.float32)])
    return dict(wgate=inp["L0_ffn_w_gate"].T.reshape(DC, P, EXPERTS).transpose(1, 0, 2), wup=wup,
                wdown=down.reshape(ECH, P, D).transpose(1, 0, 2))


KEY_HEADS, VAL_HEADS, DK, TAPS = 16, 32, 128, 4
HB = 4
KB = HB // 2
ROUNDS = VAL_HEADS // HB
AHEAD = 3
ITEMS = HB * B
QK = 2 * KB
CHUNKS = QK + HB
BL = 32
NBL = S // BL
RMS_EPS = 1e-6
TINY = 1e-12


def layer1_delta_rule(nc, sems, d, x_src, x_dst):
    ctx = ExitStack()
    with ctx:
        ph = Phase(nc, "c", ctx, sems)
        sb, sem = ph.sb, ph.sem
        ident = sb("ident", [P, P])
        identb = sb("identb", [P, P], BF16)
        tri = sb("tri", [P, P])
        hidden = sb("hidden", [P, P])
        hiddenb = sb("hiddenb", [P, P], BF16)
        ones = sb("ones", [P, 1])
        zero = sb("zero", [P, 1])
        wba = sb("wba", [P, DC, 2 * VAL_HEADS])
        bias = sb("bias", [P, 2, VAL_HEADS])
        normw = sb("normw", [P, 1])
        wqk = sb("wqk", [P, QK, DC * P])
        wv = sb("wv", [P, HB, DC * P])
        wcqk = sb("wcqk", [P, QK, TAPS])
        wcv = sb("wcv", [P, HB, TAPS])
        wz = sb("wz", [P, DC, HB * P])
        wout = sb("wout", [P, HB, D])
        acc = sb("acc", [P, B, D])
        xT = sb("xT", [P, DC, B, P])
        beta = sb("beta", [P, B, VAL_HEADS])
        g = sb("g", [P, B, VAL_HEADS])
        gcn = sb("gcn", [P, B, VAL_HEADS])
        gR, gcnR, betaR = (sb(n, [P, HB, B]) for n in ("gR", "gcnR", "betaR"))
        pad = sb("pad", [P, 2, B, TAPS - 1 + S])
        cv = sb("cv", [P, 2, B, S])
        qkT = sb("qkT", [P, KB, 2, B, S])
        sq = sb("sq", [P, 2, B, S])
        root = sb("root", [P, KB, 2, B])
        nrm = sb("nrm", [P, 3, KB, 2, B])
        qinv = sb("qinv", [P, 2, KB, B])
        cj = sb("cj", [P, HB, B])
        V = sb("V", [P, HB, B, S])
        NP = sb("NP", [P, HB, B, 2, S])
        A = sb("A", [P, BL, BL])
        sm = A[:, :, :].rearrange("p a b -> p (a b)").rearrange("p (k b h) -> p k b h", k=4, b=B)
        T = sb("T", [P, BL, BL])
        T0 = sb("T0", [P, BL, BL], BF16)
        tmp = sb("tmp", [P, 256])
        Tb = sb("Tb", [P, ITEMS, P])
        TbT = sb("TbT", [P, ITEMS, P])
        Y = sb("Y", [P, HB, B, S])
        zs = sb("zs", [P, B, HB * P])
        s2 = sb("s2", [P, HB, B])
        f = sb("f", [P, 3, HB, B])
        yT = sb("yT", [P, 2, HB, S])
        banks = [ph.bank(f"bank{n}") for n in range(8)]
        HALF_ITEMS = ITEMS // KB
        blocks = nc.dram_tensor("diagonal_blocks", (3, NBL, ITEMS, BL, BL), F32, kind="Internal").ap()
        names = """blocks_out T_out A_out weights consts pool_step x_loaded xT_ps xT_copied ba_ps gate_step gate_act gc_ps gates_ready
            qk_loaded v_loaded z_loaded out_loaded gates_used proj_ready pad_ready tap0_ready conv_step cv_ready silu_ready sq_ready norms_ps
            root_ready rms_ready csqa_ready norm_step gcrow_ps E_ready GP_ps NP_ready gathered elim_step Tb_placed TbT_placed diag_cleared
            vt_ps V_ready z_ps z_ready MT_ps MT_ready apply_ps y_ready W_ps W_ready C_ps C_ready csq_ready s2_ready
            wout_ready var_ready f_step y_scaled yT_ps yT_ready out_ps acc_step
            ln_step ln_log ln_rstd xo_ready stored""".split()
        s = {n: sem(n) for n in names}
        quads = [(h, q) for h in range(HB) for q in range(2)]
        flat = lambda ap: ap.rearrange("p a b -> p (a b)")
        ELIM = 2 * (BL - 1) + 2
        BLOCKS_OUT = 16 * KB * NBL
        F_STEPS = 2 * KB + 2
        order = [(2 * k + e, q) for k in range(KB) for q in range(2) for e in range(2)]
        block = ctx.enter_context(nc.Block())

        def project_banks(m):
            a, b = ((6, 7), (4, 5), (6, 4), (5, 6), (4, 5), (6, 7), (0, 1), (2, 3))[m]
            return banks[a], banks[b]

        def rr(t, h, q):
            return t[:, h, 4 * q:4 * q + 4]

        @block.sync
        def _(sp):
            for dst, k in ((wba, "wba"), (bias, "bias"), (normw, "normw")):
                sp.dma_start(dst[:], d[k]).then_inc(s["weights"], 16)
            sp.dma_start(acc[:, :, :], x_src.rearrange("b p c -> p b c")).then_inc(s["x_loaded"], 16)

            def load(dst, name, r, loaded):
                sp.dma_start(dst[:], d[name][bass.ds(r, 1)].rearrange("a p m n -> (a p) m n")).then_inc(s[loaded], 16)

            def load_qk(r):
                load(wqk, "wqk", r, "qk_loaded")
                load(wcqk, "wcqk", r, "qk_loaded")

            def load_v(r):
                load(wv, "wv", r, "v_loaded")
                load(wcv, "wcv", r, "v_loaded")

            def gather(i):
                for k in range(KB):
                    sp.wait_ge(s["NP_ready"], at(i, ITEMS, (k + 1) * HALF_ITEMS))
                    for r in range(NBL):
                        rows = slice(BL * r, BL * r + BL)
                        sp.dma_start(blocks[0, r, k * HALF_ITEMS:(k + 1) * HALF_ITEMS].rearrange("t j i -> j t i"),
                                     NP[rows, 2 * k:2 * k + 2, :, 0, rows].rearrange("p h b i -> p (h b) i")).then_inc(s["blocks_out"], 16)
                sp.wait_ge(s["blocks_out"], at(i, BLOCKS_OUT, BLOCKS_OUT))
                sp.dma_start(A[:, :, :], blocks[0].rearrange("r t j i -> (r t) j i")).then_inc(s["gathered"], 16)

            def scatter(i):
                sp.wait_ge(s["elim_step"], at(i, ELIM, ELIM - 1))
                sp.dma_start(blocks[1].rearrange("r t i j -> (r t) i j"), T[:, :, :]).then_inc(s["T_out"], 16)
                sp.wait_ge(s["elim_step"], at(i, ELIM, ELIM))
                sp.dma_start(blocks[2].rearrange("r t i j -> (r t) i j"), A[:, :, :]).then_inc(s["A_out"], 16)
                for n, dst, out, placed in ((1, Tb, "T_out", "Tb_placed"), (2, TbT, "A_out", "TbT_placed")):
                    sp.wait_ge(s[out], at(i, 16, 16))
                    for r in range(NBL):
                        rows = slice(BL * r, BL * r + BL)
                        sp.dma_start(dst[rows, :, rows], blocks[n, r].rearrange("t i j -> i t j")).then_inc(s[placed], 16)

            load_qk(0)
            load_v(0)
            load(wz, "wz", 0, "z_loaded")
            load(wout, "wout", 0, "out_loaded")
            sp.wait_ge(s["proj_ready"], QK)
            sp.wait_ge(s["cv_ready"], QK)
            load_qk(1)
            gather(0)
            with sp.Fori(0, ROUNDS - 1) as i:
                scatter(i)
                sp.wait_ge(s["cv_ready"], at(i, CHUNKS, CHUNKS))
                load_v(i + 1)
                sp.wait_ge(s["z_ps"], at(i, B, B))
                load(wz, "wz", i + 1, "z_loaded")
                sp.wait_ge(s["cv_ready"], at(i + 1, CHUNKS, QK))
                load_qk(i + 2)
                gather(i + 1)
                sp.wait_ge(s["out_ps"], at(i, B, B))
                load(wout, "wout", i + 1, "out_loaded")
            scatter(ROUNDS - 1)
            with sp.Fori(0, B) as b:
                sp.wait_ge(s["xo_ready"], b + 1)
                sp.dma_start(x_dst[bass.ds(b, 1)].rearrange("a p c -> p a c"), acc[:, bass.ds(b, 1), :]).then_inc(s["stored"], 16)
            sp.wait_ge(s["stored"], 16 * B)

        @block.gpsimd
        def _(pool):
            link = Linked(pool, s["pool_step"])
            fill_identity(pool, link, ident[:, :])
            link(pool.tensor_copy(identb[:, :], ident[:, :]))
            link(pool.memset(tri[:, :], 1.0))
            link(pool.affine_select(out=tri[:, :], in_=tri[:, :], compare_op=ALU.is_ge, fill=0.0, base=0,
                                    pattern=[[1, P]], channel_multiplier=-1))
            link(pool.memset(hidden[:, :], 0.0))
            link(pool.affine_select(out=hidden[:, :], in_=hidden[:, :], compare_op=ALU.is_ge, fill=MASKED, base=0,
                                    pattern=[[1, P]], channel_multiplier=-1))
            link(pool.tensor_copy(hiddenb[:, :], hidden[:, :]))
            link(pool.memset(T0[:, :, :], 0.0))
            link(pool.affine_select(out=T0[:, :, :], in_=T0[:, :, :], compare_op=ALU.not_equal, fill=1.0, base=0,
                                    pattern=[[1, BL], [-1, BL]], channel_multiplier=0))
            link(pool.memset(zero[:, :], 0.0))
            link(pool.memset(Tb[:, :, :], 0.0))
            link(pool.memset(TbT[:, :, :], 0.0))
            link(pool.memset(pad[:, :, :, :], 0.0))
            pool.memset(ones[:, :], 1.0).then_inc(s["consts"], 1)

            def tap0(r, m, first=False):
                pool.wait_ge(s["pad_ready"], at(r, 2 * CHUNKS, 2 * m + 2))
                if m < 2 and not first:
                    pool.wait_ge(s["vt_ps"], at(r, 2 * HB, 2 * m - 2))
                elif 2 <= m < QK + 2:
                    pool.wait_ge(s["silu_ready"], at(r, CHUNKS, m - 1))
                elif m >= QK + 2:
                    pool.wait_ge(s["vt_ps"], at(r, 2 * HB, 2 * (m - QK - 1)))
                w = wcqk[:, m, 0:1] if m < QK else wcv[:, m - QK, 0:1]
                pool.tensor_tensor(cv[:, m % 2], pad[:, m % 2, :, 0:S], along(w.broadcast_to([P, B]), S), ALU.mult)\
                    .then_inc(s["tap0_ready"], 1)

            def square(r, m, first=False):
                pool.wait_ge(s["silu_ready"], at(r, CHUNKS, m + 1))
                if m >= 2 or not first:
                    pool.wait_ge(s["norms_ps"], at(r, QK, m - 1))
                src = qkT[:, m // 2, m % 2]
                pool.tensor_tensor(sq[:, m % 2], src, src, ALU.mult).then_inc(s["sq_ready"], 1)

            def round_(i, more):
                tap0(i, QK)
                tap0(i, QK + 1)
                pool.wait_ge(s["blocks_out"], at(i, BLOCKS_OUT, BLOCKS_OUT))
                pool.wait_ge(s["tap0_ready"], at(i, CHUNKS, QK + 2))
                for r in range(NBL):
                    rows = slice(BL * r, BL * r + BL)
                    if r:
                        pool.wait_ge(s["diag_cleared"], at(i, NBL, r))
                    none = along(zero[rows, 0:1].broadcast_to([BL, ITEMS]), BL)
                    pool.tensor_tensor(NP[rows, :, :, 0, rows].rearrange("p h b i -> p (h b) i"), none, none, ALU.add)\
                        .then_inc(s["diag_cleared"], 1)
                pool.wait_ge(s["diag_cleared"], at(i, NBL, NBL))
                pool.wait_ge(s["out_loaded"], at(i, 16, 16))
                pool.wait_ge(s["weights"], 48)
                pool.tensor_tensor(flat(wout[:, :, :]), flat(wout[:, :, :]), normw[:, 0:1].broadcast_to([P, HB * D]), ALU.mult)\
                    .then_inc(s["wout_ready"], 1)
                tap0(i, QK + 2)
                tap0(i, QK + 3)
                if more:
                    tap0(i + 1, 0)
                    tap0(i + 1, 1)
                    square(i + 1, 0)
                    tap0(i + 1, 2)
                    square(i + 1, 1)
                    tap0(i + 1, 3)
                    square(i + 1, 2)
                    square(i + 1, 3)
                for n in range(0, 8, 2):
                    h, q = quads[n]
                    pool.wait_ge(s["C_ready"], at(i, 8, n + 1))
                    pool.tensor_tensor(rr(V, h, q), rr(Y, h, q), rr(Y, h, q), ALU.mult).then_inc(s["csq_ready"], 1)

            for m in range(QK + 1):
                if m < QK:
                    tap0(0, m, first=True)
                if m >= 1:
                    square(0, m - 1, first=True)
            with pool.Fori(0, ROUNDS - 1) as i:
                round_(i, True)
            round_(ROUNDS - 1, False)

        @block.tensor
        def _(pe):
            pe.wait_ge(s["consts"], 1)
            pe.wait_ge(s["x_loaded"], 16)
            for b in range(B):
                bank = banks[b // 2]
                for c in range(DC):
                    last = pe.transpose(bank[:, (2 * (b % 2) + c) * P:(2 * (b % 2) + c + 1) * P], acc[:, b, c * P:(c + 1) * P],
                                        ident[:, :])
                last.then_inc(s["xT_ps"], 1)
            pe.wait_ge(s["weights"], 48)
            pe.wait_ge(s["xT_copied"], 4)
            for b in range(B):
                for c in range(DC):
                    last = pe.matmul(banks[4][:, 64 * b:64 * b + 64], xT[:, c, b, :], wba[:, c, :], start=c == 0, stop=c == DC - 1)
            last.then_inc(s["ba_ps"], 1)
            pe.wait_ge(s["gate_step"], 6)
            pe.matmul(banks[5][:, 0:B * VAL_HEADS], tri[:, :], flat(g[:, :, :]), start=True, stop=True).then_inc(s["gc_ps"], 1)

            def project(r, m, first=False):
                pair, w = project_banks(m), wqk[:, m] if m < QK else wv[:, m - QK]
                if m == 0:
                    pe.wait_ge(s["qk_loaded"], at(r, 32, 32))
                if m == QK:
                    pe.wait_ge(s["v_loaded"], at(r, 32, 32))
                    pe.wait_ge(s["E_ready"], at(r, ITEMS, ITEMS))
                if m == QK + 1:
                    pe.wait_ge(s["NP_ready"], at(r, ITEMS, ITEMS))
                if m < 2 and not first:
                    used, per = (("z_ready", B), ("V_ready", 2 * HB))[m]
                    pe.wait_ge(s[used], at(r, per, 0))
                if 2 <= m < QK:
                    pe.wait_ge(s["pad_ready"], at(r, 2 * CHUNKS, 2 * m))
                for q in range(2):
                    for c in range(DC):
                        last = pe.matmul(four(pair[q][:, :]), w[:, c * P:(c + 1) * P], xT[:, c, 4 * q:4 * q + 4, :],
                                         start=c == 0, stop=c == DC - 1)
                last.then_inc(s["proj_ready"], 1)

            def norms(r, m):
                if m == 0:
                    pe.wait_ge(s["pad_ready"], at(r, 2 * CHUNKS, 2))
                pe.wait_ge(s["sq_ready"], at(r, QK, m + 1))
                for b in range(B):
                    last = pe.matmul(banks[7][:, m * B + b:m * B + b + 1], sq[:, m % 2, b, :], ones[:, :], start=True, stop=True)
                last.then_inc(s["norms_ps"], 1)

            def gcrow(i, n):
                h, q = order[n]
                bank = banks[4 + n % 2]
                if n == 0:
                    pe.wait_ge(s["pad_ready"], at(i, 2 * CHUNKS, 2 * QK))
                if n >= 2:
                    pe.wait_ge(s["E_ready"], at(i, ITEMS, 4 * (n - 1)))
                pe.matmul(four(bank[:, :]), identb[:, :], spread(hiddenb[:, :], 4), start=True, stop=False)
                for b in range(4):
                    last = pe.matmul(bank[:, b * P:(b + 1) * P], gR[:, h, 4 * q + b:4 * q + b + 1].broadcast_to([P, P]), tri[:, :],
                                     start=False, stop=b == 3)
                last.then_inc(s["gcrow_ps"], 1)

            def gram(i, u):
                k, b0 = u // 4, 2 * (u % 4)
                bank = banks[6 + u % 2]
                if u == 0:
                    pe.wait_ge(s["root_ready"], at(i, 1, 1))
                if u >= 2:
                    pe.wait_ge(s["NP_ready"], at(i, ITEMS, 4 * (u - 1)))
                for b in range(2):
                    last = pe.matmul(bank[:, b * 2 * P:(b + 1) * 2 * P].rearrange("p (a n) -> p a n", a=2),
                                     qkT[:, k, 0, b0 + b, :], qkT[:, k, :, b0 + b, :], start=True, stop=True)
                last.then_inc(s["GP_ps"], 1)

            def values(i, n):
                pe.wait_ge(s["silu_ready"], at(i, CHUNKS, QK + n + 1))
                if n == 0:
                    pe.wait_ge(s["pad_ready"], at(i, 2 * CHUNKS, 2 * (QK + 1)))
                for q in range(2):
                    if n >= 1:
                        pe.wait_ge(s["V_ready"], at(i, 2 * HB, 2 * n - 1 + q))
                    for b in range(4):
                        last = pe.transpose(banks[4 + q][:, b * P:(b + 1) * P], cv[:, n % 2, 4 * q + b, :], ident[:, :])
                    last.then_inc(s["vt_ps"], 1)

            def out_gate(i, b):
                if b == 0:
                    pe.wait_ge(s["z_loaded"], at(i, 16, 16))
                    pe.wait_ge(s["pad_ready"], at(i, 2 * CHUNKS, 2 * (QK + 2)))
                if b >= 2:
                    pe.wait_ge(s["z_ready"], at(i, B, b - 1))
                for c in range(DC):
                    last = pe.matmul(banks[6 + b % 2][:, :], xT[:, c, b, :], wz[:, c, :], start=c == 0, stop=c == DC - 1)
                last.then_inc(s["z_ps"], 1)

            def items(ps, n, lhsT, rhs):
                h, q = quads[n]
                for b in range(4):
                    last = pe.matmul(banks[n % 4][:, b * P:(b + 1) * P], lhsT(h, 4 * q + b), rhs(h, 4 * q + b), start=True, stop=True)
                last.then_inc(s[ps], 1)

            def apply(i, rep):
                y = V if rep == 0 else Y
                for n in range(8):
                    if rep == 0:
                        pe.wait_ge(s["MT_ready"], at(i, 8, min(n + 5, 8)))
                    else:
                        pe.wait_ge(s["y_ready"], at(i, 24, 8 * (rep - 1) + n + 1))
                    if n >= 4 or rep:
                        pe.wait_ge(s["y_ready"], at(i, 24, 8 * rep + n - 3))
                    items("apply_ps", n, lambda h, b: NP[:, h, b, 0, :], lambda h, b: y[:, h, b, :])

            def decays_and_grams(r, n):
                if n == 0:
                    pe.wait_ge(s["gates_used"], at(r, 3, 3))
                gcrow(r, n)
                gram(r, n)

            def round_(i, more):
                for m in range(QK, CHUNKS):
                    project(i, m)
                for b in range(B):
                    out_gate(i, b)
                values(i, 0)
                values(i, 1)
                if more:
                    project(i + 1, 0)
                pe.wait_ge(s["Tb_placed"], at(i, 16 * NBL, 16 * NBL))
                pe.wait_ge(s["diag_cleared"], at(i, NBL, NBL))
                pe.wait_ge(s["pad_ready"], at(i, 2 * CHUNKS, 2 * CHUNKS))
                for n in range(8):
                    if n >= 4:
                        pe.wait_ge(s["MT_ready"], at(i, 8, n - 3))
                    items("MT_ps", n, lambda h, b: Tb[:, h * B + b, :], lambda h, b: NP[:, h, b, 0, :])
                    if n == 2:
                        values(i, 2)
                    if n == 6:
                        values(i, 3)
                pe.wait_ge(s["V_ready"], at(i, 2 * HB, 2 * HB))
                if more:
                    project(i + 1, 1)
                apply(i, 0)
                if more:
                    project(i + 1, 2)
                apply(i, 1)
                if more:
                    project(i + 1, 3)
                    norms(i + 1, 0)
                apply(i, 2)
                if more:
                    norms(i + 1, 1)
                pe.wait_ge(s["TbT_placed"], at(i, 16 * NBL, 16 * NBL))
                for n in range(8):
                    pe.wait_ge(s["y_ready"], at(i, 24, 16 + max(n + 1, min(n + 5, 8))))
                    if n >= 4:
                        pe.wait_ge(s["W_ready"], at(i, 8, n - 3))
                    items("W_ps", n, lambda h, b: TbT[:, h * B + b, :], lambda h, b: Y[:, h, b, :])
                if more:
                    norms(i + 1, 2)
                for n in range(8):
                    pe.wait_ge(s["W_ready"], at(i, 8, min(n + 5, 8)))
                    if n >= 4:
                        pe.wait_ge(s["C_ready"], at(i, 8, n - 3))
                    items("C_ps", n, lambda h, b: NP[:, h, b, 1, :], lambda h, b: Y[:, h, b, :])
                pe.wait_ge(s["wout_ready"], at(i, 1, 1))
                pe.wait_ge(s["C_ready"], at(i, 8, 8))
                if more:
                    norms(i + 1, 3)
                    for n in range(AHEAD + 2):
                        decays_and_grams(i + 1, n)
                for b in range(B + 1):
                    if b < B:
                        if b >= 2:
                            pe.wait_ge(s["yT_ready"], at(i, B, b - 1))
                        pe.wait_ge(s["y_scaled"], at(i, ITEMS, HB * (b + 1)))
                        for h in range(HB):
                            last = pe.transpose(banks[b % 2][:, h * P:(h + 1) * P], Y[:, h, b, :], ident[:, :])
                        last.then_inc(s["yT_ps"], 1)
                    if b >= 1:
                        m = b - 1
                        pe.wait_ge(s["yT_ready"], at(i, B, m + 1))
                        if m >= 2:
                            pe.wait_ge(s["acc_step"], at(i, B, m - 1))
                        for h in range(HB):
                            last = pe.matmul(banks[2 + m % 2][:, 0:D], yT[:, m % 2, h, :], wout[:, h, :], start=h == 0, stop=h == HB - 1)
                        last.then_inc(s["out_ps"], 1)
                    if more and b + AHEAD + 2 < 8:
                        decays_and_grams(i + 1, b + AHEAD + 2)
                pe.wait_ge(s["acc_step"], at(i, B, B))

            pe.wait_ge(s["gate_step"], 8)
            for m in range(QK):
                project(0, m, first=True)
            for m in range(QK):
                norms(0, m)
            for n in range(8):
                decays_and_grams(0, n)
            with pe.Fori(0, ROUNDS - 1) as i:
                round_(i, True)
            round_(ROUNDS - 1, False)

        @block.scalar
        def _(act):
            for n in range(4):
                act.wait_ge(s["xT_ps"], 2 * n + 2)
                act.activation(xT[:, :, 2 * n:2 * n + 2, :], banks[n][:, :].rearrange("p (b c n) -> p c b n", b=2, c=DC), ACT.Copy)\
                    .then_inc(s["xT_copied"], 1)
            ba = banks[4][:, :].rearrange("p (b k h) -> p b k h", b=B, k=2)
            act.wait_ge(s["ba_ps"], 1)
            act.activation(sm[:, 0], ba[:, :, 0, :], ACT.Exp, scale=-1.0).then_inc(s["gate_act"], 1)
            act.wait_ge(s["gate_step"], 2)
            act.activation(sm[:, 2], sm[:, 2], ACT.Exp, scale=-1.0).then_inc(s["gate_act"], 1)
            act.wait_ge(s["gate_step"], 3)
            act.activation(sm[:, 2], sm[:, 3], ACT.Ln).then_inc(s["gate_act"], 1)
            act.wait_ge(s["weights"], 48)
            act.activation(bias[:, 1, :], bias[:, 1, :], ACT.Exp).then_inc(s["gate_act"], 1)

            def copy_in(r, m, first=False):
                act.wait_ge(s["proj_ready"], at(r, CHUNKS, m + 1))
                if m >= 2 or not first:
                    act.wait_ge(s["cv_ready"], at(r, CHUNKS, m - 1))
                    act.wait_ge(s["tap0_ready"], at(r, CHUNKS, m - 1))
                pair = project_banks(m)
                for q in range(2):
                    act.activation(pad[:, m % 2, 4 * q:4 * q + 4, TAPS - 1:], four(pair[q][:, :]), ACT.Copy)\
                        .then_inc(s["pad_ready"], 1)

            def silu(r, m):
                act.wait_ge(s["cv_ready"], at(r, CHUNKS, m + 1))
                dst = qkT[:, m // 2, m % 2] if m < QK else cv[:, m % 2]
                act.activation(dst, cv[:, m % 2], ACT.Silu).then_inc(s["silu_ready"], 1)

            def take_root(r):
                act.wait_ge(s["norms_ps"], at(r, QK, QK))
                act.activation(root[:, :, :, :].rearrange("p k q b -> p (k q b)"), banks[7][:, 0:QK * B], ACT.Sqrt)\
                    .then_inc(s["root_ready"], 1)

            def out_gate(i, b):
                act.wait_ge(s["z_ps"], at(i, B, b + 1))
                act.activation(zs[:, b, :], banks[6 + b % 2][:, :], ACT.Silu).then_inc(s["z_ready"], 1)

            def copy_quad(i, ps, n, dst, ready):
                act.wait_ge(s[ps], at(i, 8, n + 1))
                act.activation(dst, four(banks[n % 4][:, :]), ACT.Copy).then_inc(s[ready], 1)

            def decays(r, n):
                h, q = order[n]
                act.wait_ge(s["gcrow_ps"], at(r, 8, n + 1))
                for b in range(4):
                    act.activation(NP[:, h, 4 * q + b, 1, :], banks[4 + n % 2][:, b * P:(b + 1) * P], ACT.Exp,
                                   bias=gcnR[:, h, 4 * q + b:4 * q + b + 1]).then_inc(s["E_ready"], 1)

            def round_(i, more):
                copy_in(i, QK)
                copy_in(i, QK + 1)
                for b in range(B):
                    out_gate(i, b)
                silu(i, QK)
                copy_in(i, QK + 2)
                silu(i, QK + 1)
                copy_in(i, QK + 3)
                for n, (h, q) in enumerate(quads):
                    if n == 2:
                        silu(i, QK + 2)
                    if n == 3 and more:
                        copy_in(i + 1, 0)
                    if n == 5:
                        silu(i, QK + 3)
                    copy_quad(i, "MT_ps", n, NP[:, h, 4 * q:4 * q + 4, 0, :], "MT_ready")
                if more:
                    for m in range(3):
                        copy_in(i + 1, m + 1)
                        silu(i + 1, m)
                for n, (h, q) in enumerate(quads):
                    if more and n == 5:
                        silu(i + 1, 3)
                    copy_quad(i, "W_ps", n, rr(Y, h, q), "W_ready")
                for n, (h, q) in enumerate(quads):
                    copy_quad(i, "C_ps", n, rr(Y, h, q), "C_ready")
                    if n % 2:
                        act.wait_ge(s["C_ready"], at(i, 8, n + 1))
                        act.activation(rr(V, h, q), rr(Y, h, q), ACT.Square).then_inc(s["csqa_ready"], 1)
                if more:
                    take_root(i + 1)
                act.wait_ge(s["var_ready"], at(i, 2, 2))
                act.activation(f[:, 1], f[:, 0], ACT.Sqrt).then_inc(s["rms_ready"], 1)
                if more:
                    for n in range(AHEAD + 2):
                        decays(i + 1, n)
                for b in range(B):
                    act.wait_ge(s["yT_ps"], at(i, B, b + 1))
                    if b >= 2:
                        act.wait_ge(s["out_ps"], at(i, B, b - 1))
                    act.activation(yT[:, b % 2], four(banks[b % 2][:, :]), ACT.Copy).then_inc(s["yT_ready"], 1)
                    if more and b + AHEAD + 2 < 8:
                        decays(i + 1, b + AHEAD + 2)

            for m in range(QK + 1):
                if m < QK:
                    copy_in(0, m, first=True)
                if m >= 1:
                    silu(0, m - 1)
            take_root(0)
            for n in range(8):
                decays(0, n)
            with act.Fori(0, ROUNDS - 1) as i:
                round_(i, True)
            round_(ROUNDS - 1, False)
            act.wait_ge(s["ln_step"], 3 * B + 1)
            act.activation(f[:, 1, 0, :], f[:, 0, 0, :], ACT.Ln).then_inc(s["ln_log"], 1)
            act.wait_ge(s["ln_log"], 1)
            act.activation(f[:, 1, 0, :], f[:, 1, 0, :], ACT.Exp, scale=-0.5).then_inc(s["ln_rstd"], 1)

        @block.vector
        def _(dve):
            link = Linked(dve, s["gate_step"])
            ba = banks[4][:, :].rearrange("p (b k h) -> p b k h", b=B, k=2)
            dve.wait_ge(s["weights"], 48)
            dve.wait_ge(s["gate_act"], 1)
            link(dve.tensor_tensor(sm[:, 1], ba[:, :, 1, :], spread(bias[:, 0, :], B), ALU.add))
            link(dve.scalar_tensor_tensor(sm[:, 2], sm[:, 1], -1.0, sm[:, 1], ALU.mult, ALU.max))
            dve.wait_ge(s["gate_act"], 2)
            link(dve.tensor_scalar(sm[:, 3], sm[:, 2], 1.0, None, ALU.add))
            dve.wait_ge(s["gate_act"], 4)
            link(dve.scalar_tensor_tensor(sm[:, 1], sm[:, 1], 0.0, sm[:, 2], ALU.max, ALU.add))
            link(dve.tensor_scalar(sm[:, 0], sm[:, 0], 1.0, None, ALU.add))
            link(dve.scalar_tensor_tensor(g[:, :, :], sm[:, 1], -1.0, spread(bias[:, 1, :], B), ALU.mult, ALU.mult))
            link(dve.reciprocal(beta[:, :, :], sm[:, 0]))
            dve.wait_ge(s["gc_ps"], 1)
            link(dve.tensor_scalar(flat(gcn[:, :, :]), banks[5][:, 0:B * VAL_HEADS], -1.0, None, ALU.mult))
            dve.wait_ge(s["consts"], 1)

            def tap(r, m, t):
                if t == 1:
                    dve.wait_ge(s["tap0_ready"], at(r, CHUNKS, m + 1))
                else:
                    dve.wait_ge(s["conv_step"], at(r, 2 * CHUNKS, 2 * m + t - 1))
                w = wcqk[:, m, t:t + 1] if m < QK else wcv[:, m - QK, t:t + 1]
                dve.scalar_tensor_tensor(cv[:, m % 2], pad[:, m % 2, :, t:t + S], w, cv[:, m % 2], ALU.mult, ALU.add)\
                    .then_inc(s["conv_step" if t < TAPS - 1 else "cv_ready"], 1)

            def conv(r, m):
                for t in range(1, TAPS):
                    tap(r, m, t)

            def values(i, n, q):
                dve.wait_ge(s["vt_ps"], at(i, 2 * HB, 2 * n + q + 1))
                dve.tensor_tensor(rr(V, n, q), four(banks[4 + q][:, :]), along(nrm[:, 0, n // 2, 0, 4 * q:4 * q + 4], P), ALU.mult)\
                    .then_inc(s["V_ready"], 1)

            def gates(r):
                for dst, src in ((gR, g), (gcnR, gcn), (betaR, beta)):
                    dve.tensor_copy(dst[:, :, :], src[:, :, bass.ds(r * HB, HB)].rearrange("p b h -> p h b"))\
                        .then_inc(s["gates_used"], 1)

            def factors(r):
                link = Linked(dve, s["norm_step"], 3 + KB, r)
                dve.wait_ge(s["root_ready"], at(r, 1, 1))
                link(dve.tensor_scalar(nrm[:, 0], root[:, :, :, :], TINY, None, ALU.max))
                link(dve.reciprocal(nrm[:, 1], nrm[:, 0]))
                link(dve.tensor_tensor(nrm[:, 2], nrm[:, 1], nrm[:, 1], ALU.mult))
                dve.wait_ge(s["gates_used"], at(r, 3, 3))
                for k in range(KB):
                    link(dve.tensor_tensor(cj[:, 2 * k:2 * k + 2, :], betaR[:, 2 * k:2 * k + 2, :], spread(nrm[:, 2, k, 0, :], 2), ALU.mult))
                link.close()

            def decayed(r, n):
                k, q, u = n // 4, n // 2 % 2, n % 2
                dve.wait_ge(s["E_ready"], at(r, ITEMS, 8 * (n // 2) + 8))
                dve.wait_ge(s["GP_ps"], at(r, 8, n + 1))
                for b in range(2):
                    gp = banks[6 + u][:, b * 2 * P:(b + 1) * 2 * P].rearrange("p (a n) -> p a n", a=2)
                    for e in range(2):
                        h, bb = 2 * k + e, 4 * q + 2 * u + b
                        dve.scalar_tensor_tensor(NP[:, h, bb, :, :], spread(NP[:, h, bb, 1, :], 2), cj[:, h, bb:bb + 1], gp,
                                                 ALU.mult, ALU.mult).then_inc(s["NP_ready"], 1)

            def round_(i, more):
                dve.tensor_copy(qinv[:, :, :, :], nrm[:, 1:3, :, 1, :]).then_inc(s["f_step"], 1)
                elim = Linked(dve, s["elim_step"], ELIM, i)
                elim(dve.tensor_copy(T[:, :, :], T0[:, :, :]))
                dve.wait_ge(s["gathered"], at(i, 16, 16))
                for j in range(BL - 1):
                    n, w = BL - 1 - j, j + 1
                    part = tmp[:, 0:n * w].rearrange("p (n w) -> p n w", n=n)
                    elim(dve.tensor_tensor(part, along(A[:, j, j + 1:BL], w), spread(T[:, j, 0:w], n), ALU.mult))
                    elim(dve.tensor_tensor(T[:, j + 1:BL, 0:w], T[:, j + 1:BL, 0:w], part, ALU.subtract))
                elim(dve.tensor_copy(A[:, :, :], T[:, :, :].rearrange("p i k -> p k i")))
                elim.close()
                conv(i, QK)
                conv(i, QK + 1)
                for n in range(HB):
                    values(i, n, 0)
                    values(i, n, 1)
                    if n < 2:
                        conv(i, QK + 2 + n)
                for rep in range(3):
                    for n, (h, q) in enumerate(quads):
                        dve.wait_ge(s["apply_ps"], at(i, 24, 8 * rep + n + 1))
                        dve.tensor_tensor(rr(Y, h, q), rr(V, h, q), four(banks[n % 4][:, :]), ALU.subtract).then_inc(s["y_ready"], 1)
                        if more and n >= 5:
                            tap(i + 1, rep, n - 4)
                if more:
                    conv(i + 1, 3)
                    gates(i + 1)
                for n, (h, q) in enumerate(quads):
                    dve.wait_ge(s["csqa_ready" if n % 2 else "csq_ready"], at(i, 4, n // 2 + 1))
                    dve.tensor_reduce(s2[:, h, 4 * q:4 * q + 4], rr(V, h, q), AX.X, ALU.add).then_inc(s["s2_ready"], 1)
                dve.wait_ge(s["s2_ready"], at(i, 8, 8))
                for k in range(KB):
                    dve.tensor_tensor(f[:, 0, 2 * k:2 * k + 2, :], s2[:, 2 * k:2 * k + 2, :], spread(qinv[:, 1, k, :], 2), ALU.mult)\
                        .then_inc(s["f_step"], 1)
                dve.wait_ge(s["f_step"], at(i, F_STEPS, KB + 1))
                dve.tensor_scalar(f[:, 0], f[:, 0], 1.0 / (DK * DK), RMS_EPS, ALU.mult, ALU.add).then_inc(s["var_ready"], 2)
                if more:
                    factors(i + 1)
                dve.wait_ge(s["rms_ready"], at(i, 1, 1))
                dve.reciprocal(f[:, 0], f[:, 1]).then_inc(s["f_step"], 1)
                dve.wait_ge(s["f_step"], at(i, F_STEPS, KB + 2))
                for k in range(KB):
                    dve.scalar_tensor_tensor(f[:, 2, 2 * k:2 * k + 2, :], f[:, 0, 2 * k:2 * k + 2, :], DK ** -0.5, spread(qinv[:, 0, k, :], 2),
                                             ALU.mult, ALU.mult).then_inc(s["f_step"], 1)
                dve.wait_ge(s["f_step"], at(i, F_STEPS, F_STEPS))

                def add_out(b):
                    dve.wait_ge(s["out_ps"], at(i, B, b + 1))
                    dve.tensor_tensor(acc[:, b, :], acc[:, b, :], banks[2 + b % 2][:, 0:D], ALU.add).then_inc(s["acc_step"], 1)

                if more:
                    for n in range(AHEAD):
                        decayed(i + 1, n)
                for b in range(B):
                    for h in range(HB):
                        dve.scalar_tensor_tensor(Y[:, h, b, :], Y[:, h, b, :], f[:, 2, h, b:b + 1], zs[:, b, h * P:(h + 1) * P],
                                                 ALU.mult, ALU.mult).then_inc(s["y_scaled"], 1)
                    if b >= 2:
                        add_out(b - 2)
                    if more and b + AHEAD < 8:
                        decayed(i + 1, b + AHEAD)
                add_out(B - 2)
                add_out(B - 1)

            for m in range(QK):
                conv(0, m)
            gates(0)
            factors(0)
            for n in range(8):
                decayed(0, n)
            with dve.Fori(0, ROUNDS - 1) as i:
                round_(i, True)
            round_(ROUNDS - 1, False)
            dve.wait_ge(s["acc_step"], ROUNDS * B)
            link = Linked(dve, s["ln_step"])
            for b in range(B):
                dve.bn_stats(cj[:, 0, 0:6], acc[:, b, :]).then_inc(s["ln_step"], 1)
                dve.wait_ge(s["ln_step"], 3 * b + 1)
                dve.bn_aggr(gR[:, 0, 0:2], cj[:, 0, 0:6]).then_inc(s["ln_step"], 1)
                dve.wait_ge(s["ln_step"], 3 * b + 2)
                dve.tensor_copy(f[:, 2, 0:2, b], gR[:, 0, 0:2]).then_inc(s["ln_step"], 1)
                dve.wait_ge(s["ln_step"], 3 * b + 3)
            dve.tensor_scalar(f[:, 0, 0, :], f[:, 2, 1, :], LN_EPS, None, ALU.add).then_inc(s["ln_step"], 1)
            dve.wait_ge(s["ln_rstd"], 1)
            for b in range(B):
                dve.tensor_scalar(acc[:, b, :], acc[:, b, :], f[:, 2, 0, b:b + 1], f[:, 1, 0, b:b + 1], ALU.subtract, ALU.mult)\
                    .then_inc(s["xo_ready"], 1)


def layout_layer1_delta_rule(inp):
    W = inp["L1_attn_W_qkv"]
    q, k, v = (a.reshape(-1, P, D) for a in np.split(W, [KEY_HEADS * DK, 2 * KEY_HEADS * DK]))
    cw = inp["L1_attn_conv_w"]
    cq, ck, cvv = (a.reshape(-1, P, TAPS) for a in np.split(cw, [KEY_HEADS * DK, 2 * KEY_HEADS * DK]))

    def rounds(k, q, v):
        kq = np.stack([k, q], axis=1).reshape(ROUNDS, QK, *k.shape[1:])
        return np.concatenate([kq, v.reshape(ROUNDS, HB, *v.shape[1:])], axis=1)
    wqkv = rounds(k, q, v).reshape(ROUNDS, CHUNKS, P, DC, P).transpose(0, 4, 1, 3, 2)
    wconv = rounds(ck, cq, cvv).transpose(0, 2, 1, 3)
    wz = inp["L1_attn_W_z"].reshape(ROUNDS, HB * P, DC, P).transpose(0, 3, 2, 1)
    wout = inp["L1_attn_W_out"].T.reshape(ROUNDS, HB, P, D).transpose(0, 2, 1, 3)
    wba = np.concatenate([inp["L1_attn_W_b"], inp["L1_attn_W_a"]]).T.reshape(DC, P, 2 * VAL_HEADS).transpose(1, 0, 2)
    bias = np.broadcast_to(np.stack([inp["L1_attn_dt_bias"], inp["L1_attn_A_log"]])[None], (P, 2, VAL_HEADS))
    wqk, wcqk = (np.concatenate([a, a[:1]]) for a in (wqkv.reshape(ROUNDS, P, CHUNKS, DC * P)[:, :, :QK], wconv[:, :, :QK]))
    return dict(wqk=wqk, wcqk=wcqk, wv=wqkv.reshape(ROUNDS, P, CHUNKS, DC * P)[:, :, QK:], wcv=wconv[:, :, QK:], wz=wz, wout=wout, wba=wba, bias=bias, normw=inp["L1_attn_norm_w"].reshape(P, 1))


LEVELS, QUANT_EPS = 127.0, 1e-8
MAGIC = 1.5 * 2.0 ** 23


class Quantizer:

    STEPS = 5

    def __init__(self, ph, name, per):
        self.col = ph.sb(name + "_col", [P, 2])
        self.t = ph.sb(name + "_t", [P, 2, D])
        self.step = ph.sem(name + "_step")
        self.done = ph.sem(name + "_done")
        self.per = per

    def on_vector(self, dve, i, n, src, out, step_out):
        link = Linked(dve, self.step, self.STEPS * self.per, i)
        link.n = self.STEPS * n
        link(dve.tensor_reduce(self.col[:, 0:1], src, AX.X, ALU.max, apply_absolute_value=True))
        link(dve.tensor_scalar(step_out, self.col[:, 0:1], 1.0 / LEVELS, QUANT_EPS, ALU.mult, ALU.max))
        link(dve.reciprocal(self.col[:, 1:2], step_out))
        link(dve.tensor_scalar(self.t[:, 0, :], src, self.col[:, 1:2], LEVELS, ALU.mult, ALU.min))
        link(dve.tensor_scalar(self.t[:, 1, :], self.t[:, 0, :], -LEVELS, MAGIC, ALU.max, ALU.add))
        dve.tensor_scalar(out, self.t[:, 1, :], MAGIC, None, ALU.subtract).then_inc(self.done, 1)
        dve.wait_ge(self.done, at(i, self.per, n + 1))


class Layer1Lane:

    def __init__(self, nc, ctx, sems, n, ident):
        self.n = n
        ph = Phase(nc, f"d{n}", ctx, sems)
        sb = ph.sb
        self.xt = sb("xt", [P, D])
        self.ct = sb("ct", [P, D])
        self.mask = sb("mask", [P, P])
        self.cT = sb("cT", [P, DC, P])
        self.xstep = sb("xstep", [P, 2])
        self.y8 = sb("y8", [P, 2, D])
        self.yb = sb("yb", [P, 2, D])
        self.qT = sb("qT", [P, DC, P])
        self.kT = sb("kT", [P, DC, P])
        self.kexp = sb("kexp", [P, DC, 8, P])
        self.vaug = sb("vaug", [P, H, HD + 1])
        self.pbuf = sb("pbuf", [P, 2, 4, P])
        self.ptbuf = sb("ptbuf", [P, 2, 4, P])
        self.stats = sb("stats", [P, 32])
        self.osb = sb("osb", [P, H, HD])
        self.x5 = sb("x5", [P, D])
        self.x5T = sb("x5T", [P, DC, P])
        self.col = sb("col", [P, 6])
        self.prob = sb("prob", [P, 5, H])
        self.qT2 = sb("qT2", [P, DC, P])
        self.kv = sb("kv", [P, 2, H, HD])
        self.best = sb("best", [P, 2, HD])
        self.krep = sb("krep", [P, 8, HD])
        self.krepT = sb("krepT", [P, P])
        self.vaug2 = sb("vaug2", [P, HD + 1])
        self.osb2 = sb("osb2", [P, H, HD])
        self.xo = sb("xo", [P, D])
        self.x8 = sb("x8", [P, 2, D], BF16)
        self.x8T = sb("x8T", [P, 2, DC, P], BF16)
        self.M, self.S, self.T, self.O = (ph.bank(k) for k in "MSTO")
        self.Mb = self.M[:, :].bitcast(BF16)
        self.ln1, self.ln2 = LayerNorm(ph, "ln1"), LayerNorm(ph, "ln2")
        self.xquant = Quantizer(ph, "xquant", 2)
        banks = (self.S, self.T, self.O)
        self.cross_att = Attention(ph, "cross", HD, banks, self.pbuf, self.ptbuf, self.stats, self.osb, ident)
        self.self_att = Attention(ph, "self", HD, banks, self.pbuf, self.ptbuf, self.stats, self.osb2, ident)
        self.x_loaded, self.ctx_loaded, self.mask_loaded, self.stored = (
            ph.sem(k) for k in "x_loaded ctx_loaded mask_loaded stored".split())
        self.xo_free, self.cT_ps, self.cT_ready, self.kv_ps = (
            ph.sem(k) for k in "xo_free cT_ps cT_ready kv_ps".split())
        self.kT_ready, self.v_ready, self.kexp_ready, self.x8T_ps = (
            ph.sem(k) for k in "kT_ready v_ready kexp_ready x8T_ps".split())
        self.x8T_ready, self.y8_ps, self.y8_step, self.yb_ready = (
            ph.sem(k) for k in "x8T_ready y8_ps y8_step yb_ready".split())
        self.qT_ps, self.qT_ready, self.x5T_ps, self.x5T_ready = (
            ph.sem(k) for k in "qT_ps qT_ready x5T_ps x5T_ready".split())
        self.logits_ps, self.top_step, self.exp_ready, self.qkv_ps = (
            ph.sem(k) for k in "logits_ps top_step exp_ready qkv_ps".split())
        self.qT2_ready, self.best_step, self.krep_ready, self.vaug2_ready = (
            ph.sem(k) for k in "qT2_ready best_step krep_ready vaug2_ready".split())
        self.krepT_ps, self.krepT_ready, self.kexp2_ready = (
            ph.sem(k) for k in "krepT_ps krepT_ready kexp2_ready".split())


def layer1_attention(nc, sems, d, x_src, x_dst):
    ctx = ExitStack()
    with ctx:
        ph = Phase(nc, "d", ctx, sems)
        sb, sem = ph.sb, ph.sem
        shapes = dict(wq8=[P, DC, D], wo8=[P, DC, D], wk=[P, DC, D], wv=[P, DC, D], bk=[P, DC], bv=[1, D],
                      bqo=[P, 2, D], wtop=[P, DC, H], wqkv=[P, DC, 3 * D])
        w = {k: sb(k, s) for k, s in shapes.items()}
        ident = sb("ident", [P, P])
        identb = sb("identb", [P, P], BF16)
        causal = sb("causal", [P, P])
        causalb = sb("causalb", [P, P], BF16)
        own_block = sb("own_block", [P, 8])
        head_id = sb("head_id", [P, 2, H])
        ones = sb("ones", [1, P])
        w8 = sb("w8", [P, 2, DC, D], BF16)
        w8T = sb("w8T", [P, 2, DC, D], BF16)
        wstep = sb("wstep", [P, 2, DC])
        wstep_row = sb("wstep_row", [P, 2, D])
        wquant = Quantizer(ph, "wquant", 2 * DC)
        s = {n: sem(n) for n in "weights pool_step consts w8T_ps w8T_ready wstep_ps wstep_ready".split()}

        lanes = [Layer1Lane(nc, ctx, sems, n, ident[:, :]) for n in range(LANES)]
        TOP = 10
        half = lambda ap: ap.rearrange("p (c n) -> p c n", c=DC)
        block = ctx.enter_context(nc.Block())

        @block.sync
        def _(sp):
            for k in shapes:
                sp.dma_start(w[k][:], d[k]).then_inc(s["weights"], 16)
            for L in lanes:
                sp.dma_start(L.ct[:, :], batch(d["ctx"], L.n)).then_inc(L.ctx_loaded, 16)
                sp.dma_start(L.xt[:, :], batch(x_src, L.n)).then_inc(L.x_loaded, 16)
                sp.dma_start(L.mask[:, :], batch(d["mask"], L.n)).then_inc(L.mask_loaded, 16)
                sp.sem_inc(L.xo_free, 1)
            with sp.Fori(0, B // LANES - 1) as i:
                for L in lanes:
                    sp.wait_ge(L.cT_ps, i + 1)
                    sp.dma_start(L.ct[:, :], batch(d["ctx"], (i + 1) * LANES + L.n)).then_inc(L.ctx_loaded, 16)
                for L in lanes:
                    sp.wait_ge(L.cross_att.scores_ready, at(i, QUADS, QUADS))
                    sp.dma_start(L.mask[:, :], batch(d["mask"], (i + 1) * LANES + L.n)).then_inc(L.mask_loaded, 16)
                for L in lanes:
                    sp.wait_ge(L.ln1.step, at(i, L.ln1.DVE_STEPS, 1))
                    sp.dma_start(L.xt[:, :], batch(x_src, (i + 1) * LANES + L.n)).then_inc(L.x_loaded, 16)
                for L in lanes:
                    store_batch(sp, i, i * LANES + L.n, L.ln2.done, L.xo[:, :], x_dst, L.stored, L.xo_free)
            for L in lanes:
                store_batch(sp, B // LANES - 1, B - LANES + L.n, L.ln2.done, L.xo[:, :], x_dst, L.stored, L.xo_free)

        @block.gpsimd
        def _(pool):
            link = Linked(pool, s["pool_step"])
            fill_identity(pool, link, ident[:, :])
            link(pool.tensor_copy(identb[:, :], ident[:, :]))
            link(pool.memset(causal[:, :], 0.0))
            link(pool.affine_select(out=causal[:, :], in_=causal[:, :], compare_op=ALU.is_ge, fill=MASKED,
                                    base=0, pattern=[[-1, P]], channel_multiplier=1))
            link(pool.tensor_copy(causalb[:, :], causal[:, :]))
            link(pool.memset(own_block[:, :], 1.0))
            link(pool.affine_select(out=own_block[:, :], in_=own_block[:, :], compare_op=ALU.is_ge, fill=0.0,
                                    base=0, pattern=[[-HD, 8]], channel_multiplier=1))
            link(pool.affine_select(out=own_block[:, :], in_=own_block[:, :], compare_op=ALU.is_ge, fill=0.0,
                                    base=HD - 1, pattern=[[HD, 8]], channel_multiplier=-1))
            link(pool.iota(head_id[:, :, :], pattern=[[H, 2], [1, H]], base=0, channel_multiplier=0,
                           allow_small_or_imprecise_dtypes=True))
            link(pool.memset(ones[:, :], 1.0))
            for L in lanes:
                link(pool.memset(L.vaug2[:, :], 1.0))
                link(pool.memset(L.vaug[:, :, :], 1.0))
            pool.sem_inc(s["consts"], 1)
            with pool.Fori(0, B // LANES) as i:
                for c in range(DC):
                    for L in lanes:
                        if c == 0:
                            pool.wait_ge(L.kT_ready, at(i, DC, DC))
                        pool.tensor_tensor(L.kexp[:, c], spread(L.kT[:, c, :], 8), along(own_block[:, :], P), ALU.mult)\
                            .then_inc(L.kexp_ready, 1)
                for L in lanes:
                    pool.wait_ge(L.krepT_ready, i + 1)
                    pool.tensor_tensor(L.kexp[:, 0], spread(L.krepT[:, :], 8), along(own_block[:, :], P), ALU.mult)\
                        .then_inc(L.kexp2_ready, 1)

        @block.tensor
        def _(pe):
            pe.wait_ge(s["weights"], 16 * len(shapes))
            pe.wait_ge(s["consts"], 1)
            for k in range(2):
                for c in range(DC):
                    pe.wait_ge(wquant.done, 2 * k + c + 1)
                    for m in range(DC):
                        last = pe.transpose(lanes[k].Mb[:, m * D + c * P:m * D + (c + 1) * P],
                                            w8[:, k, c, m * P:(m + 1) * P], identb[:, :])
                last.then_inc(s["w8T_ps"], 1)
            for k in range(2):
                for c in range(DC):
                    last = pe.matmul(lanes[0].S[:, (2 * k + c) * P:(2 * k + c + 1) * P], wstep[:, k, c:c + 1].broadcast_to([P, P]), ident[:, :],
                                     start=True, stop=True)
            last.then_inc(s["wstep_ps"], 1)
            pe.wait_ge(s["w8T_ready"], 2)
            pe.wait_ge(s["wstep_ready"], 1)

            def project8(i, L, n, out):
                yield
                pe.wait_ge(L.xquant.done, at(i, 2, n + 1))
                for c in range(DC):
                    last = pe.transpose(L.Mb[:, c * P:(c + 1) * P], L.x8[:, n, c * P:(c + 1) * P], identb[:, :])
                last.then_inc(L.x8T_ps, 1)
                yield
                pe.wait_ge(L.x8T_ready, at(i, 2, n + 1))
                for c in range(DC):
                    last = pe.matmul(out, L.x8T[:, n, c, :], w8T[:, n, c, :], start=c == 0, stop=c == DC - 1)
                last.then_inc(L.y8_ps, 1)

            def start_batch(i, L):
                pe.wait_ge(L.ctx_loaded, at(i, 16, 16))
                for c in range(DC):
                    last = pe.transpose(L.M[:, c * P:(c + 1) * P], L.ct[:, c * P:(c + 1) * P], ident[:, :])
                last.then_inc(L.cT_ps, 1)
                yield
                pe.wait_ge(L.cT_ready, i + 1)
                for m in range(DC):
                    for c in range(DC):
                        pe.matmul(L.S[:, m * P:(m + 1) * P], w["wk"][:, c, m * P:(m + 1) * P], L.cT[:, c, :], start=c == 0, stop=c == DC - 1)
                pe.matmul(L.T[:, 0:D], ones[:, :], w["bv"][:, :], start=True, stop=False)
                for c in range(DC):
                    last = pe.matmul(L.T[:, 0:D], L.cT[:, c, :], w["wv"][:, c, :], start=False, stop=c == DC - 1)
                last.then_inc(L.kv_ps, 1)


                yield from project8(i, L, 0, L.M[:, D:2 * D])
                yield
                pe.wait_ge(L.yb_ready, at(i, 2, 1))
                for c in range(DC):
                    last = pe.transpose(L.M[:, c * P:(c + 1) * P], L.yb[:, 0, c * P:(c + 1) * P], ident[:, :])
                last.then_inc(L.qT_ps, 1)
                yield

            def lane_program(i, L, more):
                pe.wait_ge(L.qT_ready, i + 1)
                pe.wait_ge(L.v_ready, i + 1)
                pe.wait_ge(L.mask_loaded, at(i, 16, 16))

                def cross_scores(n, bank):
                    if n % 2 == 0:
                        pe.wait_ge(L.kexp_ready, at(i, DC, n // 2 + 1))
                    pe.matmul(four(bank[:, :]), ident[:, :], spread(L.mask[:, :], 4), start=True, stop=False)
                    return pe.matmul(four(bank[:, :]), L.qT[:, n // 2, :], L.kexp[:, n // 2, 4 * (n % 2):4 * (n % 2) + 4, :],
                                     start=False, stop=True)

                yield from L.cross_att.on_tensor(pe, i, cross_scores, lambda n, h: L.vaug[:, 4 * n + h, :])
                yield from project8(i, L, 1, L.M[:, D:2 * D])
                yield
                yield
                pe.wait_ge(L.ln1.done, i + 1)
                for c in range(DC):
                    last = pe.transpose(L.M[:, c * P:(c + 1) * P], L.x5[:, c * P:(c + 1) * P], ident[:, :])
                last.then_inc(L.x5T_ps, 1)
                yield
                pe.wait_ge(L.x5T_ready, i + 1)
                for c in range(DC):
                    last = pe.matmul(L.M[:, D:D + H], L.x5T[:, c, :], w["wtop"][:, c, :], start=c == 0, stop=c == DC - 1)
                last.then_inc(L.logits_ps, 1)
                yield
                for c in range(DC):
                    last = pe.matmul(L.O[:, :], L.x5T[:, c, :], w["wqkv"][:, c, D:3 * D], start=c == 0, stop=c == DC - 1)
                for m in range(DC):
                    for c in range(DC):
                        last = pe.matmul(L.T[:, m * P:(m + 1) * P], w["wqkv"][:, c, m * P:(m + 1) * P], L.x5T[:, c, :],
                                         start=c == 0, stop=c == DC - 1)
                last.then_inc(L.qkv_ps, 1)
                yield
                pe.wait_ge(L.krep_ready, i + 1)
                pe.transpose(L.M[:, 0:P], L.krep[:, :, :].rearrange("p r d -> p (r d)"), ident[:, :]).then_inc(L.krepT_ps, 1)
                yield
                pe.wait_ge(L.vaug2_ready, i + 1)
                pe.wait_ge(L.qT2_ready, i + 1)

                def self_scores(n, bank):
                    if n == 0:
                        pe.wait_ge(L.kexp2_ready, i + 1)
                    pe.matmul(four(bank[:, :]), identb[:, :], spread(causalb[:, :], 4), start=True, stop=False)
                    return pe.matmul(four(bank[:, :]), L.qT2[:, n // 2, :], L.kexp[:, 0, 4 * (n % 2):4 * (n % 2) + 4, :],
                                     start=False, stop=True)

                yield from L.self_att.on_tensor(pe, i, self_scores, lambda n, h: L.vaug2[:, :])
                if more:
                    yield from start_batch(i + 1, L)

            in_turns([start_batch(0, L) for L in lanes])
            with pe.Fori(0, B // LANES - 1) as i:
                in_turns([lane_program(i, L, True) for L in lanes])
            in_turns([lane_program(B // LANES - 1, L, False) for L in lanes])

        @block.scalar
        def _(act):
            for k, bank in enumerate((lanes[0].Mb, lanes[1].Mb)):
                act.wait_ge(s["w8T_ps"], k + 1)
                act.activation(w8T[:, k], half(bank[:, 0:2 * D]), ACT.Copy).then_inc(s["w8T_ready"], 1)
            act.wait_ge(s["wstep_ps"], 1)
            act.activation(wstep_row[:, :, :], lanes[0].S[:, :].rearrange("p (k n) -> p k n", k=2), ACT.Copy).then_inc(s["wstep_ready"], 1)

            def copy8(i, L, n):
                act.wait_ge(L.x8T_ps, at(i, 2, n + 1))
                act.activation(L.x8T[:, n], half(L.Mb[:, 0:D]), ACT.Copy).then_inc(L.x8T_ready, 1)

            def start_batch(i, L):
                act.wait_ge(L.cT_ps, i + 1)
                act.activation(L.cT[:, :, :], half(L.M[:, 0:D]), ACT.Copy).then_inc(L.cT_ready, 1)
                yield
                act.wait_ge(L.kv_ps, i + 1)
                act.activation(L.vaug[:, :, 0:HD], L.T[:, 0:D].rearrange("p (h d) -> p h d", h=H), ACT.Copy).then_inc(L.v_ready, 1)


                yield
                copy8(i, L, 0)
                yield
                act.wait_ge(L.qT_ps, i + 1)
                act.activation(L.qT[:, :, :], half(L.M[:, 0:D]), ACT.Copy, scale=0.25).then_inc(L.qT_ready, 1)
                yield

            def lane_program(i, L, more):
                yield from L.cross_att.on_scalar(act, i)
                yield
                copy8(i, L, 1)
                yield
                L.ln1.on_scalar(act, i)
                yield
                act.wait_ge(L.x5T_ps, i + 1)
                act.activation(L.x5T[:, :, :], half(L.M[:, 0:D]), ACT.Copy).then_inc(L.x5T_ready, 1)
                yield
                act.wait_ge(L.top_step, at(i, TOP, 2))
                act.activation(L.prob[:, 0, :], L.prob[:, 0, :], ACT.Exp).then_inc(L.exp_ready, 1)
                yield
                act.wait_ge(L.qkv_ps, i + 1)
                act.activation(L.qT2[:, :, :], half(L.T[:, 0:D]), ACT.Copy, scale=0.25).then_inc(L.qT2_ready, 1)
                yield
                act.wait_ge(L.krepT_ps, i + 1)
                act.activation(L.krepT[:, :], L.M[:, 0:P], ACT.Copy).then_inc(L.krepT_ready, 1)
                yield
                yield from L.self_att.on_scalar(act, i)
                yield
                if not more:
                    L.ln2.on_scalar(act, i)
                    return
                next_start = start_batch(i + 1, L)
                next(next_start)
                yield
                L.ln2.on_scalar(act, i)
                yield from next_start

            in_turns([start_batch(0, L) for L in lanes])
            with act.Fori(0, B // LANES - 1) as i:
                in_turns([lane_program(i, L, True) for L in lanes])
            in_turns([lane_program(B // LANES - 1, L, False) for L in lanes])

        @block.vector
        def _(dve):
            dve.wait_ge(s["weights"], 16 * len(shapes))
            dve.wait_ge(s["consts"], 1)
            for k, name in enumerate(("wq8", "wo8")):
                for c in range(DC):
                    wquant.on_vector(dve, 0, 2 * k + c, w[name][:, c, :], w8[:, k, c, :], wstep[:, k, c:c + 1])
            dve.wait_ge(s["wstep_ready"], 1)

            def scale8(i, L, n):
                dve.tensor_scalar(L.y8[:, 0, :], wstep_row[:, n, :], L.xstep[:, n:n + 1], None, ALU.mult).then_inc(L.y8_step, 1)
                dve.wait_ge(L.y8_step, at(i, 4, 2 * n + 1))
                dve.wait_ge(L.y8_ps, at(i, 2, n + 1))
                dve.tensor_tensor(L.y8[:, 1, :], L.y8[:, 0, :], L.M[:, D:2 * D], ALU.mult).then_inc(L.y8_step, 1)
                dve.wait_ge(L.y8_step, at(i, 4, 2 * n + 2))
                dve.tensor_tensor(L.yb[:, n, :], L.y8[:, 1, :], w["bqo"][:, n, :], ALU.add).then_inc(L.yb_ready, 1)

            def quantize_input(i, L):
                dve.wait_ge(L.x_loaded, at(i, 16, 16))
                L.xquant.on_vector(dve, i, 0, L.xt[:, :], L.x8[:, 0, :], L.xstep[:, 0:1])

            def start_batch(i, L):
                dve.wait_ge(L.kv_ps, i + 1)
                for c in range(DC):
                    dve.tensor_scalar(L.kT[:, c, :], L.S[:, c * P:(c + 1) * P], w["bk"][:, c:c + 1], None, ALU.add).then_inc(L.kT_ready, 1)
                yield
                scale8(i, L, 0)
                yield

            def lane_program(i, L, more):
                yield from L.cross_att.on_vector(dve, i)
                dve.wait_ge(L.cross_att.o_done, at(i, QUADS, QUADS))
                L.xquant.on_vector(dve, i, 1, L.osb[:, :, :].rearrange("p h d -> p (h d)"), L.x8[:, 1, :], L.xstep[:, 1:2])
                yield
                scale8(i, L, 1)
                yield
                dve.wait_ge(L.yb_ready, at(i, 2, 2))
                yield from L.ln1.on_vector(dve, i, L.x5[:, :], L.xt[:, :], L.yb[:, 1, :])
                link = Linked(dve, L.top_step, TOP, i)
                yield
                dve.wait_ge(L.logits_ps, i + 1)
                logits = L.M[:, D:D + H]
                link(dve.tensor_reduce(L.col[:, 0:1], logits, AX.X, ALU.max))
                link(dve.tensor_scalar(L.prob[:, 0, :], logits, L.col[:, 0:1], None, ALU.subtract))
                yield
                dve.wait_ge(L.exp_ready, i + 1)
                link(dve.tensor_reduce(L.col[:, 1:2], L.prob[:, 0, :], AX.X, ALU.add))
                link(dve.reciprocal(L.col[:, 2:3], L.col[:, 1:2]))
                link(dve.tensor_scalar(L.prob[:, 1, :], L.prob[:, 0, :], L.col[:, 2:3], None, ALU.mult))
                link(dve.tensor_reduce(L.col[:, 3:4], L.prob[:, 1, :], AX.X, ALU.max))
                link(dve.tensor_scalar(L.prob[:, 2, :], L.prob[:, 1, :], L.col[:, 3:4], -float(H), ALU.is_equal, ALU.mult))
                link(dve.tensor_tensor(L.prob[:, 3, :], L.prob[:, 2, :], head_id[:, 1, :], ALU.add))
                link(dve.tensor_reduce(L.col[:, 4:5], L.prob[:, 3, :], AX.X, ALU.min))
                link(dve.tensor_scalar(L.prob[:, 4, :], head_id[:, 0, :], L.col[:, 4:5], None, ALU.is_equal))
                link.close()
                yield
                dve.wait_ge(L.qkv_ps, i + 1)
                kvp = L.O[:, :].rearrange("p (a h d) -> p a h d", a=2, h=H)
                for a in range(2):
                    dve.tensor_tensor(L.kv[:, a], kvp[:, a], along(L.prob[:, 4, :], HD), ALU.mult).then_inc(L.best_step, 1)
                for a in range(2):
                    dve.wait_ge(L.best_step, at(i, 4, a + 1))
                    dve.tensor_reduce(L.best[:, a, :], L.kv[:, a].rearrange("p h d -> p d h"), AX.X, ALU.add).then_inc(L.best_step, 1)
                dve.wait_ge(L.best_step, at(i, 4, 4))
                dve.tensor_copy(L.krep[:, :, :], spread(L.best[:, 0, :], 8)).then_inc(L.krep_ready, 1)
                dve.tensor_scalar(L.vaug2[:, 0:HD], L.best[:, 1, :], L.col[:, 3:4], None, ALU.mult).then_inc(L.vaug2_ready, 1)
                yield
                if more:
                    quantize_input(i + 1, L)
                yield
                yield from L.self_att.on_vector(dve, i)
                dve.wait_ge(L.self_att.o_done, at(i, QUADS, QUADS))
                dve.wait_ge(L.xo_free, i + 1)
                yield from L.ln2.on_vector(dve, i, L.xo[:, :], L.x5[:, :], L.osb2[:, :, :].rearrange("p h d -> p (h d)"))
                if more:
                    yield from start_batch(i + 1, L)

            for L in lanes:
                quantize_input(0, L)
            in_turns([start_batch(0, L) for L in lanes])
            with dve.Fori(0, B // LANES - 1) as i:
                in_turns([lane_program(i, L, True) for L in lanes])
            in_turns([lane_program(B // LANES - 1, L, False) for L in lanes])


def layout_layer1_attention(inp):
    by_chunk = lambda a: a.reshape(DC, P, -1).transpose(1, 0, 2)
    bqo = np.broadcast_to(np.stack([inp["L1_xattn_bq"], inp["L1_xattn_bo"]])[None], (P, 2, D))
    return dict(ctx=inp["ctx_2048"], mask=inp["mask_BxSxS2_ff0"], wq8=by_chunk(inp["L1_xattn_wq"]), wo8=by_chunk(inp["L1_xattn_wo"]),
                wk=by_chunk(inp["L1_xattn_wk"].T), wv=by_chunk(inp["L1_xattn_wv"].T), bk=inp["L1_xattn_bk"].reshape(DC, P).T,
                bv=inp["L1_xattn_bv"].reshape(1, D), bqo=bqo, wtop=by_chunk(inp["L1_ffn_W_gate"].T),
                wqkv=by_chunk(inp["L1_ffn_W_qkv"].T))


PHASES = (("a", layout_layer0_attention, layer0_attention), ("b", layout_layer0_experts, layer0_experts),
          ("c", layout_layer1_delta_rule, layer1_delta_rule), ("d", layout_layer1_attention, layer1_attention))


def decoder(nc, x, weights, out):
    src = x
    for n, (tag, _, build) in enumerate(PHASES):
        last = n == len(PHASES) - 1
        dst = out if last else nc.dram_tensor(f"x_after_{tag}", (B, S, D), F32, kind="Internal").ap()
        sems = []
        build(nc, sems, weights[tag], src, dst)
        if not last:
            nc.all_engine_barrier()
            nc.clear_and_free_semaphores(sems)
            nc.all_engine_barrier()
        src = dst


def kernel(**inputs):
    import concourse.bacc as bacc
    from concourse.bass_utils import run_bass_kernel_spmd

    inputs = {k: np.asarray(v) for k, v in inputs.items()}
    nc = bacc.Bacc("TRN2", target_bir_lowering=False, num_devices=1)
    arrays = {"x": np.ascontiguousarray(inputs["x"])}
    handles = {"x": nc.dram_tensor("x", arrays["x"].shape, F32, kind="ExternalInput").ap()}
    weights = {}
    for tag, layout, _ in PHASES:
        weights[tag] = {}
        for name, a in layout(inputs).items():
            full = f"{tag}_in_{name}"
            arrays[full] = np.ascontiguousarray(a)
            weights[tag][name] = nc.dram_tensor(full, a.shape, mybir.dt.from_np(a.dtype), kind="ExternalInput").ap()
    out = nc.dram_tensor("out", (B, S, D), F32, kind="ExternalOutput").ap()
    decoder(nc, handles["x"], weights, out)
    return run_bass_kernel_spmd(nc, [arrays], core_ids=[0]).results[0]["out"]
```
